# Optimizing a Trainium2 kernel written in Bass

```python
import numpy as np
import jax
import jax.numpy as jnp

def _softmax(x, axis=-1):
    return jax.nn.softmax(x, axis=axis)

def _gelu(x):
    return jax.nn.gelu(x, approximate=True)

def _silu(x):
    return jax.nn.silu(x)

def _sigmoid(x):
    return jax.nn.sigmoid(x)

def _layernorm(x, axis=-1, eps=1e-05):
    m = jnp.mean(x, axis=axis, keepdims=True)
    v = jnp.var(x, axis=axis, keepdims=True)
    return (x - m) / jnp.sqrt(v + eps)

def _scatter_add(tgt, idx, src, axis=0):
    return tgt.at[idx].add(src)

def _segment_sum(src, seg, n):
    return jax.ops.segment_sum(src, seg, n)
kernel_name = 'mk_macaron_d1_jaxref_r8_43d6f5'

def setup_inputs(seed: int=0):
    np.random.seed(seed)
    _w = jnp.asarray

    def _L0_attn_setup():
        import jax, jax.numpy as jnp
        import numpy as np
        NUM_HEADS = 16
        EPS = 1e-06

        def elu_plus_one(x):
            return jax.nn.elu(x) + 1.0

        def _retrieve(q, memories, memory_norms):
            sigma_q = elu_plus_one(q)
            a_mem = jnp.einsum('bsd,mde->mbse', sigma_q, memories)
            raw = jnp.einsum('bsd,md->mbs', sigma_q, memory_norms)
            per_mem = a_mem / jnp.clip(raw, EPS, None)[..., None]
            rel = raw.mean(axis=-1)
            w = jax.nn.softmax(rel, axis=0)
            return jnp.einsum('mbse,mb->bse', per_mem, w)

        def _local_causal_attention(q, k, v):
            B, S, D = q.shape
            hd = D // NUM_HEADS
            qh = q.reshape(B, S, NUM_HEADS, hd).transpose(0, 2, 1, 3)
            kh = k.reshape(B, S, NUM_HEADS, hd).transpose(0, 2, 1, 3)
            vh = v.reshape(B, S, NUM_HEADS, hd).transpose(0, 2, 1, 3)
            scores = jnp.einsum('bhqd,bhkd->bhqk', qh, kh) * hd ** (-0.5)
            causal = jnp.tril(jnp.ones((S, S), dtype=bool))
            scores = jnp.where(causal, scores, jnp.float32(-1000000000.0))
            attn = jax.nn.softmax(scores, axis=-1)
            out = jnp.einsum('bhqk,bhkd->bhqd', attn, vh)
            return out.transpose(0, 2, 1, 3).reshape(B, S, D)
        key = jax.random.key(seed)
        ks = jax.random.split(key, 8)
        B, S, H, D, M = (2, 256, 256, 256, 4)
        x = jax.random.normal(ks[0], (B, S, H), jnp.float32)
        w_q = jax.random.normal(ks[1], (D, H), jnp.float32) * 0.02
        w_k = jax.random.normal(ks[2], (D, H), jnp.float32) * 0.02
        w_v = jax.random.normal(ks[3], (D, H), jnp.float32) * 0.02
        w_o = jax.random.normal(ks[4], (H, D), jnp.float32) * 0.02
        gate = jnp.zeros((1,), jnp.float32)
        memories = jax.random.normal(ks[5], (M, D, D), jnp.float32) * 0.02
        memory_norms = jax.random.uniform(ks[6], (M, D), jnp.float32) * float(S)
        return {'x': x, 'w_q': w_q, 'w_k': w_k, 'w_v': w_v, 'w_o': w_o, 'gate': gate, 'memories': memories, 'memory_norms': memory_norms}
    _L0_attn_in = _L0_attn_setup()

    def _L0_ffn_setup():
        import jax, jax.numpy as jnp
        import numpy as np
        DIM_IN = 256
        DIM_HIDDEN = 1024
        key = jax.random.key(seed)
        k_x, k_g, k_u, k_d = jax.random.split(key, 4)
        s_in = 1.0 / np.sqrt(DIM_IN)
        s_hid = 1.0 / np.sqrt(DIM_HIDDEN)
        x = jax.random.normal(k_x, (4, 256, DIM_IN), dtype=jnp.float32)
        w_gate = jax.random.uniform(k_g, (DIM_HIDDEN, DIM_IN), jnp.float32, -s_in, s_in)
        w_up = jax.random.uniform(k_u, (DIM_HIDDEN, DIM_IN), jnp.float32, -s_in, s_in)
        w_down = jax.random.uniform(k_d, (DIM_IN, DIM_HIDDEN), jnp.float32, -s_hid, s_hid)
        return {'x': x, 'w_gate': w_gate, 'w_up': w_up, 'w_down': w_down}
    _L0_ffn_in = _L0_ffn_setup()
    _d = {'L0_attn_x': _L0_attn_in['x'], 'L0_attn_w_q': _L0_attn_in['w_q'], 'L0_attn_w_k': _L0_attn_in['w_k'], 'L0_attn_w_v': _L0_attn_in['w_v'], 'L0_attn_w_o': _L0_attn_in['w_o'], 'L0_attn_gate': _L0_attn_in['gate'], 'L0_attn_memories': _L0_attn_in['memories'], 'L0_attn_memory_norms': _L0_attn_in['memory_norms'], 'L0_ffn_w_gate': _L0_ffn_in['w_gate'], 'L0_ffn_w_up': _L0_ffn_in['w_up'], 'L0_ffn_w_down': _L0_ffn_in['w_down']}
    _x0 = _d['L0_attn_x']
    _d['L0_attn_x'] = jax.random.normal(jax.random.fold_in(jax.random.key(seed), 1), (4, 1024, 256), dtype=_x0.dtype)
    del _x0
    return _d

def reference(L0_attn_x, L0_attn_w_q, L0_attn_w_k, L0_attn_w_v, L0_attn_w_o, L0_attn_gate, L0_attn_memories, L0_attn_memory_norms, L0_ffn_w_gate, L0_ffn_w_up, L0_ffn_w_down):

    def _L0_attn_ref(x, w_q, w_k, w_v, w_o, gate, memories, memory_norms):
        import jax, jax.numpy as jnp
        import numpy as np
        NUM_HEADS = 16
        EPS = 1e-06

        def elu_plus_one(x):
            return jax.nn.elu(x) + 1.0

        def _retrieve(q, memories, memory_norms):
            sigma_q = elu_plus_one(q)
            a_mem = jnp.einsum('bsd,mde->mbse', sigma_q, memories)
            raw = jnp.einsum('bsd,md->mbs', sigma_q, memory_norms)
            per_mem = a_mem / jnp.clip(raw, EPS, None)[..., None]
            rel = raw.mean(axis=-1)
            w = jax.nn.softmax(rel, axis=0)
            return jnp.einsum('mbse,mb->bse', per_mem, w)

        def _local_causal_attention(q, k, v):
            B, S, D = q.shape
            hd = D // NUM_HEADS
            qh = q.reshape(B, S, NUM_HEADS, hd).transpose(0, 2, 1, 3)
            kh = k.reshape(B, S, NUM_HEADS, hd).transpose(0, 2, 1, 3)
            vh = v.reshape(B, S, NUM_HEADS, hd).transpose(0, 2, 1, 3)
            scores = jnp.einsum('bhqd,bhkd->bhqk', qh, kh) * hd ** (-0.5)
            causal = jnp.tril(jnp.ones((S, S), dtype=bool))
            scores = jnp.where(causal, scores, jnp.float32(-1000000000.0))
            attn = jax.nn.softmax(scores, axis=-1)
            out = jnp.einsum('bhqk,bhkd->bhqd', attn, vh)
            return out.transpose(0, 2, 1, 3).reshape(B, S, D)
        q = x @ w_q.T
        k = x @ w_k.T
        v = x @ w_v.T
        mem_out = _retrieve(q, memories, memory_norms)
        local_out = _local_causal_attention(q, k, v)
        g = jax.nn.sigmoid(gate)
        out = g * mem_out + (1.0 - g) * local_out
        return out @ w_o.T

    def _L0_ffn_ref(x, w_gate, w_up, w_down):
        import jax, jax.numpy as jnp
        import numpy as np
        DIM_IN = 256
        DIM_HIDDEN = 1024
        gate = jnp.einsum('bsd,hd->bsh', x, w_gate)
        up = jnp.einsum('bsd,hd->bsh', x, w_up)
        gated = jax.nn.silu(gate) * up
        return jnp.einsum('bsh,dh->bsd', gated, w_down)
    x = L0_attn_x
    x = x + 0.5 * _L0_ffn_ref(_layernorm(x, axis=-1), L0_ffn_w_gate, L0_ffn_w_up, L0_ffn_w_down)
    x = x + _L0_attn_ref(_layernorm(x, axis=-1), L0_attn_w_q, L0_attn_w_k, L0_attn_w_v, L0_attn_w_o, L0_attn_gate, L0_attn_memories, L0_attn_memory_norms)
    x = x + 0.5 * _L0_ffn_ref(_layernorm(x, axis=-1), L0_ffn_w_gate, L0_ffn_w_up, L0_ffn_w_down)
    return x

_drawn_inputs = setup_inputs


def setup_inputs(seed=0):
    import zlib

    import numpy as np

    out = dict(_drawn_inputs(seed))
    spreads = {}
    factors = {'L0_attn_w_q': 8.0,
     'L0_attn_w_k': 8.0,
     'L0_attn_w_v': 8.0,
     'L0_attn_w_o': 8.0,
     'L0_attn_memories': 8.0,
     'L0_attn_memory_norms': 8.0}
    for name, (base, spread) in spreads.items():
        noise = np.random.default_rng([zlib.crc32(name.encode()), seed]).standard_normal(out[name].shape)
        drawn = base * np.exp(spread * noise) if base else spread * noise
        out[name] = jnp.asarray(drawn.astype(out[name].dtype))
    for name, factor in factors.items():
        out[name] = (out[name] * factor).astype(out[name].dtype)
    return out
```

```python
from contextlib import ExitStack

import concourse.bass as bass
from concourse import mybir

F32 = mybir.dt.float32
F32R = mybir.dt.float32r
BF16 = mybir.dt.bfloat16
ALU = mybir.AluOpType
ACT = mybir.ActivationFunctionType
AX = mybir.AxisListType

P = 128
B, S, D, F = 4, 1024, 256, 1024
HEADS, HD, MEM = 16, 16, 4
TOK = B * S
TILES = TOK // P
CT = 4
CW = CT * P
CHUNKS = TILES // CT
DK = D // P
FK = F // P
LN_EPS, MEM_EPS = 1e-5, 1e-6
SCALE = float(HD) ** -0.5
GROUPS, GH = 4, 4
BT = S // P
PARTS = 6 * HD
ROWS = PARTS + 3
VW = 2 * HD
MASKED = -1.0e30
RAW = 7
Q_ROWS = (0, 0, 0, 1, 1, 2)
K_ROWS = (0, 1, 2, 0, 1, 0)


class Tally:

    def __init__(self, sem, credit=0, step=1):
        self.sem, self.credit, self.step = sem, credit, step

    def after(self, i):
        return (i + (self.credit + 1)) * self.step

    def give(self, eng):
        if self.credit:
            eng.sem_inc(self.sem, self.credit * self.step)


def quads():
    out = []
    for qc in range(2):
        for kb in range(CT * (qc + 1)):
            q0 = max(qc * CW, kb * P)
            out.append((qc, kb, (qc + 1) * CW - q0, kb >= qc * CT))
    return out


QUADS = quads()
NQ = len(QUADS)
LAST_QUAD = (CT - 1, NQ - 1)
DIAG = [sum(q[3] for q in QUADS[:i]) for i in range(NQ)]
NDIAG = sum(q[3] for q in QUADS)
UNITS = [(qt, h) for qt in range(BT) for h in range(GH)]
NU = len(UNITS)


def timeline(ahead):
    out, u, done, blocks = [], 0, 0, 0
    total = sum(w for _, _, w, _ in QUADS) * GH
    hold = 2 * (BT - 1)
    max0 = False
    for i, (qc, kb, w, _) in enumerate(QUADS):
        out.append(("scores2", i))
        if i == 1:
            out.append(("maxrows", 0, 1))
        done += w * GH
        while ahead and u < NU and blocks * P < done - (hold * P if i == NQ - 1 else 0):
            out.append(("scores1", u))
            blocks += UNITS[u][0] + 1
            u += 1
            if u == NU // 2 + 3:
                out.append(("maxrows", 1, 0))
                max0 = True
        if i:
            out.append(("pv", i - 1))
        if i == LAST_QUAD[0] + 2:
            out.append(("outT", 0))
    out.append(("pv", NQ - 1))
    while ahead and u < NU:
        out.append(("scores1", u))
        u += 1
    out.append(("outT", 1))
    assert max0 or not ahead
    return out


def build(nc, x, wg, wu, wd, wq, wk, wv, wo, memT, norms, gate, out):
    ctx = ExitStack()
    with ctx:
        def sem(name):
            return ctx.enter_context(nc.semaphore(name))

        def sb(name, shape, dt=F32, where=ctx):
            return where.enter_context(nc.sbuf_tensor(name, shape, dt))

        def pair(name, shape, where=ctx):
            return sb(name + "_h", shape, F32R, where), sb(name + "_l", shape, F32R, where)

        def first(n):
            return isinstance(n, int) and n == 0

        def is_last(c):
            return isinstance(c, int) and c == CHUNKS - 1

        q_parts = nc.dram_tensor("q_parts", [3, D, TOK], BF16, kind="Internal").ap()
        k_parts = nc.dram_tensor("k_parts", [3, D, TOK], BF16, kind="Internal").ap()
        v_dram = nc.dram_tensor("v_groups", [B, GROUPS, P, BT, GH * VW], F32, kind="Internal").ap()
        o_dram = nc.dram_tensor("o_groups", [B, GROUPS, P, BT, GH * HD], F32, kind="Internal").ap()

        X = sb("X", [P, TILES, D])
        wgs, wus = pair("wg", [P, DK, F]), pair("wu", [P, DK, F])
        wds = pair("wd", [P, FK, D])
        wqs, wks, wvs, wos = (pair(n, [P, DK, D]) for n in ("wq", "wk", "wv", "wo"))
        mwo = pair("mwo", [P, DK, MEM * D])
        nrm = pair("nrm", [P, DK, MEM])
        ident = sb("ident", [P, P])
        mask = sb("mask", [P, S], BF16)
        mean_w = sb("mean_w", [P, P])
        xT = pair("xT", [P, DK, CW])
        xn = sb("xn", [P, CT, D])
        stats = sb("stats", [P, CT, 6])
        mv = sb("mv", [P, CT, 2])
        veps = sb("veps", [P, CT])
        rstd = sb("rstd", [P, CT])
        neg_half = sb("neg_half", [P, CT])
        gate_sb = sb("gate_sb", [P, 1])
        gate_e = sb("gate_e", [P, 1])
        gate_d = sb("gate_d", [P, 1])
        g_mem = sb("g_mem", [P, 1])
        g_loc = sb("g_loc", [P, 1])
        nrm_raw = sb("nrm_raw", [P, DK, MEM])

        with ExitStack() as r:
            gT = pair("gT", [P, FK, CW], r)
            silu = sb("silu", [P, 2, CW], F32, r)
            gated = sb("gated", [P, 2, CW], F32, r)
            with ExitStack() as r2:
                wg_raw, wu_raw = sb("wg_raw", [P, DK, F], F32, r2), sb("wu_raw", [P, DK, F], F32, r2)
                wd_raw = sb("wd_raw", [P, FK, D], F32, r2)
                wqkvo_raw = sb("wqkvo_raw", [P, 4, DK, D], F32, r2)
                memT_raw = sb("memT_raw", [P, MEM, DK, D], F32, r2)
            with ExitStack() as r2:
                oT = pair("oT", [P, DK, CW], r2)
                o_in = sb("o_in", [P, CT, GROUPS, GH * HD], F32, r2)
        with ExitStack() as r:
            memTs = pair("memTs", [P, MEM, DK, D], r)
            sig = pair("sig", [P, DK, S], r)
            q_min = sb("q_min", [P, 2, CW], F32, r)
            q_exp = sb("q_exp", [P, 2, CW], F32, r)
            sig_f = sb("sig_f", [P, 2, CW], F32, r)
            rest = sb("rest", [P, 2, CW], F32, r)
            part = [sb(f"part_{n}", [P, 2 * DK, CW], BF16, r) for n in "hml"]
            va = sb("va", [P, CT, HEADS, VW], F32, r)
            raw_sb = sb("raw_sb", [P, BT, MEM], F32, r)
            rawc = sb("rawc", [P, BT, MEM], F32, r)
            rinv = sb("rinv", [P, BT, MEM], F32, r)
            rel = sb("rel", [P, MEM], F32, r)
            rmax = sb("rmax", [P, 1], F32, r)
            rexp = sb("rexp", [P, MEM], F32, r)
            rsum = sb("rsum", [P, 1], F32, r)
            rnorm = sb("rnorm", [P, 1], F32, r)
            wmem = sb("wmem", [P, MEM], F32, r)
            coef = sb("coef", [P, BT, MEM], F32, r)
        with ExitStack() as r:
            Q = sb("Q", [P, 2, GH, S], BF16, r)
            K = sb("K", [P, 2, GH, S], BF16, r)
            Vg = sb("Vg", [P, 2, BT, GH * VW], F32, r)
            PT = sb("PT", [P, 2 * GH, CW], F32, r)
            Osb = sb("Osb", [P, 2, CW], F32, r)
            Lg = sb("Lg", [P, 2, BT, GH * HD], F32, r)
            rmx = sb("rmx", [P, 2, NU], F32, r)
            mx_rest = sb("mx_rest", [CT * GH, 2, P], F32, r)
            mx_part = [sb(f"mx_{n}", [CT * GH, 2, P], BF16, r) for n in "hml"]
            rden = sb("rden", [P, 2, CT * GH], F32, r)

        big = [ctx.enter_context(nc.psum_tensor(f"big{i}", [P, 2 * CW], F32)) for i in range(2)]
        bank = [ctx.enter_context(nc.psum_tensor(f"bank{i}", [P, CW], F32)) for i in range(4)]

        def half(i):
            return big[i // 2][:, (i % 2) * CW:(i % 2 + 1) * CW]

        x0_in, xr_in = sem("x0_in"), sem("xr_in")
        w_in = {n: sem(f"{n}_in") for n in ("wg", "wu", "wd", "wqkvo", "memT", "small")}
        consts, ident_ok = sem("consts"), sem("ident_ok")
        w_hi, w_lo = sem("w_hi"), sem("w_lo")
        st_done, mv_done, ve_done, rs_done = sem("st_done"), sem("mv_done"), sem("ve_done"), sem("rs_done")
        xn_done, xTr_done, xh_done, xl_done = sem("xn_done"), sem("xTr_done"), sem("xh_done"), sem("xl_done")

        class Ffn:
            def __init__(self, tag):
                self.second = tag == "2"
                self.g_ready, self.u_ready = Tally(sem("g_ready" + tag)), Tally(sem("u_ready" + tag))
                self.silu_done = Tally(sem("silu_done" + tag), 2)
                self.mul_done = Tally(sem("mul_done" + tag), 2)
                self.hi_done = Tally(sem("hi_done" + tag))
                self.lo_done = Tally(sem("lo_done" + tag), 2)
                self.d_ready = Tally(sem("d_ready" + tag), 1)
                self.x_done = Tally(sem("x_done" + tag), 2)
                if self.second:
                    self.o_in = Tally(sem("o_in_done"), 0, 16)
                    self.oTr = Tally(sem("oTr"))
                    self.oh, self.ol = Tally(sem("oh")), Tally(sem("ol"))
                    self.stored = sem("out_stored")

            def down_at(self, c):
                if not self.second:
                    return c * CT
                return c * (2 * CT) + (CT if is_last(c) else 2 * CT)

            def proj_at(self, c):
                return 0 if first(c) else c * (2 * CT) - CT

        ffn1, ffn2 = Ffn("1"), Ffn("2")
        sp_hi, sp_lo, mwo_ready = sem("sp_hi"), sem("sp_lo"), Tally(sem("mwo_ready"))
        mwo_hi, mwo_lo = sem("mwo_hi"), Tally(sem("mwo_lo"), 2)
        gate_step = sem("gate_step")
        va_ones = sem("va_ones")
        qk_ready = Tally(sem("qk_ready"))
        ph_done, rest_done = Tally(sem("ph_done")), Tally(sem("rest_done"), 2)
        pm_done, pl_done = Tally(sem("pm_done")), Tally(sem("pl_done"), 2)
        part_out = [Tally(sem(f"part_out{o}"), 1, 48) for o in range(2 * DK)]
        min_done, qe_done = Tally(sem("min_done")), Tally(sem("qe_done"), 2)
        sf_done, sh_done, sl_done = Tally(sem("sf_done"), 2), Tally(sem("sh_done")), Tally(sem("sl_done"), 2)
        v_ready, v_free = Tally(sem("v_ready")), Tally(sem("v_free"), 2)
        va_out = [Tally(sem(f"va_out{t}"), 1, 16) for t in range(CT)]
        raw_ready, raw_step = Tally(sem("raw_ready"), 1), sem("raw_step")
        rel_ready, rexp_done, rmax_done = Tally(sem("rel_ready")), Tally(sem("rexp_done")), Tally(sem("rmax_done"))
        am_ready, am_done = Tally(sem("am_ready"), 1), Tally(sem("am_done"), 2)
        am_step = sem("am_step")
        stack_in = [Tally(sem(f"stack_in{r}"), 0, 16 * 13) for r in range(2)]
        k_ones = sem("k_ones")
        s_ready, mx_done = Tally(sem("s_ready")), Tally(sem("mx_done"), 2)
        st_ready, p_done = Tally(sem("st_ready")), Tally(sem("p_done"), 2)
        masked, pv_done = Tally(sem("masked")), Tally(sem("pv_done"), 2)
        mT_ready = Tally(sem("mT_ready"), 1)
        mh_done, mr_done = Tally(sem("mh_done")), Tally(sem("mr_done"))
        mm_done, ml_done = Tally(sem("mm_done")), Tally(sem("ml_done"))
        mrow_in = [Tally(sem(f"mrow_in{i}"), 1, 16 * 3 * GH) for i in range(2)]
        o_out, oT_ready = Tally(sem("o_out"), 1), Tally(sem("oT_ready"), 2)
        rden_done, L_done = Tally(sem("rden_done")), Tally(sem("L_done"), 1)
        L_out = [Tally(sem(f"L_out{r}"), 1, 16) for r in range(2)]

        def apart(eng):
            eng.nop(nofuse=True)

        def dve_stats(dve, n, chunk):
            if not first(n):
                dve.wait_ge(mv_done, n * CT)
                dve.wait_ge(ve_done, n)
                apart(dve)
            for t in range(CT):
                dve.bn_stats(stats[:, t, :], X[:, chunk * CT + t, :]).then_inc(st_done, 1)
            for t in range(CT):
                dve.wait_ge(st_done, n * CT + (t + 1))
                apart(dve)
                dve.bn_aggr(mv[:, t, :], stats[:, t, :]).then_inc(mv_done, 1)

        def pool_rstd(pool, n):
            pool.wait_ge(mv_done, n * CT + CT)
            if not first(n):
                pool.wait_ge(rs_done, n)
            apart(pool)
            pool.tensor_scalar(veps[:, :], mv[:, :, 1], LN_EPS, None, ALU.add).then_inc(ve_done, 1)
            pool.wait_ge(ve_done, n + 1)
            if not first(n):
                pool.wait_ge(xn_done, n * CT)
            pool.tensor_tensor(rstd[:, :], veps[:, :], neg_half[:, :], ALU.pow).then_inc(rs_done, 1)

        def dve_norm(dve, n, chunk):
            dve.wait_ge(rs_done, n + 1)
            if not first(n):
                dve.wait_ge(xTr_done, n * DK)
            for t in range(CT):
                dve.tensor_scalar(xn[:, t, :], X[:, chunk * CT + t, :], mv[:, t, 0:1], rstd[:, t:t + 1],
                                  ALU.subtract, ALU.mult).then_inc(xn_done, 1)

        def pe_xT(pe, n):
            pe.wait_ge(xn_done, n * CT + CT)
            if not first(n):
                pe.wait_ge(xl_done, n * DK)
            for k in range(DK):
                for t in range(CT):
                    last = pe.transpose(bank[k][:, t * P:(t + 1) * P], xn[:, t, k * P:(k + 1) * P], ident[:, :])
                last.then_inc(xTr_done, 1)

        def act_xT(act, n):
            for k in range(DK):
                act.wait_ge(xTr_done, n * DK + (k + 1))
                act.activation(xT[0][:, k, :], bank[k][:, :], ACT.Copy).then_inc(xh_done, 1)

        def dve_xT(dve, n):
            for k in range(DK):
                dve.wait_ge(xh_done, n * DK + (k + 1))
                dve.tensor_tensor(xT[1][:, k, :], bank[k][:, :], xT[0][:, k, :].bitcast(F32),
                                  ALU.subtract).then_inc(xl_done, 1)

        def products(pe, dst, w, x_, wi, xi, nk):
            n = 0
            for k in range(nk):
                for a, b in ((0, 0), (0, 1), (1, 0)):
                    last = pe.matmul(dst, wi(w[a], k), xi(x_[b], k), start=n == 0, stop=n == 3 * nk - 1)
                    n += 1
            return last

        def pe_ffn_up(pe, f, c, more):
            for j in range(FK):
                i = c * FK + j
                for w, dst, ready, free in ((wgs, half(j % 2), f.g_ready, f.silu_done),
                                            (wus, half(2 + j % 2), f.u_ready, f.mul_done)):
                    pe.wait_ge(free.sem, free.after(i - 2))
                    products(pe, dst, w, xT, lambda a, k: a[:, k, j * P:(j + 1) * P],
                             lambda a, k: a[:, k, :], DK).then_inc(ready.sem, 1)
                if f.second and more and j == 3:
                    pe_proj_T(pe, f, c + 1)

        def pe_ffn_down(pe, f, c, t):
            i = f.down_at(c) + t
            dst = bank[2 + t % 2][:, 0:D]
            pe.wait_ge(f.x_done.sem, f.x_done.after(i - 2))
            for j in range(FK):
                if t == 0:
                    pe.wait_ge(f.lo_done.sem, f.lo_done.after(c * FK + j))
                for n, (a, b) in enumerate(((0, 0), (0, 1), (1, 0))):
                    last = pe.matmul(dst, gT[a][:, j, t * P:(t + 1) * P], wds[b][:, j, :],
                                     start=j == 0 and n == 0, stop=j == FK - 1 and n == 2)
            last.then_inc(f.d_ready.sem, 1)

        def pe_proj_T(pe, f, c):
            pe.wait_ge(f.o_in.sem, f.o_in.after(c * GROUPS + (GROUPS - 1)))
            pe.wait_ge(xl_done, (c + 2 * CHUNKS) * DK)
            for k in range(DK):
                for t in range(CT):
                    last = pe.transpose(bank[k][:, t * P:(t + 1) * P],
                                        o_in[:, t, 2 * k:2 * k + 2, :].rearrange("p g e -> p (g e)"), ident[:, :])
                last.then_inc(f.oTr.sem, 1)

        def pe_proj(pe, f, c):
            for t in range(CT):
                dst = bank[2 + t % 2][:, 0:D]
                pe.wait_ge(f.x_done.sem, f.x_done.after(f.proj_at(c) + t - 2))
                pe.wait_ge(f.ol.sem, f.ol.after(c * DK + (DK - 1)))
                products(pe, dst, oT, wos, lambda a, k: a[:, k, t * P:(t + 1) * P],
                         lambda a, k: a[:, k, :], DK).then_inc(f.d_ready.sem, 1)

        def pe_ffn(pe, f, c, n_next):
            pe_ffn_up(pe, f, c, n_next is not None)
            if f.second and n_next is not None:
                pe_proj(pe, f, c + 1)
            for t in range(CT):
                if n_next is not None and t == (CT - 1 if f.second else 0):
                    pe_xT(pe, n_next)
                pe_ffn_down(pe, f, c, t)

        def act_ffn(act, f, c, n_next):
            def hi(j):
                i = c * FK + j
                act.wait_ge(f.mul_done.sem, f.mul_done.after(i))
                if j == 0:
                    act.wait_ge(f.d_ready.sem, f.d_ready.after(c * 2 * CT + (CT - 1) if f.second else c * CT - 1))
                act.activation(gT[0][:, j, :], gated[:, j % 2, :], ACT.Copy).then_inc(f.hi_done.sem, 1)

            for j in range(FK):
                i = c * FK + j
                act.wait_ge(f.g_ready.sem, f.g_ready.after(i))
                act.wait_ge(f.mul_done.sem, f.mul_done.after(i - 2))
                act.activation(silu[:, j % 2, :], half(j % 2), ACT.Silu).then_inc(f.silu_done.sem, 1)
                if j:
                    hi(j - 1)
                if f.second and n_next is not None and j == 4:
                    act_proj(act, f, c + 1)
            hi(FK - 1)
            if n_next is not None:
                act_xT(act, n_next)

        def act_proj(act, f, c):
            for k in range(DK):
                act.wait_ge(f.oTr.sem, f.oTr.after(c * DK + k))
                act.activation(oT[0][:, k, :], bank[k][:, :], ACT.Copy).then_inc(f.oh.sem, 1)

        def dve_proj_lo(dve, f, c):
            for k in range(DK):
                dve.wait_ge(f.oh.sem, f.oh.after(c * DK + k))
                dve.tensor_tensor(oT[1][:, k, :], bank[k][:, :], oT[0][:, k, :].bitcast(F32),
                                  ALU.subtract).then_inc(f.ol.sem, 1)

        def dve_residual(dve, f, chunk, i0, scale):
            for t in range(CT):
                dve.wait_ge(f.d_ready.sem, f.d_ready.after(i0 + t))
                dve.scalar_tensor_tensor(X[:, chunk * CT + t, :], bank[2 + t % 2][:, 0:D], scale,
                                         X[:, chunk * CT + t, :], ALU.mult, ALU.add).then_inc(f.x_done.sem, 1)

        def dve_ffn(dve, f, c, n_next, next_chunk):
            for j in range(FK):
                i = c * FK + j
                dve.wait_ge(f.silu_done.sem, f.silu_done.after(i))
                dve.wait_ge(f.u_ready.sem, f.u_ready.after(i))
                dve.wait_ge(f.lo_done.sem, f.lo_done.after(i - 2))
                dve.tensor_tensor(gated[:, j % 2, :], silu[:, j % 2, :], half(2 + j % 2),
                                  ALU.mult).then_inc(f.mul_done.sem, 1)
                if n_next is not None and not f.second:
                    if j == 2:
                        if f is ffn1:
                            dve.wait_ge(xr_in, 16 * (CHUNKS - 1))
                            if isinstance(c, int) and next_chunk == 0:
                                dve.wait_ge(f.x_done.sem, f.x_done.after(CT - 1))
                        dve_stats(dve, n_next, next_chunk)
                    if j == 5:
                        dve_norm(dve, n_next, next_chunk)
                if n_next is not None and f.second and j == 4:
                    dve_proj_lo(dve, f, c + 1)
            if n_next is not None and f.second:
                dve_residual(dve, f, next_chunk, f.proj_at(c + 1), 1.0)
                dve.wait_ge(f.x_done.sem, f.x_done.after(f.proj_at(c + 1) + (CT - 1)))
                dve_stats(dve, n_next, next_chunk)
                dve_down(dve, f, c, (0, 1))
                dve_norm(dve, n_next, next_chunk)
                dve_down(dve, f, c, (2,))
                dve_xT(dve, n_next)
                dve_down(dve, f, c, (3,))
            elif n_next is not None:
                dve_xT(dve, n_next)
                dve_down(dve, f, c, range(CT))
            else:
                dve_down(dve, f, c, range(CT))

        def dve_down(dve, f, c, ts):
            for t in ts:
                i = f.down_at(c) + t
                dve.wait_ge(f.d_ready.sem, f.d_ready.after(i))
                dve.scalar_tensor_tensor(X[:, c * CT + t, :], bank[2 + t % 2][:, 0:D], 0.5,
                                         X[:, c * CT + t, :], ALU.mult, ALU.add).then_inc(f.x_done.sem, 1)

        def pool_ffn(pool, f, c, n_next):
            for j in range(FK):
                i = c * FK + j
                pool.wait_ge(f.hi_done.sem, f.hi_done.after(i))
                pool.tensor_tensor(gT[1][:, j, :], gated[:, j % 2, :], gT[0][:, j, :].bitcast(F32),
                                   ALU.subtract).then_inc(f.lo_done.sem, 1)
                if j == 3 and n_next is not None and not f.second:
                    pool_rstd(pool, n_next)
            if n_next is not None and f.second:
                pool_rstd(pool, n_next)

        def stage_of(c):
            return c + 1

        block = ctx.enter_context(nc.Block())

        @block.sync
        def _(sp):
            x_v = x.rearrange("(n p) d -> p n d", p=P)
            out_v = out.rearrange("(n p) d -> p n d", p=P)
            sp.dma_start(X[:, 0:CT, :], x_v[:, 0:CT, :]).then_inc(x0_in, 16)
            sp.dma_start(wg_raw[:, :, :], wg).then_inc(w_in["wg"], 16)
            sp.dma_start(wd_raw[:, :, :], wd).then_inc(w_in["wd"], 16)
            for c in range(1, CHUNKS):
                sp.dma_start(X[:, c * CT:(c + 1) * CT, :], x_v[:, c * CT:(c + 1) * CT, :]).then_inc(xr_in, 16)
            sp.dma_start(nrm_raw[:, :, :], norms).then_inc(w_in["small"], 16)
            sp.dma_start(gate_sb[:, :], gate.partition_broadcast(P)).then_inc(w_in["small"], 16)
            for i, w in enumerate((wq, wk, wv, wo)):
                sp.dma_start(wqkvo_raw[:, i, :, :], w).then_inc(w_in["wqkvo"], 16)
            sp.dma_start(memT_raw[:, :, :, :], memT).then_inc(w_in["memT"], 16)

            for t in part_out + va_out:
                t.give(sp)

            def project_chunk(b, cc):
                k = b * 2 + cc
                for o in range(2 * DK):
                    dst = q_parts if o < DK else k_parts
                    for s, done in enumerate((ph_done, pm_done, pl_done)):
                        sp.wait_ge(done.sem, done.after(k * 4 + o))
                        sp.dma_start(dst[s, (o % DK) * P:(o % DK + 1) * P, bass.ds(b * S + cc * CW, CW)],
                                     part[s][:, o, :]).then_inc(part_out[o].sem, 16)
                for t in range(CT):
                    sp.wait_ge(v_free.sem, v_free.after(k * CT + t))
                    sp.dma_start(v_dram[b, :, :, cc * CT + t, :].rearrange("g p e -> p g e"),
                                 va[:, t, :, :].rearrange("p (g h) e -> p g (h e)", g=GROUPS)
                                 ).then_inc(va_out[t].sem, 16)

            with sp.Fori(0, B) as b:
                for cc in range(2):
                    project_chunk(b, cc)
            for t in part_out + va_out:
                sp.wait_ge(t.sem, t.after(2 * B - 1))
            sp.wait_ge(am_done.sem, am_done.after(B * BT - 1))

            mrow_in[0].give(sp)
            mrow_in[1].give(sp)
            for t in L_out:
                t.give(sp)

            def load(b, g):
                r = g % 2
                done = stack_in[r].sem
                for rows, src, dst in ((Q_ROWS, q_parts, Q), (K_ROWS, k_parts, K)):
                    for i, s in enumerate(rows):
                        v = src[s, g * GH * HD:(g + 1) * GH * HD, bass.ds(b * S, S)]
                        sp.dma_start(dst[i * HD:(i + 1) * HD, r, :, :],
                                     v.rearrange("(h d) t -> d h t", h=GH)).then_inc(done, 16)
                sp.dma_start(Vg[:, r, :, :], v_dram[b, g, :, :, :]).then_inc(done, 16)

            def max_rows(b, g, i):
                G = b * GROUPS + g
                for s, done in enumerate((mh_done, mm_done, ml_done)):
                    sp.wait_ge(done.sem, done.after(2 * G + i))
                    for h in range(GH):
                        dst = Q[PARTS + s:PARTS + s + 1, g % 2, h, i * CW:(i + 1) * CW]
                        sp.dma_start(dst.rearrange("o (t q) -> o t q", q=P),
                                     mx_part[s][h * CT:(h + 1) * CT, i, :]).then_inc(mrow_in[i].sem, 16)

            def core_turn(b, last=False):
                for g in range(GROUPS):
                    G = b * GROUPS + g
                    ahead = not (last and g == GROUPS - 1)
                    nb, ng = (b, g + 1) if g + 1 < GROUPS else (b + 1, 0)
                    if ahead:
                        sp.wait_ge(pv_done.sem, pv_done.after(G * NQ - 1))
                        load(nb, ng)
                    max_rows(b, g, 1)
                    if ahead:
                        max_rows(nb, ng, 0)
                    sp.wait_ge(L_done.sem, L_done.after(2 * G + 1))
                    sp.dma_start(o_dram[b, g, :, :, :], Lg[:, g % 2, :, :]).then_inc(L_out[g % 2].sem, 16)

            load(0, 0)
            max_rows(0, 0, 0)
            with sp.Fori(0, B - 1) as b:
                core_turn(b)
            core_turn(B - 1, True)
            for t in L_out:
                sp.wait_ge(t.sem, t.after(2 * B - 1))

            def load_o(b, cc):
                for g in range(GROUPS):
                    sp.dma_start(o_in[:, :, g, :], o_dram[b, g, :, cc * CT:(cc + 1) * CT, :]).then_inc(ffn2.o_in.sem, 16)

            load_o(0, 0)
            sp.wait_ge(ffn2.oTr.sem, ffn2.oTr.after(DK - 1))
            load_o(0, 1)

            def ffn2_pair(b, last=False):
                for cc in range(2):
                    c = b * 2 + cc
                    if not last:
                        sp.wait_ge(ffn2.oTr.sem, ffn2.oTr.after((c + 1) * DK + (DK - 1)))
                        load_o(b + 1, cc)
                    sp.wait_ge(ffn2.x_done.sem, ffn2.x_done.after(ffn2.down_at(c) + (CT - 1)))
                    sp.dma_start(out_v[:, bass.ds(c * CT, CT), :],
                                 X[:, bass.ds(c * CT, CT), :]).then_inc(ffn2.stored, 16)

            with sp.Fori(0, B - 1) as b:
                ffn2_pair(b)
            ffn2_pair(B - 1, True)
            sp.wait_ge(ffn2.stored, 16 * CHUNKS)

        @block.gpsimd
        def _(pool):
            pool.memset(neg_half[:, :], -0.5).then_inc(consts, 1)
            pool.memset(ident[:, :], 0.0).then_inc(ident_ok, 1)
            pool.memset(mask[:, :], 0.0).then_inc(ident_ok, 1)
            pool.memset(mean_w[:, :], 1.0 / S).then_inc(consts, 1)
            pool.wait_ge(ident_ok, 2)
            pool.affine_select(out=ident[:, :], in_=ident[:, :], compare_op=ALU.not_equal, fill=1.0, base=0,
                               pattern=[[-1, P]], channel_multiplier=1).then_inc(consts, 1)
            tri = mask[:, S - P:S]
            pool.affine_select(out=tri, in_=tri, compare_op=ALU.is_ge, fill=MASKED, base=0,
                               pattern=[[-1, P]], channel_multiplier=1).then_inc(consts, 1)
            pool.wait_ge(consts, 4)
            pool_rstd(pool, 0)
            pool.wait_ge(w_hi, 3)
            for t in (ffn1.lo_done, ffn2.lo_done):
                t.give(pool)
            pool.tensor_tensor(wds[1][:, :, :], wd_raw[:, :, :], wds[0][:, :, :].bitcast(F32),
                               ALU.subtract).then_inc(w_lo, 1)
            with pool.Fori(0, CHUNKS - 1) as c:
                pool_ffn(pool, ffn1, c, c + 1)
            pool_ffn(pool, ffn1, CHUNKS - 1, CHUNKS)

            for i, w in enumerate((wqs, wks, wvs, wos)):
                pool.wait_ge(sp_hi, i + 1)
                pool.tensor_tensor(w[1][:, :, :], wqkvo_raw[:, i, :, :], w[0][:, :, :].bitcast(F32),
                                   ALU.subtract).then_inc(sp_lo, 1)
            pool.wait_ge(sp_hi, 6)
            pool.tensor_tensor(nrm[1][:, :, :], nrm_raw[:, :, :], nrm[0][:, :, :].bitcast(F32),
                               ALU.subtract).then_inc(sp_lo, 1)
            pool.tensor_tensor(memTs[1][:, :, :, :], memT_raw[:, :, :, :], memTs[0][:, :, :, :].bitcast(F32),
                               ALU.subtract).then_inc(sp_lo, 1)
            pool.wait_ge(sp_lo, 6)
            pool.memset(va[:, :, :, HD:VW], 1.0).then_inc(va_ones, 1)
            pl_done.give(pool)
            sl_done.give(pool)

            def project_chunk(b, cc):
                k = b * 2 + cc
                for o in range(2 * DK):
                    i = k * 4 + o
                    pool.wait_ge(rest_done.sem, rest_done.after(i))
                    pool.wait_ge(part_out[o].sem, part_out[o].after(k - 1))
                    apart(pool)
                    pool.tensor_copy(part[1][:, o, :], rest[:, o % 2, :]).then_inc(pm_done.sem, 1)
                    pool.wait_ge(pm_done.sem, pm_done.after(i))
                    pool.tensor_tensor(part[2][:, o, :], rest[:, o % 2, :], part[1][:, o, :],
                                       ALU.subtract).then_inc(pl_done.sem, 1)
                    if o < DK:
                        j = k * DK + o
                        pool.wait_ge(sh_done.sem, sh_done.after(j))
                        pool.tensor_tensor(sig[1][:, o, cc * CW:(cc + 1) * CW], sig_f[:, o, :],
                                           sig[0][:, o, cc * CW:(cc + 1) * CW].bitcast(F32),
                                           ALU.subtract).then_inc(sl_done.sem, 1)

            def pool_project(b, last=False):
                for cc in range(2):
                    if not (last and cc == 1):
                        pool_rstd(pool, b * 2 + (cc + CHUNKS + 1))
                    project_chunk(b, cc)

            with pool.Fori(0, B - 1) as b:
                pool_project(b)
            pool_project(B - 1, True)

            pool.wait_ge(am_done.sem, am_done.after(B * BT - 1))
            for t in part_out + va_out:
                pool.wait_ge(t.sem, t.after(2 * B - 1))
            pool.memset(K[PARTS:ROWS, :, :, :], 1.0).then_inc(k_ones, 1)

            def core_maxrows(b, g, i):
                m = 2 * (b * GROUPS + g) + i
                pool.wait_ge(mr_done.sem, mr_done.after(m))
                pool.wait_ge(mrow_in[i].sem, mrow_in[i].after(b * GROUPS + (g - 1)))
                apart(pool)
                pool.tensor_copy(mx_part[1][:, i, :], mx_rest[:, i, :]).then_inc(mm_done.sem, 1)
                pool.wait_ge(mm_done.sem, mm_done.after(m))
                pool.tensor_tensor(mx_part[2][:, i, :], mx_rest[:, i, :], mx_part[1][:, i, :],
                                   ALU.subtract).then_inc(ml_done.sem, 1)

            def core_turn(b, last=False):
                for g in range(GROUPS):
                    G = b * GROUPS + g
                    ahead = not (last and g == GROUPS - 1)
                    for step, *a in timeline(ahead):
                        if step == "scores2":
                            i = a[0]
                            if QUADS[i][3]:
                                pool.wait_ge(p_done.sem, p_done.after((G * NQ + i) * GH + (GH - 1)))
                                diag = PT[:, (i % 2) * GH:(i % 2 + 1) * GH, 0:P]
                                apart(pool)
                                pool.affine_select(out=diag, in_=diag, compare_op=ALU.is_ge, fill=0.0, base=0,
                                                   pattern=[[0, GH], [1, P]],
                                                   channel_multiplier=-1).then_inc(masked.sem, 1)
                        elif step == "maxrows":
                            nb, ng = (b, g + a[0]) if g + a[0] < GROUPS else (b + 1, 0)
                            core_maxrows(nb, ng, a[1])

            core_maxrows(0, 0, 0)
            with pool.Fori(0, B - 1) as b:
                core_turn(b)
            core_turn(B - 1, True)

            pool_rstd(pool, 2 * CHUNKS)
            with pool.Fori(0, CHUNKS - 1) as c:
                pool_ffn(pool, ffn2, c, c + (2 * CHUNKS + 1))
            pool_ffn(pool, ffn2, CHUNKS - 1, None)

        @block.scalar
        def _(act):
            act.dma_start(wu_raw[:, :, :], wu).then_inc(w_in["wu"], 16)
            for t in (ffn1.silu_done, ffn2.silu_done):
                t.give(act)
            act.preload_act_table(ACT.Silu)
            for n, dst, src in (("wg", wgs, wg_raw), ("wu", wus, wu_raw), ("wd", wds, wd_raw)):
                act.wait_ge(w_in[n], 16)
                act.activation(dst[0][:, :, :], src[:, :, :], ACT.Copy).then_inc(w_hi, 1)
                if n == "wg":
                    act_xT(act, 0)
            with act.Fori(0, CHUNKS - 1) as c:
                act_ffn(act, ffn1, c, c + 1)
            act_ffn(act, ffn1, CHUNKS - 1, CHUNKS)

            act.preload_act_table(ACT.Exp)
            act.wait_ge(w_in["wqkvo"], 64)
            for i, w in enumerate((wqs, wks, wvs, wos)):
                act.activation(w[0][:, :, :], wqkvo_raw[:, i, :, :], ACT.Copy).then_inc(sp_hi, 1)
            act.wait_ge(w_in["small"], 32)
            act.activation(nrm[0][:, :, :], nrm_raw[:, :, :], ACT.Copy).then_inc(sp_hi, 1)
            act.wait_ge(w_in["memT"], 16)
            act.wait_ge(ffn1.d_ready.sem, ffn1.d_ready.after(CHUNKS * CT - 1))
            act.activation(memTs[0][:, :, :, :], memT_raw[:, :, :, :], ACT.Copy).then_inc(sp_hi, 1)
            act.activation(gate_e[:, :], gate_sb[:, :], ACT.Exp, scale=-1.0).then_inc(gate_step, 1)
            for i in range(DK * MEM):
                act.wait_ge(mwo_ready.sem, mwo_ready.after(i))
                act.activation(mwo[0][:, i // MEM, (i % MEM) * D:(i % MEM + 1) * D], half(i % 2)[:, 0:D],
                               ACT.Copy).then_inc(mwo_hi, 1)
            qe_done.give(act)
            v_free.give(act)
            act.wait_ge(va_ones, 1)

            def project_chunk(b, cc, more):
                k = b * 2 + cc
                for o in range(2 * DK):
                    i = k * 4 + o
                    act.wait_ge(qk_ready.sem, qk_ready.after(i))
                    act.wait_ge(part_out[o].sem, part_out[o].after(k - 1))
                    act.activation(part[0][:, o, :], half(o % 2), ACT.Copy).then_inc(ph_done.sem, 1)
                    if o < DK:
                        j = k * DK + o
                        act.wait_ge(min_done.sem, min_done.after(j))
                        act.wait_ge(sf_done.sem, sf_done.after(j - 2))
                        act.activation(q_exp[:, o, :], q_min[:, o, :], ACT.Exp).then_inc(qe_done.sem, 1)
                        act.wait_ge(sf_done.sem, sf_done.after(j))
                        act.wait_ge(am_ready.sem, am_ready.after(b * BT - 1))
                        act.activation(sig[0][:, o, cc * CW:(cc + 1) * CW], sig_f[:, o, :],
                                       ACT.Copy).then_inc(sh_done.sem, 1)
                for t in range(CT):
                    act.wait_ge(v_ready.sem, v_ready.after(k * CT + t))
                    act.wait_ge(va_out[t].sem, va_out[t].after(k - 1))
                    act.activation(va[:, t, :, 0:HD], half(2 + t % 2)[:, 0:D].rearrange("p (h e) -> p h e", h=HEADS),
                                   ACT.Copy).then_inc(v_free.sem, 1)
                if more:
                    act_xT(act, k + (CHUNKS + 1))

            def act_project(b, last=False):
                for cc in range(2):
                    project_chunk(b, cc, not (last and cc == 1))
                act.wait_ge(rmax_done.sem, rmax_done.after(b))
                act.activation(rexp[:, :], rel[:, :], ACT.Exp, bias=rmax[:, 0:1],
                               accum_out=rsum[:, 0:1]).then_inc(rexp_done.sem, 1)

            with act.Fori(0, B - 1) as b:
                act_project(b)
            act_project(B - 1, True)

            p_done.give(act)
            o_out.give(act)
            act.wait_ge(am_done.sem, am_done.after(B * BT - 1))

            def core_maxrows(b, g, i):
                m = 2 * (b * GROUPS + g) + i
                act.wait_ge(mT_ready.sem, mT_ready.after(m))
                act.wait_ge(mrow_in[i].sem, mrow_in[i].after(b * GROUPS + (g - 1)))
                act.activation(mx_part[0][:, i, :], bank[3][0:CT * GH, 0:P], ACT.Copy, scale=-1.0).then_inc(mh_done.sem, 1)

            def core_turn(b, last=False):
                for g in range(GROUPS):
                    G = b * GROUPS + g
                    ahead = not (last and g == GROUPS - 1)
                    for step, *a in timeline(ahead):
                        if step == "scores2":
                            i = a[0]
                            w = QUADS[i][2]
                            act.wait_ge(pv_done.sem, pv_done.after(G * NQ + i - 2))
                            for h in range(GH):
                                n = (G * NQ + i) * GH + h
                                act.wait_ge(st_ready.sem, st_ready.after(n))
                                act.activation(PT[:, (i % 2) * GH + h, 0:w], bank[h % 2][:, 0:w], ACT.Exp,
                                               scale=SCALE).then_inc(p_done.sem, 1)
                        elif step == "maxrows":
                            nb, ng = (b, g + a[0]) if g + a[0] < GROUPS else (b + 1, 0)
                            core_maxrows(nb, ng, a[1])
                        elif step == "pv" and a[0] in LAST_QUAD:
                            qc = LAST_QUAD.index(a[0])
                            act.wait_ge(pv_done.sem, pv_done.after(G * NQ + a[0]))
                            act.wait_ge(oT_ready.sem, oT_ready.after(2 * G + qc - 2))
                            act.activation(Osb[:, qc, :], bank[2][:, :], ACT.Copy).then_inc(o_out.sem, 1)

            core_maxrows(0, 0, 0)
            with act.Fori(0, B - 1) as b:
                core_turn(b)
            core_turn(B - 1, True)

            act.preload_act_table(ACT.Silu)
            act_proj(act, ffn2, 0)
            act_xT(act, 2 * CHUNKS)
            with act.Fori(0, CHUNKS - 1) as c:
                act_ffn(act, ffn2, c, c + (2 * CHUNKS + 1))
            act_ffn(act, ffn2, CHUNKS - 1, None)

        @block.vector
        def _(dve):
            for f in (ffn1, ffn2):
                f.mul_done.give(dve)
                f.x_done.give(dve)
            dve.wait_ge(x0_in, 16)
            dve_stats(dve, 0, 0)
            dve_norm(dve, 0, 0)
            dve.wait_ge(w_hi, 1)
            dve.tensor_tensor(wgs[1][:, :, :], wg_raw[:, :, :], wgs[0][:, :, :].bitcast(F32),
                              ALU.subtract).then_inc(w_lo, 1)
            dve_xT(dve, 0)
            dve.wait_ge(w_hi, 2)
            dve.tensor_tensor(wus[1][:, :, :], wu_raw[:, :, :], wus[0][:, :, :].bitcast(F32),
                              ALU.subtract).then_inc(w_lo, 1)
            with dve.Fori(0, CHUNKS - 1) as c:
                dve_ffn(dve, ffn1, c, c + 1, c + 1)
            dve_ffn(dve, ffn1, CHUNKS - 1, CHUNKS, 0)

            dve.wait_ge(gate_step, 1)
            dve.tensor_scalar(gate_d[:, :], gate_e[:, :], 1.0, None, ALU.add).then_inc(gate_step, 1)
            dve.wait_ge(gate_step, 2)
            dve.reciprocal(g_mem[:, :], gate_d[:, :]).then_inc(gate_step, 1)
            dve.wait_ge(gate_step, 3)
            dve.tensor_scalar(g_loc[:, :], g_mem[:, :], -1.0, 1.0, ALU.mult, ALU.add).then_inc(gate_step, 1)
            dve.wait_ge(gate_step, 4)
            mwo_lo.give(dve)
            for i in range(DK * MEM):
                dve.wait_ge(mwo_hi, i + 1)
                at = (slice(None), i // MEM, slice((i % MEM) * D, (i % MEM + 1) * D))
                dve.tensor_tensor(mwo[1][at], half(i % 2)[:, 0:D], mwo[0][at].bitcast(F32),
                                  ALU.subtract).then_inc(mwo_lo.sem, 1)
            for t in (rest_done, sf_done, am_done):
                t.give(dve)
            dve.wait_ge(ffn1.x_done.sem, ffn1.x_done.after(CHUNKS * CT - 1))

            def project_chunk(b, cc, more):
                k = b * 2 + cc
                for o in range(2 * DK):
                    i = k * 4 + o
                    src = half(o % 2)
                    dve.wait_ge(ph_done.sem, ph_done.after(i))
                    dve.wait_ge(pl_done.sem, pl_done.after(i - 2))
                    last = dve.tensor_tensor(rest[:, o % 2, :], src, part[0][:, o, :], ALU.subtract)
                    last.then_inc(rest_done.sem, 1)
                    if o < DK:
                        j = k * DK + o
                        dve.wait_ge(qe_done.sem, qe_done.after(j - 2))
                        dve.tensor_scalar(q_min[:, o, :], src, 0.0, None, ALU.min).then_inc(min_done.sem, 1)
                        dve.wait_ge(qe_done.sem, qe_done.after(j))
                        dve.wait_ge(sl_done.sem, sl_done.after(j - 2))
                        dve.scalar_tensor_tensor(sig_f[:, o, :], src, 0.0, q_exp[:, o, :], ALU.max,
                                                 ALU.add).then_inc(sf_done.sem, 1)
                    if more and o == 1:
                        dve_stats(dve, k + (CHUNKS + 1), k + 1)
                if more:
                    dve_norm(dve, k + (CHUNKS + 1), k + 1)
                    dve_xT(dve, k + (CHUNKS + 1))

            def dve_project(b, last=False):
                for cc in range(2):
                    project_chunk(b, cc, not (last and cc == 1))
                dve.wait_ge(raw_ready.sem, raw_ready.after(b * BT + (BT - 1)))
                raw = bank[2][:, 0:BT * MEM].rearrange("p (t m) -> p t m", m=MEM)
                dve.tensor_copy(raw_sb[:, :, :], raw).then_inc(raw_step, 1)
                dve.tensor_scalar(rawc[:, :, :], raw, MEM_EPS, None, ALU.max).then_inc(raw_step, 1)
                dve.wait_ge(raw_step, RAW * b + 2)
                dve.reciprocal(rinv[:, :, :], rawc[:, :, :]).then_inc(raw_step, 1)
                dve.wait_ge(rel_ready.sem, rel_ready.after(b))
                dve.tensor_copy(rel[:, :], bank[3][:, 0:MEM]).then_inc(raw_step, 1)
                dve.wait_ge(raw_step, RAW * b + 4)
                dve.tensor_reduce(rmax[:, :], rel[:, :], AX.X, ALU.max, negate=True).then_inc(rmax_done.sem, 1)
                dve.wait_ge(rexp_done.sem, rexp_done.after(b))
                dve.reciprocal(rnorm[:, :], rsum[:, :]).then_inc(raw_step, 1)
                dve.wait_ge(raw_step, RAW * b + 5)
                dve.tensor_scalar(wmem[:, :], rexp[:, :], rnorm[:, 0:1], g_mem[:, 0:1], ALU.mult,
                                  ALU.mult).then_inc(raw_step, 1)
                dve.wait_ge(raw_step, RAW * b + 6)
                dve.tensor_tensor(coef[:, :, :], rinv[:, :, :], wmem[:, :].unsqueeze(1).broadcast_to([P, BT, MEM]),
                                  ALU.mult).then_inc(raw_step, 1)
                dve.wait_ge(raw_step, RAW * b + 7)
                for t in range(BT):
                    i = b * BT + t
                    dve.wait_ge(am_ready.sem, am_ready.after(i))
                    for m in range(MEM):
                        tile = X[:, b * BT + t, :]
                        last = dve.scalar_tensor_tensor(tile, big[t % 2][:, m * D:(m + 1) * D], coef[:, t, m:m + 1],
                                                        tile, ALU.mult, ALU.add)
                        if m < MEM - 1:
                            last.then_inc(am_step, 1)
                            dve.wait_ge(am_step, i * (MEM - 1) + (m + 1))
                    last.then_inc(am_done.sem, 1)

            with dve.Fori(0, B - 1) as b:
                dve_project(b)
            dve_project(B - 1, True)

            dve.wait_ge(am_done.sem, am_done.after(B * BT - 1))
            mx_done.give(dve)
            L_done.give(dve)

            def row_max(b, g, u):
                G = b * GROUPS + g
                qt, h = UNITS[u]
                n = (qt + 1) * P
                s = big[u % 2][:, 0:n]
                col = qt // CT * (NU // 2) + h * CT + qt % CT
                dve.wait_ge(s_ready.sem, s_ready.after(G * NU + u))
                if u == 0 and not first(G):
                    dve.wait_ge(mT_ready.sem, mT_ready.after(2 * G - 3))
                apart(dve)
                dve.tensor_tensor_reduce(out=s, in0=s, in1=mask[:, S - n:S], scale=1.0, scalar=-3.0e38,
                                         op0=ALU.add, op1=ALU.max,
                                         accum_out=rmx[:, g % 2, col:col + 1]).then_inc(mx_done.sem, 1)

            def core_maxrows(b, g, i):
                m = 2 * (b * GROUPS + g) + i
                dve.wait_ge(mh_done.sem, mh_done.after(m))
                dve.wait_ge(mrow_in[i].sem, mrow_in[i].after(b * GROUPS + (g - 1)))
                dve.scalar_tensor_tensor(mx_rest[:, i, :], bank[3][0:CT * GH, 0:P], -1.0, mx_part[0][:, i, :],
                                         ALU.mult, ALU.subtract).then_inc(mr_done.sem, 1)

            def heads_out(b, g, qc):
                G = b * GROUPS + g
                i = 2 * G + qc
                o = bank[3][:, :].rearrange("p (x e) -> p x e", e=VW)
                dve.wait_ge(oT_ready.sem, oT_ready.after(i))
                dve.reciprocal(rden[:, qc, :], o[:, :, HD]).then_inc(rden_done.sem, 1)
                dve.wait_ge(rden_done.sem, rden_done.after(i))
                if qc == 0:
                    dve.wait_ge(L_out[g % 2].sem, L_out[g % 2].after(b * 2 + (g // 2 - 1)))
                dve.scalar_tensor_tensor(
                    Lg[:, g % 2, qc * CT:(qc + 1) * CT, :].rearrange("p t (h e) -> p (t h) e", e=HD),
                    o[:, :, 0:HD], g_loc[:, 0:1], rden[:, qc, :].unsqueeze(2).broadcast_to([P, CT * GH, HD]),
                    ALU.mult, ALU.mult).then_inc(L_done.sem, 1)

            def core_turn(b, last=False):
                for g in range(GROUPS):
                    ahead = not (last and g == GROUPS - 1)
                    nb, ng = (b, g + 1) if g + 1 < GROUPS else (b + 1, 0)
                    for step, *a in timeline(ahead):
                        if step == "scores1":
                            row_max(nb, ng, a[0])
                        elif step == "maxrows":
                            core_maxrows(*((nb, ng) if a[0] else (b, g)), a[1])
                        elif step == "outT":
                            heads_out(b, g, a[0])

            for u in range(NU):
                row_max(0, 0, u)
                if u == NU // 2 + 2:
                    core_maxrows(0, 0, 0)
            with dve.Fori(0, B - 1) as b:
                core_turn(b)
            core_turn(B - 1, True)

            dve_proj_lo(dve, ffn2, 0)
            dve_residual(dve, ffn2, 0, 0, 1.0)
            dve.wait_ge(ffn2.x_done.sem, ffn2.x_done.after(CT - 1))
            dve_stats(dve, 2 * CHUNKS, 0)
            dve_norm(dve, 2 * CHUNKS, 0)
            dve_xT(dve, 2 * CHUNKS)
            with dve.Fori(0, CHUNKS - 1) as c:
                dve_ffn(dve, ffn2, c, c + (2 * CHUNKS + 1), c + 1)
            dve_ffn(dve, ffn2, CHUNKS - 1, None, None)

        @block.tensor
        def _(pe):
            pe.wait_ge(consts, 4)
            for f in (ffn1, ffn2):
                f.d_ready.give(pe)
            pe_xT(pe, 0)
            pe.wait_ge(xl_done, DK)
            pe.wait_ge(w_lo, 2)
            pe.wait_ge(w_lo, 3)
            with pe.Fori(0, CHUNKS - 1) as c:
                pe.wait_ge(xl_done, c * DK + DK)
                pe_ffn(pe, ffn1, c, c + 1)
            pe.wait_ge(xl_done, CHUNKS * DK)
            pe_ffn(pe, ffn1, CHUNKS - 1, CHUNKS)

            pe.wait_ge(sp_lo, 6)
            for i in range(DK * MEM):
                dk, m = i // MEM, i % MEM
                if i >= 2:
                    pe.wait_ge(mwo_lo.sem, mwo_lo.after(i - 2))
                products(pe, half(i % 2)[:, 0:D], memTs, wos, lambda a, k: a[:, m, k, dk * P:(dk + 1) * P],
                         lambda a, k: a[:, k, :], DK).then_inc(mwo_ready.sem, 1)
            pe.wait_ge(mwo_lo.sem, mwo_lo.after(DK * MEM - 1))
            am_ready.give(pe)
            raw_ready.give(pe)

            def project_chunk(b, cc, more):
                k = b * 2 + cc
                pe.wait_ge(xl_done, (k + CHUNKS) * DK + DK)
                for o in range(2 * DK):
                    i = k * 4 + o
                    w = wqs if o < DK else wks
                    if o < DK:
                        pe.wait_ge(rest_done.sem, rest_done.after(i - 2))
                    else:
                        pe.wait_ge(sf_done.sem, sf_done.after(k * DK + o - DK))
                    if cc == 0 and o < 2:
                        pe.wait_ge(am_done.sem, am_done.after(b * BT - 2))
                    products(pe, half(o % 2), w, xT, lambda a, kk: a[:, kk, (o % DK) * P:(o % DK + 1) * P],
                             lambda a, kk: a[:, kk, :], DK).then_inc(qk_ready.sem, 1)
                for t in range(CT):
                    pe.wait_ge(v_free.sem, v_free.after(k * CT + t - 2))
                    if cc == 0 and t < 2:
                        pe.wait_ge(am_done.sem, am_done.after(b * BT - 1))
                    products(pe, half(2 + t % 2)[:, 0:D], xT, wvs, lambda a, kk: a[:, kk, t * P:(t + 1) * P],
                             lambda a, kk: a[:, kk, :], DK).then_inc(v_ready.sem, 1)
                if more:
                    pe_xT(pe, k + (CHUNKS + 1))

            def pe_project(b, last=False):
                for cc in range(2):
                    project_chunk(b, cc, not (last and cc == 1))
                pe.wait_ge(sl_done.sem, sl_done.after(b * 4 + 3))
                for t in range(BT):
                    products(pe, bank[2][:, t * MEM:(t + 1) * MEM], sig, nrm, lambda a, k: a[:, k, t * P:(t + 1) * P],
                             lambda a, k: a[:, k, :], DK).then_inc(raw_ready.sem, 1)
                pe.wait_ge(raw_step, RAW * b + 1)
                for t in range(BT):
                    m = pe.matmul(bank[3][:, 0:MEM], mean_w[:, :], raw_sb[:, t, :], start=t == 0, stop=t == BT - 1)
                m.then_inc(rel_ready.sem, 1)
                pe.wait_ge(rest_done.sem, rest_done.after(b * 8 + 7))
                pe.wait_ge(v_free.sem, v_free.after(b * 8 + 7))
                for t in range(BT):
                    pe.wait_ge(am_done.sem, am_done.after(b * BT + t - 2))
                    for hf in range(2):
                        last = products(pe, big[t % 2][:, hf * CW:(hf + 1) * CW], sig, mwo,
                                        lambda a, k: a[:, k, t * P:(t + 1) * P],
                                        lambda a, k: a[:, k, hf * CW:(hf + 1) * CW], DK)
                    last.then_inc(am_ready.sem, 1)

            with pe.Fori(0, B - 1) as b:
                pe_project(b)
            pe_project(B - 1, True)

            pe.wait_ge(am_done.sem, am_done.after(B * BT - 1))
            pv_done.give(pe)
            mT_ready.give(pe)
            oT_ready.give(pe)

            def scores1(b, g, u):
                r, (qt, h) = g % 2, UNITS[u]
                n = (qt + 1) * P
                pe.wait_ge(mx_done.sem, mx_done.after((b * GROUPS + g) * NU + u - 2))
                if u == 0:
                    pe.wait_ge(stack_in[r].sem, stack_in[r].after(b * 2 + g // 2))
                for k0 in range(0, n, CW):
                    k1 = min(k0 + CW, n)
                    last = pe.matmul(big[u % 2][:, k0:k1], Q[0:PARTS, r, h, qt * P:(qt + 1) * P],
                                     K[0:PARTS, r, h, k0:k1], start=True, stop=True)
                last.then_inc(s_ready.sem, 1)

            def scores2(b, g, i):
                r, (qc, kb, w, _) = g % 2, QUADS[i]
                G = b * GROUPS + g
                if i in (0, CT):
                    pe.wait_ge(mrow_in[qc].sem, mrow_in[qc].after(G))
                for h in range(GH):
                    n = (G * NQ + i) * GH + h
                    pe.wait_ge(p_done.sem, p_done.after(n - 2))
                    q1 = (qc + 1) * CW
                    pe.matmul(bank[h % 2][:, 0:w], K[0:ROWS, r, h, kb * P:(kb + 1) * P],
                              Q[0:ROWS, r, h, q1 - w:q1], start=True, stop=True).then_inc(st_ready.sem, 1)

            def pv(b, g, i):
                r, (qc, kb, w, diag) = g % 2, QUADS[i]
                G = b * GROUPS + g
                if kb == 0:
                    pe.wait_ge(o_out.sem, o_out.after(2 * G + qc - 1))
                if diag:
                    pe.wait_ge(masked.sem, masked.after(G * NDIAG + DIAG[i]))
                else:
                    pe.wait_ge(p_done.sem, p_done.after((G * NQ + i) * GH + (GH - 1)))
                for h in range(GH):
                    last = pe.matmul(bank[2][h * VW:(h + 1) * VW, CW - w:CW], Vg[:, r, kb, h * VW:(h + 1) * VW],
                                     PT[:, (i % 2) * GH + h, 0:w], start=kb == 0, stop=i in LAST_QUAD)
                last.then_inc(pv_done.sem, 1)

            def core_maxrows(b, g, i):
                m = 2 * (b * GROUPS + g) + i
                if not first(m):
                    pe.wait_ge(mr_done.sem, mr_done.after(m - 1))
                if i == 1:
                    pe.wait_ge(L_done.sem, L_done.after(m - 2))
                pe.wait_ge(mx_done.sem, mx_done.after((b * GROUPS + g) * NU + (i + 1) * (NU // 2) - 1))
                n = NU // 2
                pe.transpose(bank[3][0:n, 0:P], rmx[:, g % 2, i * n:(i + 1) * n], ident[:, :]).then_inc(mT_ready.sem, 1)

            def core_outT(b, g, qc, ahead):
                i = 2 * (b * GROUPS + g) + qc
                if qc == 0:
                    pe.wait_ge(mr_done.sem, mr_done.after(i + 1 + ahead))
                else:
                    pe.wait_ge(L_done.sem, L_done.after(i - 1))
                pe.wait_ge(o_out.sem, o_out.after(i))
                for t in range(CT):
                    last = pe.transpose(bank[3][:, t * P:(t + 1) * P], Osb[:, qc, t * P:(t + 1) * P], ident[:, :])
                last.then_inc(oT_ready.sem, 1)

            def core_turn(b, last=False):
                for g in range(GROUPS):
                    ahead = not (last and g == GROUPS - 1)
                    nb, ng = (b, g + 1) if g + 1 < GROUPS else (b + 1, 0)
                    for step, *a in timeline(ahead):
                        if step == "scores1":
                            scores1(nb, ng, a[0])
                        elif step == "scores2":
                            scores2(b, g, a[0])
                        elif step == "pv":
                            pv(b, g, a[0])
                        elif step == "maxrows":
                            core_maxrows(*((nb, ng) if a[0] else (b, g)), a[1])
                        elif step == "outT":
                            core_outT(b, g, a[0], ahead)

            pe.wait_ge(k_ones, 1)
            for u in range(NU):
                scores1(0, 0, u)
                if u == NU // 2 + 2:
                    core_maxrows(0, 0, 0)
            with pe.Fori(0, B - 1) as b:
                core_turn(b)
            core_turn(B - 1, True)

            pe.wait_ge(L_done.sem, L_done.after(2 * B * GROUPS - 1))
            pe_proj_T(pe, ffn2, 0)
            pe_proj(pe, ffn2, 0)
            pe_xT(pe, 2 * CHUNKS)
            with pe.Fori(0, CHUNKS - 1) as c:
                pe.wait_ge(xl_done, c * DK + (2 * CHUNKS + 1) * DK)
                pe_ffn(pe, ffn2, c, c + (2 * CHUNKS + 1))
            pe.wait_ge(xl_done, 3 * CHUNKS * DK)
            pe_ffn(pe, ffn2, CHUNKS - 1, None)


_INS = ("x", "wg", "wu", "wd", "wq", "wk", "wv", "wo", "memT", "norms", "gate")


def kernel(L0_attn_x, L0_attn_w_q, L0_attn_w_k, L0_attn_w_v, L0_attn_w_o, L0_attn_gate, L0_attn_memories,
           L0_attn_memory_norms, L0_ffn_w_gate, L0_ffn_w_up, L0_ffn_w_down):
    import numpy as np
    import concourse.bacc as bacc
    from concourse.bass_utils import run_bass_kernel_spmd

    def by_partition(w):
        k, n = w.shape
        return w.reshape(k // P, P, n).transpose(1, 0, 2)

    mem = np.asarray(L0_attn_memories).transpose(2, 0, 1)
    data = dict(
        x=np.asarray(L0_attn_x).reshape(TOK, D),
        wg=by_partition(np.asarray(L0_ffn_w_gate).T), wu=by_partition(np.asarray(L0_ffn_w_up).T),
        wd=by_partition(np.asarray(L0_ffn_w_down).T),
        wq=by_partition(np.asarray(L0_attn_w_q).T), wk=by_partition(np.asarray(L0_attn_w_k).T),
        wv=by_partition(np.asarray(L0_attn_w_v).T), wo=by_partition(np.asarray(L0_attn_w_o).T),
        memT=mem.reshape(DK, P, MEM, D).transpose(1, 2, 0, 3),
        norms=by_partition(np.asarray(L0_attn_memory_norms).T),
        gate=np.asarray(L0_attn_gate),
    )
    nc = bacc.Bacc("TRN2", target_bir_lowering=False, num_devices=1)
    arrays, args = {}, []
    for name in _INS:
        a = np.ascontiguousarray(data[name])
        arrays["in_" + name] = a
        args.append(nc.dram_tensor("in_" + name, a.shape, mybir.dt.from_np(a.dtype), kind="ExternalInput").ap())
    args.append(nc.dram_tensor("out_0", (TOK, D), F32, kind="ExternalOutput").ap())
    build(nc, *args)
    r = run_bass_kernel_spmd(nc, [arrays], core_ids=[0])
    return r.results[0]["out_0"].reshape(B, S, D)
```

```python
from contextlib import ExitStack

import concourse.bass as bass
from concourse import mybir

F32 = mybir.dt.float32
F32R = mybir.dt.float32r
BF16 = mybir.dt.bfloat16
ALU = mybir.AluOpType
ACT = mybir.ActivationFunctionType
AX = mybir.AxisListType

P = 128
B, S, D, F = 4, 1024, 256, 1024
HEADS, HD, MEM = 16, 16, 4
TOK = B * S
TILES = TOK // P
CT = 4
CW = CT * P
CHUNKS = TILES // CT
DK = D // P
FK = F // P
LN_EPS, MEM_EPS = 1e-5, 1e-6
SCALE = float(HD) ** -0.5
GROUPS, GH = 4, 4
BT = S // P
PARTS = 6 * HD
ROWS = PARTS + 3
VW = 2 * HD
MASKED = -1.0e30
RAW = 7
Q_ROWS = (0, 0, 0, 1, 1, 2)
K_ROWS = (0, 1, 2, 0, 1, 0)


class Tally:

    def __init__(self, sem, credit=0, step=1):
        self.sem, self.credit, self.step = sem, credit, step

    def after(self, i):
        return (i + (self.credit + 1)) * self.step

    def give(self, eng):
        if self.credit:
            eng.sem_inc(self.sem, self.credit * self.step)


def quads():
    out = []
    for qc in range(2):
        for kb in range(CT * (qc + 1)):
            q0 = max(qc * CW, kb * P)
            out.append((qc, kb, (qc + 1) * CW - q0, kb >= qc * CT))
    return out


QUADS = quads()
NQ = len(QUADS)
LAST_QUAD = (CT - 1, NQ - 1)
DIAG = [sum(q[3] for q in QUADS[:i]) for i in range(NQ)]
NDIAG = sum(q[3] for q in QUADS)
UNITS = [(qt, h, k0, min(k0 + CW, (qt + 1) * P))
         for qt in range(BT) for h in range(GH) for k0 in range(0, (qt + 1) * P, CW)]
NU = len(UNITS)
NU0 = CT * GH
MX = CT * GH


def after_groups(b, g, k):
    return (b + 1, g + k - GROUPS) if g + k >= GROUPS else (b, g + k)


def timeline(next1, next2):
    units = [(1, u) for u in range(NU0, NU)] * next1 + [(2, u) for u in range(NU0)] * next2

    def blocks(us):
        return sum((UNITS[u][3] - UNITS[u][2]) // P for _, u in us)

    total = sum(w for _, _, w, _ in QUADS)
    hold = 3 * CT
    out, n, done = [], 0, 0

    def walk1(share, limit):
        nonlocal n
        while n < len(units) and blocks(units[:n]) < share and len(units) - n > limit:
            out.append(("scores1", *units[n]))
            n += 1
            if n == NU - NU0 + 3:
                out.append(("maxrows", 1, 1))

    spread = max(blocks(units) - hold, 0)
    for i, (qc, kb, w, _) in enumerate(QUADS):
        for pair in range(2):
            out.append(("scores2", i, pair))
            done += w / 2
            walk1(spread * done / total, 3)
        if i == 1 and next1:
            out.append(("maxrows", 1, 0))
        if i:
            out.append(("pv", i - 1))
        if i == LAST_QUAD[0] + 2:
            out.append(("outT", 0))
    walk1(1e9, 3)
    out.append(("pv", NQ - 1))
    walk1(1e9, 0)
    if next1 and n < NU - NU0 + 3:
        out.append(("maxrows", 1, 1))
    out.append(("outT", 1))
    return out


def build(nc, x, wg, wu, wd, wq, wk, wv, wo, memT, norms, gate, out):
    ctx = ExitStack()
    with ctx:
        def sem(name):
            return ctx.enter_context(nc.semaphore(name))

        def sb(name, shape, dt=F32, where=ctx):
            return where.enter_context(nc.sbuf_tensor(name, shape, dt))

        def pair(name, shape, where=ctx):
            return sb(name + "_h", shape, F32R, where), sb(name + "_l", shape, F32R, where)

        def first(n):
            return isinstance(n, int) and n == 0

        def is_last(c):
            return isinstance(c, int) and c == CHUNKS - 1

        q_parts = nc.dram_tensor("q_parts", [3, D, TOK], BF16, kind="Internal").ap()
        k_parts = nc.dram_tensor("k_parts", [3, D, TOK], BF16, kind="Internal").ap()
        v_dram = nc.dram_tensor("v_groups", [B, GROUPS, P, BT, GH * VW], F32, kind="Internal").ap()
        o_dram = nc.dram_tensor("o_groups", [B, GROUPS, P, BT, GH * HD], F32, kind="Internal").ap()

        X = sb("X", [P, TILES, D])
        wgs, wus = pair("wg", [P, DK, F]), pair("wu", [P, DK, F])
        wds = pair("wd", [P, FK, D])
        wos = pair("wo", [P, DK, D])
        ident = sb("ident", [P, P])
        mask = sb("mask", [P, S], BF16)
        mean_w = sb("mean_w", [P, P])
        xT = pair("xT", [P, DK, CW])
        xn = sb("xn", [P, CT, D])
        stats = sb("stats", [P, CT, 6])
        mv = sb("mv", [P, CT, 2])
        veps = sb("veps", [P, CT])
        rstd = sb("rstd", [P, CT])
        neg_half = sb("neg_half", [P, CT])
        gate_sb = sb("gate_sb", [P, 1])
        gate_e = sb("gate_e", [P, 1])
        gate_d = sb("gate_d", [P, 1])
        g_mem = sb("g_mem", [P, 1])
        g_loc = sb("g_loc", [P, 1])

        with ExitStack() as att:
            wqs, wks, wvs = (pair(n, [P, DK, D], att) for n in ("wq", "wk", "wv"))
            mwo = pair("mwo", [P, DK, MEM * D], att)
            nrm = pair("nrm", [P, DK, MEM], att)
            nrm_raw = sb("nrm_raw", [P, DK, MEM], F32, att)
            with ExitStack() as r:
                gT = pair("gT", [P, FK, CW], r)
                silu = sb("silu", [P, 2, CW], F32, r)
                gated = sb("gated", [P, 2, CW], F32, r)
                with ExitStack() as r2:
                    wg_raw, wu_raw = sb("wg_raw", [P, DK, F], F32, r2), sb("wu_raw", [P, DK, F], F32, r2)
                    wd_raw = sb("wd_raw", [P, FK, D], F32, r2)
                    wqkvo_raw = sb("wqkvo_raw", [P, 4, DK, D], F32, r2)
                    memT_raw = sb("memT_raw", [P, MEM, DK, D], F32, r2)
                with ExitStack() as r2:
                    oT = pair("oT", [P, DK, CW], r2)
                    o_in = sb("o_in", [P, CT, GROUPS, GH * HD], F32, r2)
            with ExitStack() as r:
                memTs = pair("memTs", [P, MEM, DK, D], r)
                sig = pair("sig", [P, DK, S], r)
                q_min = sb("q_min", [P, 2, CW], F32, r)
                q_exp = sb("q_exp", [P, 2, CW], F32, r)
                sig_f = sb("sig_f", [P, 2, CW], F32, r)
                rest = sb("rest", [P, 2, CW], F32, r)
                part = [sb(f"part_{n}", [P, 2 * DK, CW], BF16, r) for n in "hml"]
                va = sb("va", [P, CT, HEADS, VW], F32, r)
                raw_sb = sb("raw_sb", [P, BT, MEM], F32, r)
                rawc = sb("rawc", [P, BT, MEM], F32, r)
                rinv = sb("rinv", [P, BT, MEM], F32, r)
                rel = sb("rel", [P, MEM], F32, r)
                rmax = sb("rmax", [P, 1], F32, r)
                rexp = sb("rexp", [P, MEM], F32, r)
                rsum = sb("rsum", [P, 1], F32, r)
                rnorm = sb("rnorm", [P, 1], F32, r)
                wmem = sb("wmem", [P, MEM], F32, r)
                coef = sb("coef", [P, BT, MEM], F32, r)
        with ExitStack() as r:
            Q = sb("Q", [P, GROUPS, GH, S], BF16, r)
            K = sb("K", [P, GROUPS, GH, S], BF16, r)
            Vg = sb("Vg", [P, GROUPS, BT, GH * VW], F32, r)
            PT = sb("PT", [P, 2 * GH, CW], F32, r)
            Osb = sb("Osb", [P, 2, CW], F32, r)
            Lg = sb("Lg", [P, 2, BT, GH * HD], F32, r)
            rmx = sb("rmx", [P, 2, 3 * MX], F32, r)
            mx_rest = sb("mx_rest", [CT * GH, 2, P], F32, r)
            mx_part = [sb(f"mx_{n}", [CT * GH, 2, P], BF16, r) for n in "hml"]
            rden = sb("rden", [P, 2, CT * GH], F32, r)

        big = [ctx.enter_context(nc.psum_tensor(f"big{i}", [P, 2 * CW], F32)) for i in range(2)]
        bank = [ctx.enter_context(nc.psum_tensor(f"bank{i}", [P, CW], F32)) for i in range(4)]

        def half(i):
            return big[i // 2][:, (i % 2) * CW:(i % 2 + 1) * CW]

        x0_in, xr_in = sem("x0_in"), sem("xr_in")
        w_in = {n: sem(f"{n}_in") for n in ("wg", "wu", "wd", "wqkvo", "memT", "small")}
        consts, ident_ok = sem("consts"), sem("ident_ok")
        w_hi, w_lo = sem("w_hi"), sem("w_lo")
        st_done, mv_done, ve_done, rs_done = sem("st_done"), sem("mv_done"), sem("ve_done"), sem("rs_done")
        xn_done, xTr_done, xh_done, xl_done = sem("xn_done"), sem("xTr_done"), sem("xh_done"), sem("xl_done")

        class Ffn:
            def __init__(self, tag):
                self.second = tag == "2"
                self.g_ready, self.u_ready = Tally(sem("g_ready" + tag)), Tally(sem("u_ready" + tag))
                self.silu_done = Tally(sem("silu_done" + tag), 2)
                self.mul_done = Tally(sem("mul_done" + tag), 2)
                self.hi_done = Tally(sem("hi_done" + tag))
                self.lo_done = Tally(sem("lo_done" + tag), 2)
                self.d_ready = Tally(sem("d_ready" + tag), 1)
                self.x_done = Tally(sem("x_done" + tag), 2)
                if self.second:
                    self.o_in = Tally(sem("o_in_done"), 0, 16)
                    self.oTr = Tally(sem("oTr"))
                    self.oh, self.ol = Tally(sem("oh")), Tally(sem("ol"))
                    self.stored = sem("out_stored")

            def down_at(self, c):
                if not self.second:
                    return c * CT
                return c * (2 * CT) + (CT if is_last(c) else 2 * CT)

            def proj_at(self, c):
                return 0 if first(c) else c * (2 * CT) - CT

        ffn1, ffn2 = Ffn("1"), Ffn("2")
        sp_hi, sp_lo, mwo_ready = sem("sp_hi"), sem("sp_lo"), Tally(sem("mwo_ready"))
        mwo_hi, mwo_lo = sem("mwo_hi"), Tally(sem("mwo_lo"), 2)
        gate_step = sem("gate_step")
        va_ones = sem("va_ones")
        qk_ready = Tally(sem("qk_ready"))
        ph_done, rest_done = Tally(sem("ph_done")), Tally(sem("rest_done"), 2)
        pm_done, pl_done = Tally(sem("pm_done")), Tally(sem("pl_done"), 2)
        part_out = [Tally(sem(f"part_out{o}"), 1, 48) for o in range(2 * DK)]
        min_done, qe_done = Tally(sem("min_done")), Tally(sem("qe_done"), 2)
        sf_done, sh_done, sl_done = Tally(sem("sf_done"), 2), Tally(sem("sh_done")), Tally(sem("sl_done"), 2)
        v_ready, v_free = Tally(sem("v_ready")), Tally(sem("v_free"), 2)
        va_out = [Tally(sem(f"va_out{t}"), 1, 16) for t in range(CT)]
        raw_ready, raw_step = Tally(sem("raw_ready"), 1), sem("raw_step")
        rel_ready, rexp_done, rmax_done = Tally(sem("rel_ready")), Tally(sem("rexp_done")), Tally(sem("rmax_done"))
        am_ready, am_done = Tally(sem("am_ready"), 1), Tally(sem("am_done"), 2)
        am_step = sem("am_step")
        stack_in = [Tally(sem(f"stack_in{g}"), 0, 16 * 13) for g in range(GROUPS)]
        k_ones = sem("k_ones")
        s_ready, mx_done = Tally(sem("s_ready")), Tally(sem("mx_done"), 2)
        mx_both = Tally(sem("mx_both"))
        st_ready, p_done = Tally(sem("st_ready")), Tally(sem("p_done"), 2)
        masked, pv_done = Tally(sem("masked")), Tally(sem("pv_done"), 2)
        mT_ready = Tally(sem("mT_ready"), 1)
        mh_done, mr_done = Tally(sem("mh_done")), Tally(sem("mr_done"))
        mm_done, ml_done = Tally(sem("mm_done")), Tally(sem("ml_done"))
        mrow_in = [Tally(sem(f"mrow_in{i}"), 1, 16 * 3 * GH) for i in range(2)]
        o_out, oT_ready = Tally(sem("o_out"), 1), Tally(sem("oT_ready"), 2)
        rden_done, L_done = Tally(sem("rden_done")), Tally(sem("L_done"), 1)
        L_out = [Tally(sem(f"L_out{r}"), 1, 16) for r in range(2)]

        def apart(eng):
            eng.nop(nofuse=True)

        def dve_stats(dve, n, chunk):
            if not first(n):
                dve.wait_ge(mv_done, n * CT)
                dve.wait_ge(ve_done, n)
                apart(dve)
            for t in range(CT):
                dve.bn_stats(stats[:, t, :], X[:, chunk * CT + t, :]).then_inc(st_done, 1)
            for t in range(CT):
                dve.wait_ge(st_done, n * CT + (t + 1))
                apart(dve)
                dve.bn_aggr(mv[:, t, :], stats[:, t, :]).then_inc(mv_done, 1)

        def pool_rstd(pool, n):
            pool.wait_ge(mv_done, n * CT + CT)
            if not first(n):
                pool.wait_ge(rs_done, n)
            apart(pool)
            pool.tensor_scalar(veps[:, :], mv[:, :, 1], LN_EPS, None, ALU.add).then_inc(ve_done, 1)
            pool.wait_ge(ve_done, n + 1)
            if not first(n):
                pool.wait_ge(xn_done, n * CT)
            pool.tensor_tensor(rstd[:, :], veps[:, :], neg_half[:, :], ALU.pow).then_inc(rs_done, 1)

        def dve_norm(dve, n, chunk):
            dve.wait_ge(rs_done, n + 1)
            if not first(n):
                dve.wait_ge(xTr_done, n * DK)
            for t in range(CT):
                dve.tensor_scalar(xn[:, t, :], X[:, chunk * CT + t, :], mv[:, t, 0:1], rstd[:, t:t + 1],
                                  ALU.subtract, ALU.mult).then_inc(xn_done, 1)

        def pe_xT(pe, n):
            pe.wait_ge(xn_done, n * CT + CT)
            if not first(n):
                pe.wait_ge(xl_done, n * DK)
            for k in range(DK):
                for t in range(CT):
                    last = pe.transpose(bank[k][:, t * P:(t + 1) * P], xn[:, t, k * P:(k + 1) * P], ident[:, :])
                last.then_inc(xTr_done, 1)

        def act_xT(act, n):
            for k in range(DK):
                act.wait_ge(xTr_done, n * DK + (k + 1))
                act.activation(xT[0][:, k, :], bank[k][:, :], ACT.Copy).then_inc(xh_done, 1)

        def dve_xT(dve, n):
            for k in range(DK):
                dve.wait_ge(xh_done, n * DK + (k + 1))
                dve.tensor_tensor(xT[1][:, k, :], bank[k][:, :], xT[0][:, k, :].bitcast(F32),
                                  ALU.subtract).then_inc(xl_done, 1)

        def products(pe, dst, w, x_, wi, xi, nk):
            n = 0
            for k in range(nk):
                for a, b in ((0, 0), (0, 1), (1, 0)):
                    last = pe.matmul(dst, wi(w[a], k), xi(x_[b], k), start=n == 0, stop=n == 3 * nk - 1)
                    n += 1
            return last

        def pe_ffn_up(pe, f, c, more):
            for j in range(FK):
                i = c * FK + j
                for w, dst, ready, free in ((wgs, half(j % 2), f.g_ready, f.silu_done),
                                            (wus, half(2 + j % 2), f.u_ready, f.mul_done)):
                    pe.wait_ge(free.sem, free.after(i - 2))
                    products(pe, dst, w, xT, lambda a, k: a[:, k, j * P:(j + 1) * P],
                             lambda a, k: a[:, k, :], DK).then_inc(ready.sem, 1)
                if f.second and more and j == 3:
                    pe_proj_T(pe, f, c + 1)

        def pe_ffn_down(pe, f, c, t):
            i = f.down_at(c) + t
            dst = bank[2 + t % 2][:, 0:D]
            pe.wait_ge(f.x_done.sem, f.x_done.after(i - 2))
            for j in range(FK):
                if t == 0:
                    pe.wait_ge(f.lo_done.sem, f.lo_done.after(c * FK + j))
                for n, (a, b) in enumerate(((0, 0), (0, 1), (1, 0))):
                    last = pe.matmul(dst, gT[a][:, j, t * P:(t + 1) * P], wds[b][:, j, :],
                                     start=j == 0 and n == 0, stop=j == FK - 1 and n == 2)
            last.then_inc(f.d_ready.sem, 1)

        def pe_proj_T(pe, f, c):
            pe.wait_ge(f.o_in.sem, f.o_in.after(c * GROUPS + (GROUPS - 1)))
            pe.wait_ge(xl_done, (c + 2 * CHUNKS) * DK)
            for k in range(DK):
                for t in range(CT):
                    last = pe.transpose(bank[k][:, t * P:(t + 1) * P],
                                        o_in[:, t, 2 * k:2 * k + 2, :].rearrange("p g e -> p (g e)"), ident[:, :])
                last.then_inc(f.oTr.sem, 1)

        def pe_proj(pe, f, c):
            for t in range(CT):
                dst = bank[2 + t % 2][:, 0:D]
                pe.wait_ge(f.x_done.sem, f.x_done.after(f.proj_at(c) + t - 2))
                pe.wait_ge(f.ol.sem, f.ol.after(c * DK + (DK - 1)))
                products(pe, dst, oT, wos, lambda a, k: a[:, k, t * P:(t + 1) * P],
                         lambda a, k: a[:, k, :], DK).then_inc(f.d_ready.sem, 1)

        def pe_ffn(pe, f, c, n_next):
            pe_ffn_up(pe, f, c, n_next is not None)
            if f.second and n_next is not None:
                pe_proj(pe, f, c + 1)
            for t in range(CT):
                if n_next is not None and t == (CT - 1 if f.second else 0):
                    pe_xT(pe, n_next)
                pe_ffn_down(pe, f, c, t)

        def act_ffn(act, f, c, n_next):
            def hi(j):
                i = c * FK + j
                act.wait_ge(f.mul_done.sem, f.mul_done.after(i))
                if j == 0:
                    act.wait_ge(f.d_ready.sem, f.d_ready.after(c * 2 * CT + (CT - 1) if f.second else c * CT - 1))
                act.activation(gT[0][:, j, :], gated[:, j % 2, :], ACT.Copy).then_inc(f.hi_done.sem, 1)

            for j in range(FK):
                i = c * FK + j
                act.wait_ge(f.g_ready.sem, f.g_ready.after(i))
                act.wait_ge(f.mul_done.sem, f.mul_done.after(i - 2))
                act.activation(silu[:, j % 2, :], half(j % 2), ACT.Silu).then_inc(f.silu_done.sem, 1)
                if j:
                    hi(j - 1)
                if f.second and n_next is not None and j == 4:
                    act_proj(act, f, c + 1)
            hi(FK - 1)
            if n_next is not None:
                act_xT(act, n_next)

        def act_proj(act, f, c):
            for k in range(DK):
                act.wait_ge(f.oTr.sem, f.oTr.after(c * DK + k))
                act.activation(oT[0][:, k, :], bank[k][:, :], ACT.Copy).then_inc(f.oh.sem, 1)

        def dve_proj_lo(dve, f, c):
            for k in range(DK):
                dve.wait_ge(f.oh.sem, f.oh.after(c * DK + k))
                dve.tensor_tensor(oT[1][:, k, :], bank[k][:, :], oT[0][:, k, :].bitcast(F32),
                                  ALU.subtract).then_inc(f.ol.sem, 1)

        def dve_residual(dve, f, chunk, i0, scale):
            for t in range(CT):
                dve.wait_ge(f.d_ready.sem, f.d_ready.after(i0 + t))
                dve.scalar_tensor_tensor(X[:, chunk * CT + t, :], bank[2 + t % 2][:, 0:D], scale,
                                         X[:, chunk * CT + t, :], ALU.mult, ALU.add).then_inc(f.x_done.sem, 1)

        def dve_ffn(dve, f, c, n_next, next_chunk):
            for j in range(FK):
                i = c * FK + j
                dve.wait_ge(f.silu_done.sem, f.silu_done.after(i))
                dve.wait_ge(f.u_ready.sem, f.u_ready.after(i))
                dve.wait_ge(f.lo_done.sem, f.lo_done.after(i - 2))
                dve.tensor_tensor(gated[:, j % 2, :], silu[:, j % 2, :], half(2 + j % 2),
                                  ALU.mult).then_inc(f.mul_done.sem, 1)
                if n_next is not None and not f.second:
                    if j == 2:
                        if f is ffn1:
                            dve.wait_ge(xr_in, 16 * (CHUNKS - 1))
                            if isinstance(c, int) and next_chunk == 0:
                                dve.wait_ge(f.x_done.sem, f.x_done.after(CT - 1))
                        dve_stats(dve, n_next, next_chunk)
                    if j == 5:
                        dve_norm(dve, n_next, next_chunk)
                if n_next is not None and f.second and j == 4:
                    dve_proj_lo(dve, f, c + 1)
            if n_next is not None and f.second:
                dve_residual(dve, f, next_chunk, f.proj_at(c + 1), 1.0)
                dve.wait_ge(f.x_done.sem, f.x_done.after(f.proj_at(c + 1) + (CT - 1)))
                dve_stats(dve, n_next, next_chunk)
                dve_down(dve, f, c, (0, 1))
                dve_norm(dve, n_next, next_chunk)
                dve_down(dve, f, c, (2,))
                dve_xT(dve, n_next)
                dve_down(dve, f, c, (3,))
            elif n_next is not None:
                dve_xT(dve, n_next)
                dve_down(dve, f, c, range(CT))
            else:
                dve_down(dve, f, c, range(CT))

        def dve_down(dve, f, c, ts):
            for t in ts:
                i = f.down_at(c) + t
                dve.wait_ge(f.d_ready.sem, f.d_ready.after(i))
                dve.scalar_tensor_tensor(X[:, c * CT + t, :], bank[2 + t % 2][:, 0:D], 0.5,
                                         X[:, c * CT + t, :], ALU.mult, ALU.add).then_inc(f.x_done.sem, 1)

        def pool_ffn(pool, f, c, n_next):
            for j in range(FK):
                i = c * FK + j
                pool.wait_ge(f.hi_done.sem, f.hi_done.after(i))
                pool.tensor_tensor(gT[1][:, j, :], gated[:, j % 2, :], gT[0][:, j, :].bitcast(F32),
                                   ALU.subtract).then_inc(f.lo_done.sem, 1)
                if j == 3 and n_next is not None and not f.second:
                    pool_rstd(pool, n_next)
            if n_next is not None and f.second:
                pool_rstd(pool, n_next)

        def core_steps(last, g):
            return timeline(not (last and g + 1 >= GROUPS), not (last and g + 2 >= GROUPS))

        block = ctx.enter_context(nc.Block())

        @block.sync
        def _(sp):
            x_v = x.rearrange("(n p) d -> p n d", p=P)
            out_v = out.rearrange("(n p) d -> p n d", p=P)
            sp.dma_start(X[:, 0:CT, :], x_v[:, 0:CT, :]).then_inc(x0_in, 16)
            sp.dma_start(wg_raw[:, :, :], wg).then_inc(w_in["wg"], 16)
            sp.dma_start(wd_raw[:, :, :], wd).then_inc(w_in["wd"], 16)
            for c in range(1, CHUNKS):
                sp.dma_start(X[:, c * CT:(c + 1) * CT, :], x_v[:, c * CT:(c + 1) * CT, :]).then_inc(xr_in, 16)
            sp.dma_start(nrm_raw[:, :, :], norms).then_inc(w_in["small"], 16)
            sp.dma_start(gate_sb[:, :], gate.partition_broadcast(P)).then_inc(w_in["small"], 16)
            for i, w in enumerate((wq, wk, wv, wo)):
                sp.dma_start(wqkvo_raw[:, i, :, :], w).then_inc(w_in["wqkvo"], 16)
            sp.dma_start(memT_raw[:, :, :, :], memT).then_inc(w_in["memT"], 16)

            for t in part_out + va_out:
                t.give(sp)

            def project_chunk(b, cc):
                k = b * 2 + cc
                for o in range(2 * DK):
                    dst = q_parts if o < DK else k_parts
                    for s, done in enumerate((ph_done, pm_done, pl_done)):
                        sp.wait_ge(done.sem, done.after(k * 4 + o))
                        sp.dma_start(dst[s, (o % DK) * P:(o % DK + 1) * P, bass.ds(b * S + cc * CW, CW)],
                                     part[s][:, o, :]).then_inc(part_out[o].sem, 16)
                for t in range(CT):
                    sp.wait_ge(v_free.sem, v_free.after(k * CT + t))
                    sp.dma_start(v_dram[b, :, :, cc * CT + t, :].rearrange("g p e -> p g e"),
                                 va[:, t, :, :].rearrange("p (g h) e -> p g (h e)", g=GROUPS)
                                 ).then_inc(va_out[t].sem, 16)

            with sp.Fori(0, B) as b:
                for cc in range(2):
                    project_chunk(b, cc)
            for t in part_out + va_out:
                sp.wait_ge(t.sem, t.after(2 * B - 1))
            sp.wait_ge(am_done.sem, am_done.after(B * BT - 1))

            mrow_in[0].give(sp)
            mrow_in[1].give(sp)
            for t in L_out:
                t.give(sp)

            def load(b, g):
                done = stack_in[g].sem
                for rows, src, dst in ((Q_ROWS, q_parts, Q), (K_ROWS, k_parts, K)):
                    for i, s in enumerate(rows):
                        v = src[s, g * GH * HD:(g + 1) * GH * HD, bass.ds(b * S, S)]
                        sp.dma_start(dst[i * HD:(i + 1) * HD, g, :, :],
                                     v.rearrange("(h d) t -> d h t", h=GH)).then_inc(done, 16)
                sp.dma_start(Vg[:, g, :, :], v_dram[b, g, :, :, :]).then_inc(done, 16)

            def max_rows(b, g, i):
                G = b * GROUPS + g
                for s, done in enumerate((mh_done, mm_done, ml_done)):
                    sp.wait_ge(done.sem, done.after(2 * G + i))
                    for h in range(GH):
                        dst = Q[PARTS + s:PARTS + s + 1, g, h, i * CW:(i + 1) * CW]
                        sp.dma_start(dst.rearrange("o (t q) -> o t q", q=P),
                                     mx_part[s][h * CT:(h + 1) * CT, i, :]).then_inc(mrow_in[i].sem, 16)

            def core_turn(b, last=False):
                for g in range(GROUPS):
                    G = b * GROUPS + g
                    if not (last and g > 0):
                        if not first(G):
                            sp.wait_ge(pv_done.sem, pv_done.after(G * NQ - 1))
                        load(*after_groups(b, g, 3))
                    if not (last and g == GROUPS - 1):
                        max_rows(*after_groups(b, g, 1), 0)
                        max_rows(*after_groups(b, g, 1), 1)
                    sp.wait_ge(L_done.sem, L_done.after(2 * G + 1))
                    sp.dma_start(o_dram[b, g, :, :, :], Lg[:, g % 2, :, :]).then_inc(L_out[g % 2].sem, 16)

            for g in range(3):
                load(0, g)
            max_rows(0, 0, 0)
            max_rows(0, 0, 1)
            with sp.Fori(0, B - 1) as b:
                core_turn(b)
            core_turn(B - 1, True)
            for t in L_out:
                sp.wait_ge(t.sem, t.after(2 * B - 1))

            def load_o(b, cc):
                for g in range(GROUPS):
                    sp.dma_start(o_in[:, :, g, :], o_dram[b, g, :, cc * CT:(cc + 1) * CT, :]).then_inc(ffn2.o_in.sem, 16)

            load_o(0, 0)
            sp.wait_ge(ffn2.oTr.sem, ffn2.oTr.after(DK - 1))
            load_o(0, 1)

            def ffn2_pair(b, last=False):
                for cc in range(2):
                    c = b * 2 + cc
                    if not last:
                        sp.wait_ge(ffn2.oTr.sem, ffn2.oTr.after((c + 1) * DK + (DK - 1)))
                        load_o(b + 1, cc)
                    sp.wait_ge(ffn2.x_done.sem, ffn2.x_done.after(ffn2.down_at(c) + (CT - 1)))
                    sp.dma_start(out_v[:, bass.ds(c * CT, CT), :],
                                 X[:, bass.ds(c * CT, CT), :]).then_inc(ffn2.stored, 16)

            with sp.Fori(0, B - 1) as b:
                ffn2_pair(b)
            ffn2_pair(B - 1, True)
            sp.wait_ge(ffn2.stored, 16 * CHUNKS)

        @block.gpsimd
        def _(pool):
            pool.memset(neg_half[:, :], -0.5).then_inc(consts, 1)
            pool.memset(ident[:, :], 0.0).then_inc(ident_ok, 1)
            pool.memset(mask[:, :], 0.0).then_inc(ident_ok, 1)
            pool.memset(mean_w[:, :], 1.0 / S).then_inc(consts, 1)
            pool.wait_ge(ident_ok, 2)
            pool.affine_select(out=ident[:, :], in_=ident[:, :], compare_op=ALU.not_equal, fill=1.0, base=0,
                               pattern=[[-1, P]], channel_multiplier=1).then_inc(consts, 1)
            tri = mask[:, S - P:S]
            pool.affine_select(out=tri, in_=tri, compare_op=ALU.is_ge, fill=MASKED, base=0,
                               pattern=[[-1, P]], channel_multiplier=1).then_inc(consts, 1)
            pool.wait_ge(consts, 4)
            pool_rstd(pool, 0)
            pool.wait_ge(w_hi, 3)
            for t in (ffn1.lo_done, ffn2.lo_done):
                t.give(pool)
            pool.tensor_tensor(wds[1][:, :, :], wd_raw[:, :, :], wds[0][:, :, :].bitcast(F32),
                               ALU.subtract).then_inc(w_lo, 1)
            with pool.Fori(0, CHUNKS - 1) as c:
                pool_ffn(pool, ffn1, c, c + 1)
            pool_ffn(pool, ffn1, CHUNKS - 1, CHUNKS)

            for i, w in enumerate((wqs, wks, wvs, wos)):
                pool.wait_ge(sp_hi, i + 1)
                pool.tensor_tensor(w[1][:, :, :], wqkvo_raw[:, i, :, :], w[0][:, :, :].bitcast(F32),
                                   ALU.subtract).then_inc(sp_lo, 1)
            pool.wait_ge(sp_hi, 6)
            pool.tensor_tensor(nrm[1][:, :, :], nrm_raw[:, :, :], nrm[0][:, :, :].bitcast(F32),
                               ALU.subtract).then_inc(sp_lo, 1)
            pool.tensor_tensor(memTs[1][:, :, :, :], memT_raw[:, :, :, :], memTs[0][:, :, :, :].bitcast(F32),
                               ALU.subtract).then_inc(sp_lo, 1)
            pool.wait_ge(sp_lo, 6)
            pool.memset(va[:, :, :, HD:VW], 1.0).then_inc(va_ones, 1)
            pl_done.give(pool)
            sl_done.give(pool)

            def project_chunk(b, cc):
                k = b * 2 + cc
                for o in range(2 * DK):
                    i = k * 4 + o
                    pool.wait_ge(rest_done.sem, rest_done.after(i))
                    pool.wait_ge(part_out[o].sem, part_out[o].after(k - 1))
                    apart(pool)
                    pool.tensor_copy(part[1][:, o, :], rest[:, o % 2, :]).then_inc(pm_done.sem, 1)
                    pool.wait_ge(pm_done.sem, pm_done.after(i))
                    pool.tensor_tensor(part[2][:, o, :], rest[:, o % 2, :], part[1][:, o, :],
                                       ALU.subtract).then_inc(pl_done.sem, 1)
                    if o < DK:
                        j = k * DK + o
                        pool.wait_ge(sh_done.sem, sh_done.after(j))
                        pool.tensor_tensor(sig[1][:, o, cc * CW:(cc + 1) * CW], sig_f[:, o, :],
                                           sig[0][:, o, cc * CW:(cc + 1) * CW].bitcast(F32),
                                           ALU.subtract).then_inc(sl_done.sem, 1)

            def pool_project(b, last=False):
                for cc in range(2):
                    if not (last and cc == 1):
                        pool_rstd(pool, b * 2 + (cc + CHUNKS + 1))
                    project_chunk(b, cc)

            with pool.Fori(0, B - 1) as b:
                pool_project(b)
            pool_project(B - 1, True)

            pool.wait_ge(am_done.sem, am_done.after(B * BT - 1))
            for t in part_out + va_out:
                pool.wait_ge(t.sem, t.after(2 * B - 1))
            pool.memset(K[PARTS:ROWS, :, :, :], 1.0).then_inc(k_ones, 1)

            def core_maxrows(b, g, i):
                m = 2 * (b * GROUPS + g) + i
                pool.wait_ge(mr_done.sem, mr_done.after(m))
                pool.wait_ge(mrow_in[i].sem, mrow_in[i].after(b * GROUPS + (g - 1)))
                apart(pool)
                pool.tensor_copy(mx_part[1][:, i, :], mx_rest[:, i, :]).then_inc(mm_done.sem, 1)
                pool.wait_ge(mm_done.sem, mm_done.after(m))
                pool.tensor_tensor(mx_part[2][:, i, :], mx_rest[:, i, :], mx_part[1][:, i, :],
                                   ALU.subtract).then_inc(ml_done.sem, 1)

            def core_turn(b, last=False):
                for g in range(GROUPS):
                    G = b * GROUPS + g
                    for step, *a in core_steps(last, g):
                        if step == "scores2" and a[1]:
                            i = a[0]
                            if QUADS[i][3]:
                                pool.wait_ge(p_done.sem, p_done.after((G * NQ + i) * 2 + 1))
                                diag = PT[:, (i % 2) * GH:(i % 2 + 1) * GH, 0:P]
                                apart(pool)
                                pool.affine_select(out=diag, in_=diag, compare_op=ALU.is_ge, fill=0.0, base=0,
                                                   pattern=[[0, GH], [1, P]],
                                                   channel_multiplier=-1).then_inc(masked.sem, 1)
                        elif step == "maxrows":
                            core_maxrows(*after_groups(b, g, a[0]), a[1])

            core_maxrows(0, 0, 0)
            core_maxrows(0, 0, 1)
            with pool.Fori(0, B - 1) as b:
                core_turn(b)
            core_turn(B - 1, True)

            pool_rstd(pool, 2 * CHUNKS)
            with pool.Fori(0, CHUNKS - 1) as c:
                pool_ffn(pool, ffn2, c, c + (2 * CHUNKS + 1))
            pool_ffn(pool, ffn2, CHUNKS - 1, None)

        @block.scalar
        def _(act):
            act.dma_start(wu_raw[:, :, :], wu).then_inc(w_in["wu"], 16)
            for t in (ffn1.silu_done, ffn2.silu_done):
                t.give(act)
            act.preload_act_table(ACT.Silu)
            for n, dst, src in (("wg", wgs, wg_raw), ("wu", wus, wu_raw), ("wd", wds, wd_raw)):
                act.wait_ge(w_in[n], 16)
                act.activation(dst[0][:, :, :], src[:, :, :], ACT.Copy).then_inc(w_hi, 1)
                if n == "wg":
                    act_xT(act, 0)
            with act.Fori(0, CHUNKS - 1) as c:
                act_ffn(act, ffn1, c, c + 1)
            act_ffn(act, ffn1, CHUNKS - 1, CHUNKS)

            act.preload_act_table(ACT.Exp)
            act.wait_ge(w_in["wqkvo"], 64)
            for i, w in enumerate((wqs, wks, wvs, wos)):
                act.activation(w[0][:, :, :], wqkvo_raw[:, i, :, :], ACT.Copy).then_inc(sp_hi, 1)
            act.wait_ge(w_in["small"], 32)
            act.activation(nrm[0][:, :, :], nrm_raw[:, :, :], ACT.Copy).then_inc(sp_hi, 1)
            act.wait_ge(w_in["memT"], 16)
            act.wait_ge(ffn1.d_ready.sem, ffn1.d_ready.after(CHUNKS * CT - 1))
            act.activation(memTs[0][:, :, :, :], memT_raw[:, :, :, :], ACT.Copy).then_inc(sp_hi, 1)
            act.activation(gate_e[:, :], gate_sb[:, :], ACT.Exp, scale=-1.0).then_inc(gate_step, 1)
            for i in range(DK * MEM):
                act.wait_ge(mwo_ready.sem, mwo_ready.after(i))
                act.activation(mwo[0][:, i // MEM, (i % MEM) * D:(i % MEM + 1) * D], half(i % 2)[:, 0:D],
                               ACT.Copy).then_inc(mwo_hi, 1)
            qe_done.give(act)
            v_free.give(act)
            act.wait_ge(va_ones, 1)

            def project_chunk(b, cc, more):
                k = b * 2 + cc
                for o in range(2 * DK):
                    i = k * 4 + o
                    act.wait_ge(qk_ready.sem, qk_ready.after(i))
                    act.wait_ge(part_out[o].sem, part_out[o].after(k - 1))
                    act.activation(part[0][:, o, :], half(o % 2), ACT.Copy).then_inc(ph_done.sem, 1)
                    if o < DK:
                        j = k * DK + o
                        act.wait_ge(min_done.sem, min_done.after(j))
                        act.wait_ge(sf_done.sem, sf_done.after(j - 2))
                        act.activation(q_exp[:, o, :], q_min[:, o, :], ACT.Exp).then_inc(qe_done.sem, 1)
                        act.wait_ge(sf_done.sem, sf_done.after(j))
                        act.wait_ge(am_ready.sem, am_ready.after(b * BT - 1))
                        act.activation(sig[0][:, o, cc * CW:(cc + 1) * CW], sig_f[:, o, :],
                                       ACT.Copy).then_inc(sh_done.sem, 1)
                for t in range(CT):
                    act.wait_ge(v_ready.sem, v_ready.after(k * CT + t))
                    act.wait_ge(va_out[t].sem, va_out[t].after(k - 1))
                    act.activation(va[:, t, :, 0:HD], half(2 + t % 2)[:, 0:D].rearrange("p (h e) -> p h e", h=HEADS),
                                   ACT.Copy).then_inc(v_free.sem, 1)
                if more:
                    act_xT(act, k + (CHUNKS + 1))

            def act_project(b, last=False):
                for cc in range(2):
                    project_chunk(b, cc, not (last and cc == 1))
                act.wait_ge(rmax_done.sem, rmax_done.after(b))
                act.activation(rexp[:, :], rel[:, :], ACT.Exp, bias=rmax[:, 0:1],
                               accum_out=rsum[:, 0:1]).then_inc(rexp_done.sem, 1)

            with act.Fori(0, B - 1) as b:
                act_project(b)
            act_project(B - 1, True)

            p_done.give(act)
            o_out.give(act)
            act.wait_ge(am_done.sem, am_done.after(B * BT - 1))

            def core_maxrows(b, g, i):
                m = 2 * (b * GROUPS + g) + i
                act.wait_ge(mT_ready.sem, mT_ready.after(m))
                act.wait_ge(mrow_in[i].sem, mrow_in[i].after(b * GROUPS + (g - 1)))
                act.activation(mx_part[0][:, i, :], bank[3][0:CT * GH, 0:P], ACT.Copy, scale=-1.0).then_inc(mh_done.sem, 1)

            def core_turn(b, last=False):
                for g in range(GROUPS):
                    G = b * GROUPS + g
                    for step, *a in core_steps(last, g):
                        if step == "scores2":
                            i, pair = a
                            w, n = QUADS[i][2], (G * NQ + i) * 2 + pair
                            if pair == 0:
                                act.wait_ge(pv_done.sem, pv_done.after(G * NQ + i - 2))
                            act.wait_ge(st_ready.sem, st_ready.after(n))
                            st = big[pair][:, :].rearrange("p (h q) -> p h q", h=2)
                            h0 = (i % 2) * GH + 2 * pair
                            act.activation(PT[:, h0:h0 + 2, 0:w], st[:, :, 0:w], ACT.Exp,
                                           scale=SCALE).then_inc(p_done.sem, 1)
                        elif step == "maxrows":
                            core_maxrows(*after_groups(b, g, a[0]), a[1])
                        elif step == "pv" and a[0] in LAST_QUAD:
                            qc = LAST_QUAD.index(a[0])
                            act.wait_ge(pv_done.sem, pv_done.after(G * NQ + a[0]))
                            act.wait_ge(oT_ready.sem, oT_ready.after(2 * G + qc - 2))
                            act.activation(Osb[:, qc, :], bank[2][:, :], ACT.Copy).then_inc(o_out.sem, 1)

            core_maxrows(0, 0, 0)
            core_maxrows(0, 0, 1)
            with act.Fori(0, B - 1) as b:
                core_turn(b)
            core_turn(B - 1, True)

            act.preload_act_table(ACT.Silu)
            act_proj(act, ffn2, 0)
            act_xT(act, 2 * CHUNKS)
            with act.Fori(0, CHUNKS - 1) as c:
                act_ffn(act, ffn2, c, c + (2 * CHUNKS + 1))
            act_ffn(act, ffn2, CHUNKS - 1, None)

        @block.vector
        def _(dve):
            for f in (ffn1, ffn2):
                f.mul_done.give(dve)
                f.x_done.give(dve)
            dve.wait_ge(x0_in, 16)
            dve_stats(dve, 0, 0)
            dve_norm(dve, 0, 0)
            dve.wait_ge(w_hi, 1)
            dve.tensor_tensor(wgs[1][:, :, :], wg_raw[:, :, :], wgs[0][:, :, :].bitcast(F32),
                              ALU.subtract).then_inc(w_lo, 1)
            dve_xT(dve, 0)
            dve.wait_ge(w_hi, 2)
            dve.tensor_tensor(wus[1][:, :, :], wu_raw[:, :, :], wus[0][:, :, :].bitcast(F32),
                              ALU.subtract).then_inc(w_lo, 1)
            with dve.Fori(0, CHUNKS - 1) as c:
                dve_ffn(dve, ffn1, c, c + 1, c + 1)
            dve_ffn(dve, ffn1, CHUNKS - 1, CHUNKS, 0)

            dve.wait_ge(gate_step, 1)
            dve.tensor_scalar(gate_d[:, :], gate_e[:, :], 1.0, None, ALU.add).then_inc(gate_step, 1)
            dve.wait_ge(gate_step, 2)
            dve.reciprocal(g_mem[:, :], gate_d[:, :]).then_inc(gate_step, 1)
            dve.wait_ge(gate_step, 3)
            dve.tensor_scalar(g_loc[:, :], g_mem[:, :], -1.0, 1.0, ALU.mult, ALU.add).then_inc(gate_step, 1)
            dve.wait_ge(gate_step, 4)
            mwo_lo.give(dve)
            for i in range(DK * MEM):
                dve.wait_ge(mwo_hi, i + 1)
                at = (slice(None), i // MEM, slice((i % MEM) * D, (i % MEM + 1) * D))
                dve.tensor_tensor(mwo[1][at], half(i % 2)[:, 0:D], mwo[0][at].bitcast(F32),
                                  ALU.subtract).then_inc(mwo_lo.sem, 1)
            for t in (rest_done, sf_done, am_done):
                t.give(dve)
            dve.wait_ge(ffn1.x_done.sem, ffn1.x_done.after(CHUNKS * CT - 1))

            def project_chunk(b, cc, more):
                k = b * 2 + cc
                for o in range(2 * DK):
                    i = k * 4 + o
                    src = half(o % 2)
                    dve.wait_ge(ph_done.sem, ph_done.after(i))
                    dve.wait_ge(pl_done.sem, pl_done.after(i - 2))
                    last = dve.tensor_tensor(rest[:, o % 2, :], src, part[0][:, o, :], ALU.subtract)
                    last.then_inc(rest_done.sem, 1)
                    if o < DK:
                        j = k * DK + o
                        dve.wait_ge(qe_done.sem, qe_done.after(j - 2))
                        dve.tensor_scalar(q_min[:, o, :], src, 0.0, None, ALU.min).then_inc(min_done.sem, 1)
                        dve.wait_ge(qe_done.sem, qe_done.after(j))
                        dve.wait_ge(sl_done.sem, sl_done.after(j - 2))
                        dve.scalar_tensor_tensor(sig_f[:, o, :], src, 0.0, q_exp[:, o, :], ALU.max,
                                                 ALU.add).then_inc(sf_done.sem, 1)
                    if more and o == 1:
                        dve_stats(dve, k + (CHUNKS + 1), k + 1)
                if more:
                    dve_norm(dve, k + (CHUNKS + 1), k + 1)
                    dve_xT(dve, k + (CHUNKS + 1))

            def dve_project(b, last=False):
                for cc in range(2):
                    project_chunk(b, cc, not (last and cc == 1))
                dve.wait_ge(raw_ready.sem, raw_ready.after(b * BT + (BT - 1)))
                raw = bank[2][:, 0:BT * MEM].rearrange("p (t m) -> p t m", m=MEM)
                dve.tensor_copy(raw_sb[:, :, :], raw).then_inc(raw_step, 1)
                dve.tensor_scalar(rawc[:, :, :], raw, MEM_EPS, None, ALU.max).then_inc(raw_step, 1)
                dve.wait_ge(raw_step, RAW * b + 2)
                dve.reciprocal(rinv[:, :, :], rawc[:, :, :]).then_inc(raw_step, 1)
                dve.wait_ge(rel_ready.sem, rel_ready.after(b))
                dve.tensor_copy(rel[:, :], bank[3][:, 0:MEM]).then_inc(raw_step, 1)
                dve.wait_ge(raw_step, RAW * b + 4)
                dve.tensor_reduce(rmax[:, :], rel[:, :], AX.X, ALU.max, negate=True).then_inc(rmax_done.sem, 1)
                dve.wait_ge(rexp_done.sem, rexp_done.after(b))
                dve.reciprocal(rnorm[:, :], rsum[:, :]).then_inc(raw_step, 1)
                dve.wait_ge(raw_step, RAW * b + 5)
                dve.tensor_scalar(wmem[:, :], rexp[:, :], rnorm[:, 0:1], g_mem[:, 0:1], ALU.mult,
                                  ALU.mult).then_inc(raw_step, 1)
                dve.wait_ge(raw_step, RAW * b + 6)
                dve.tensor_tensor(coef[:, :, :], rinv[:, :, :], wmem[:, :].unsqueeze(1).broadcast_to([P, BT, MEM]),
                                  ALU.mult).then_inc(raw_step, 1)
                dve.wait_ge(raw_step, RAW * b + 7)
                for t in range(BT):
                    i = b * BT + t
                    dve.wait_ge(am_ready.sem, am_ready.after(i))
                    for m in range(MEM):
                        tile = X[:, b * BT + t, :]
                        last = dve.scalar_tensor_tensor(tile, big[t % 2][:, m * D:(m + 1) * D], coef[:, t, m:m + 1],
                                                        tile, ALU.mult, ALU.add)
                        if m < MEM - 1:
                            last.then_inc(am_step, 1)
                            dve.wait_ge(am_step, i * (MEM - 1) + (m + 1))
                    last.then_inc(am_done.sem, 1)

            with dve.Fori(0, B - 1) as b:
                dve_project(b)
            dve_project(B - 1, True)

            dve.wait_ge(am_done.sem, am_done.after(B * BT - 1))
            mx_done.give(dve)
            L_done.give(dve)

            def row_max(b, g, u):
                G = b * GROUPS + g
                qt, h, k0, k1 = UNITS[u]
                s = bank[u % 2][:, 0:k1 - k0]
                col = (qt // CT + k0 // CW) * MX + h * CT + qt % CT
                dve.wait_ge(s_ready.sem, s_ready.after(G * NU + u))
                if u == 0 and not first(G) and not first(G - 1):
                    dve.wait_ge(mT_ready.sem, mT_ready.after(2 * G - 3))
                apart(dve)
                dve.tensor_tensor_reduce(out=s, in0=s, in1=mask[:, S - qt * P - P + k0:S - qt * P - P + k1], scale=1.0,
                                         scalar=-3.0e38, op0=ALU.add, op1=ALU.max,
                                         accum_out=rmx[:, g % 2, col:col + 1]).then_inc(mx_done.sem, 1)
                if u == NU - 1:
                    dve.wait_ge(mx_done.sem, mx_done.after(G * NU + u))
                    h1 = rmx[:, g % 2, MX:2 * MX]
                    dve.tensor_tensor(h1, h1, rmx[:, g % 2, 2 * MX:3 * MX], ALU.max).then_inc(mx_both.sem, 1)

            def core_maxrows(b, g, i):
                m = 2 * (b * GROUPS + g) + i
                dve.wait_ge(mh_done.sem, mh_done.after(m))
                dve.wait_ge(mrow_in[i].sem, mrow_in[i].after(b * GROUPS + (g - 1)))
                dve.scalar_tensor_tensor(mx_rest[:, i, :], bank[3][0:CT * GH, 0:P], -1.0, mx_part[0][:, i, :],
                                         ALU.mult, ALU.subtract).then_inc(mr_done.sem, 1)

            def heads_out(b, g, qc):
                G = b * GROUPS + g
                i = 2 * G + qc
                o = bank[3][:, :].rearrange("p (x e) -> p x e", e=VW)
                dve.wait_ge(oT_ready.sem, oT_ready.after(i))
                dve.reciprocal(rden[:, qc, :], o[:, :, HD]).then_inc(rden_done.sem, 1)
                dve.wait_ge(rden_done.sem, rden_done.after(i))
                if qc == 0:
                    dve.wait_ge(L_out[g % 2].sem, L_out[g % 2].after(b * 2 + (g // 2 - 1)))
                dve.scalar_tensor_tensor(
                    Lg[:, g % 2, qc * CT:(qc + 1) * CT, :].rearrange("p t (h e) -> p (t h) e", e=HD),
                    o[:, :, 0:HD], g_loc[:, 0:1], rden[:, qc, :].unsqueeze(2).broadcast_to([P, CT * GH, HD]),
                    ALU.mult, ALU.mult).then_inc(L_done.sem, 1)

            def core_turn(b, last=False):
                for g in range(GROUPS):
                    for step, *a in core_steps(last, g):
                        if step == "scores1":
                            row_max(*after_groups(b, g, a[0]), a[1])
                        elif step == "maxrows":
                            core_maxrows(*after_groups(b, g, a[0]), a[1])
                        elif step == "outT":
                            heads_out(b, g, a[0])

            for u in range(NU):
                row_max(0, 0, u)
                if u == NU0 + 2:
                    core_maxrows(0, 0, 0)
            for u in range(NU0):
                row_max(0, 1, u)
                if u == 2:
                    core_maxrows(0, 0, 1)
            with dve.Fori(0, B - 1) as b:
                core_turn(b)
            core_turn(B - 1, True)

            dve_proj_lo(dve, ffn2, 0)
            dve_residual(dve, ffn2, 0, 0, 1.0)
            dve.wait_ge(ffn2.x_done.sem, ffn2.x_done.after(CT - 1))
            dve_stats(dve, 2 * CHUNKS, 0)
            dve_norm(dve, 2 * CHUNKS, 0)
            dve_xT(dve, 2 * CHUNKS)
            with dve.Fori(0, CHUNKS - 1) as c:
                dve_ffn(dve, ffn2, c, c + (2 * CHUNKS + 1), c + 1)
            dve_ffn(dve, ffn2, CHUNKS - 1, None, None)

        @block.tensor
        def _(pe):
            pe.wait_ge(consts, 4)
            for f in (ffn1, ffn2):
                f.d_ready.give(pe)
            pe_xT(pe, 0)
            pe.wait_ge(xl_done, DK)
            pe.wait_ge(w_lo, 2)
            pe.wait_ge(w_lo, 3)
            with pe.Fori(0, CHUNKS - 1) as c:
                pe.wait_ge(xl_done, c * DK + DK)
                pe_ffn(pe, ffn1, c, c + 1)
            pe.wait_ge(xl_done, CHUNKS * DK)
            pe_ffn(pe, ffn1, CHUNKS - 1, CHUNKS)

            pe.wait_ge(sp_lo, 6)
            for i in range(DK * MEM):
                dk, m = i // MEM, i % MEM
                if i >= 2:
                    pe.wait_ge(mwo_lo.sem, mwo_lo.after(i - 2))
                products(pe, half(i % 2)[:, 0:D], memTs, wos, lambda a, k: a[:, m, k, dk * P:(dk + 1) * P],
                         lambda a, k: a[:, k, :], DK).then_inc(mwo_ready.sem, 1)
            pe.wait_ge(mwo_lo.sem, mwo_lo.after(DK * MEM - 1))
            am_ready.give(pe)
            raw_ready.give(pe)

            def project_chunk(b, cc, more):
                k = b * 2 + cc
                pe.wait_ge(xl_done, (k + CHUNKS) * DK + DK)
                for o in range(2 * DK):
                    i = k * 4 + o
                    w = wqs if o < DK else wks
                    if o < DK:
                        pe.wait_ge(rest_done.sem, rest_done.after(i - 2))
                    else:
                        pe.wait_ge(sf_done.sem, sf_done.after(k * DK + o - DK))
                    if cc == 0 and o < 2:
                        pe.wait_ge(am_done.sem, am_done.after(b * BT - 2))
                    products(pe, half(o % 2), w, xT, lambda a, kk: a[:, kk, (o % DK) * P:(o % DK + 1) * P],
                             lambda a, kk: a[:, kk, :], DK).then_inc(qk_ready.sem, 1)
                for t in range(CT):
                    pe.wait_ge(v_free.sem, v_free.after(k * CT + t - 2))
                    if cc == 0 and t < 2:
                        pe.wait_ge(am_done.sem, am_done.after(b * BT - 1))
                    products(pe, half(2 + t % 2)[:, 0:D], xT, wvs, lambda a, kk: a[:, kk, t * P:(t + 1) * P],
                             lambda a, kk: a[:, kk, :], DK).then_inc(v_ready.sem, 1)
                if more:
                    pe_xT(pe, k + (CHUNKS + 1))

            def pe_project(b, last=False):
                for cc in range(2):
                    project_chunk(b, cc, not (last and cc == 1))
                pe.wait_ge(sl_done.sem, sl_done.after(b * 4 + 3))
                for t in range(BT):
                    products(pe, bank[2][:, t * MEM:(t + 1) * MEM], sig, nrm, lambda a, k: a[:, k, t * P:(t + 1) * P],
                             lambda a, k: a[:, k, :], DK).then_inc(raw_ready.sem, 1)
                pe.wait_ge(raw_step, RAW * b + 1)
                for t in range(BT):
                    m = pe.matmul(bank[3][:, 0:MEM], mean_w[:, :], raw_sb[:, t, :], start=t == 0, stop=t == BT - 1)
                m.then_inc(rel_ready.sem, 1)
                pe.wait_ge(rest_done.sem, rest_done.after(b * 8 + 7))
                pe.wait_ge(v_free.sem, v_free.after(b * 8 + 7))
                for t in range(BT):
                    pe.wait_ge(am_done.sem, am_done.after(b * BT + t - 2))
                    for hf in range(2):
                        last = products(pe, big[t % 2][:, hf * CW:(hf + 1) * CW], sig, mwo,
                                        lambda a, k: a[:, k, t * P:(t + 1) * P],
                                        lambda a, k: a[:, k, hf * CW:(hf + 1) * CW], DK)
                    last.then_inc(am_ready.sem, 1)

            with pe.Fori(0, B - 1) as b:
                pe_project(b)
            pe_project(B - 1, True)

            pe.wait_ge(am_done.sem, am_done.after(B * BT - 1))
            pv_done.give(pe)
            mT_ready.give(pe)
            oT_ready.give(pe)

            def scores1(b, g, u):
                qt, h, k0, k1 = UNITS[u]
                pe.wait_ge(mx_done.sem, mx_done.after((b * GROUPS + g) * NU + u - 2))
                if u == 0:
                    pe.wait_ge(stack_in[g].sem, stack_in[g].after(b))
                pe.matmul(bank[u % 2][:, 0:k1 - k0], Q[0:PARTS, g, h, qt * P:(qt + 1) * P],
                          K[0:PARTS, g, h, k0:k1], start=True, stop=True).then_inc(s_ready.sem, 1)

            def scores2(b, g, i, pair):
                qc, kb, w, _ = QUADS[i]
                G = b * GROUPS + g
                n = (G * NQ + i) * 2 + pair
                if i in (0, CT) and pair == 0:
                    pe.wait_ge(mrow_in[qc].sem, mrow_in[qc].after(G))
                pe.wait_ge(p_done.sem, p_done.after(n - 2))
                q1 = (qc + 1) * CW
                for j in range(2):
                    h = 2 * pair + j
                    last = pe.matmul(big[pair][:, j * CW:j * CW + w], K[0:ROWS, g, h, kb * P:(kb + 1) * P],
                                     Q[0:ROWS, g, h, q1 - w:q1], start=True, stop=True)
                last.then_inc(st_ready.sem, 1)

            def pv(b, g, i):
                qc, kb, w, diag = QUADS[i]
                G = b * GROUPS + g
                if kb == 0:
                    pe.wait_ge(o_out.sem, o_out.after(2 * G + qc - 1))
                if diag:
                    pe.wait_ge(masked.sem, masked.after(G * NDIAG + DIAG[i]))
                else:
                    pe.wait_ge(p_done.sem, p_done.after((G * NQ + i) * 2 + 1))
                for h in range(GH):
                    last = pe.matmul(bank[2][h * VW:(h + 1) * VW, CW - w:CW], Vg[:, g, kb, h * VW:(h + 1) * VW],
                                     PT[:, (i % 2) * GH + h, 0:w], start=kb == 0, stop=i in LAST_QUAD)
                last.then_inc(pv_done.sem, 1)

            def core_maxrows(b, g, i):
                m = 2 * (b * GROUPS + g) + i
                if not first(m):
                    pe.wait_ge(mr_done.sem, mr_done.after(m - 1))
                if not (isinstance(m, int) and m < 2):
                    pe.wait_ge(L_done.sem, L_done.after(m - 3))
                if i:
                    pe.wait_ge(mx_both.sem, mx_both.after(b * GROUPS + g))
                else:
                    pe.wait_ge(mx_done.sem, mx_done.after((b * GROUPS + g) * NU + NU0 - 1))
                pe.transpose(bank[3][0:MX, 0:P], rmx[:, g % 2, i * MX:(i + 1) * MX], ident[:, :]).then_inc(mT_ready.sem, 1)

            def core_outT(b, g, qc, m):
                i = 2 * (b * GROUPS + g) + qc
                pe.wait_ge(mr_done.sem, mr_done.after(m))
                pe.wait_ge(L_done.sem, L_done.after(i - 1))
                pe.wait_ge(o_out.sem, o_out.after(i))
                for t in range(CT):
                    last = pe.transpose(bank[3][:, t * P:(t + 1) * P], Osb[:, qc, t * P:(t + 1) * P], ident[:, :])
                last.then_inc(oT_ready.sem, 1)

            def core_turn(b, last=False):
                for g in range(GROUPS):
                    m = 2 * (b * GROUPS + g) + 1
                    for step, *a in core_steps(last, g):
                        if step == "scores1":
                            scores1(*after_groups(b, g, a[0]), a[1])
                        elif step == "scores2":
                            scores2(b, g, *a)
                        elif step == "pv":
                            pv(b, g, a[0])
                        elif step == "maxrows":
                            m = m + 1
                            core_maxrows(*after_groups(b, g, a[0]), a[1])
                        elif step == "outT":
                            core_outT(b, g, a[0], m)

            pe.wait_ge(k_ones, 1)
            for u in range(NU):
                scores1(0, 0, u)
                if u == NU0 + 2:
                    core_maxrows(0, 0, 0)
            for u in range(NU0):
                scores1(0, 1, u)
                if u == 2:
                    core_maxrows(0, 0, 1)
            with pe.Fori(0, B - 1) as b:
                core_turn(b)
            core_turn(B - 1, True)

            pe.wait_ge(L_done.sem, L_done.after(2 * B * GROUPS - 1))
            pe_proj_T(pe, ffn2, 0)
            pe_proj(pe, ffn2, 0)
            pe_xT(pe, 2 * CHUNKS)
            with pe.Fori(0, CHUNKS - 1) as c:
                pe.wait_ge(xl_done, c * DK + (2 * CHUNKS + 1) * DK)
                pe_ffn(pe, ffn2, c, c + (2 * CHUNKS + 1))
            pe.wait_ge(xl_done, 3 * CHUNKS * DK)
            pe_ffn(pe, ffn2, CHUNKS - 1, None)


_INS = ("x", "wg", "wu", "wd", "wq", "wk", "wv", "wo", "memT", "norms", "gate")


def kernel(L0_attn_x, L0_attn_w_q, L0_attn_w_k, L0_attn_w_v, L0_attn_w_o, L0_attn_gate, L0_attn_memories,
           L0_attn_memory_norms, L0_ffn_w_gate, L0_ffn_w_up, L0_ffn_w_down):
    import numpy as np
    import concourse.bacc as bacc
    from concourse.bass_utils import run_bass_kernel_spmd

    def by_partition(w):
        k, n = w.shape
        return w.reshape(k // P, P, n).transpose(1, 0, 2)

    mem = np.asarray(L0_attn_memories).transpose(2, 0, 1)
    data = dict(
        x=np.asarray(L0_attn_x).reshape(TOK, D),
        wg=by_partition(np.asarray(L0_ffn_w_gate).T), wu=by_partition(np.asarray(L0_ffn_w_up).T),
        wd=by_partition(np.asarray(L0_ffn_w_down).T),
        wq=by_partition(np.asarray(L0_attn_w_q).T), wk=by_partition(np.asarray(L0_attn_w_k).T),
        wv=by_partition(np.asarray(L0_attn_w_v).T), wo=by_partition(np.asarray(L0_attn_w_o).T),
        memT=mem.reshape(DK, P, MEM, D).transpose(1, 2, 0, 3),
        norms=by_partition(np.asarray(L0_attn_memory_norms).T),
        gate=np.asarray(L0_attn_gate),
    )
    nc = bacc.Bacc("TRN2", target_bir_lowering=False, num_devices=1)
    arrays, args = {}, []
    for name in _INS:
        a = np.ascontiguousarray(data[name])
        arrays["in_" + name] = a
        args.append(nc.dram_tensor("in_" + name, a.shape, mybir.dt.from_np(a.dtype), kind="ExternalInput").ap())
    args.append(nc.dram_tensor("out_0", (TOK, D), F32, kind="ExternalOutput").ap())
    build(nc, *args)
    r = run_bass_kernel_spmd(nc, [arrays], core_ids=[0])
    return r.results[0]["out_0"].reshape(B, S, D)
```

```python
from contextlib import ExitStack

import concourse.bass as bass
from concourse import mybir

F32 = mybir.dt.float32
F32R = mybir.dt.float32r
BF16 = mybir.dt.bfloat16
ALU = mybir.AluOpType
ACT = mybir.ActivationFunctionType
AX = mybir.AxisListType

P = 128
B, S, D, F = 4, 1024, 256, 1024
HEADS, HD, MEM = 16, 16, 4
TOK = B * S
TILES = TOK // P
CT = 4
CW = CT * P
CHUNKS = TILES // CT
DK = D // P
FK = F // P
LN_EPS, MEM_EPS = 1e-5, 1e-6
SCALE = float(HD) ** -0.5
GROUPS, GH = 4, 4
BT = S // P
PARTS = 6 * HD
ROWS = PARTS + 3
VW = 2 * HD
MASKED = -1.0e30
UP = 4
UW = F // UP
RAW = 8
Q_ROWS = (0, 0, 0, 1, 1, 2)
K_ROWS = (0, 1, 2, 0, 1, 0)


class Tally:

    def __init__(self, sem, credit=0, step=1):
        self.sem, self.credit, self.step = sem, credit, step

    def after(self, i):
        return (i + (self.credit + 1)) * self.step

    def give(self, eng):
        if self.credit:
            eng.sem_inc(self.sem, self.credit * self.step)


def quads():
    out = []
    for qc, kbs in enumerate(((0, 1, 2, 3), (4, 0, 5, 1, 6, 2, 7, 3))):
        for kb in kbs:
            q0 = max(qc * CW, kb * P)
            out.append((qc, kb, (qc + 1) * CW - q0, kb >= qc * CT))
    return out


QUADS = quads()
NQ = len(QUADS)
FIRST_QUAD, LAST_QUAD = (0, CT), (CT - 1, NQ - 1)
DIAG = [sum(q[3] for q in QUADS[:i]) for i in range(NQ)]
NDIAG = sum(q[3] for q in QUADS)
UNITS = [(qt, h, k0, min(k0 + CW, (qt + 1) * P))
         for qt in range(BT) for h in range(GH) for k0 in range(0, (qt + 1) * P, CW)]
NU = len(UNITS)
NU0 = CT * GH
MX = CT * GH


def after_groups(b, g, k):
    return (b + 1, g + k - GROUPS) if g + k >= GROUPS else (b, g + k)


PE_COL, DVE_COL, DVE_STEP, ACT_COL, ACT_STEP, POOL_MASK, HOP = 0.42, 1.05, 70, 0.72, 180, 350, 60


def timeline(next1, next2):
    walk1 = [(1, u) for u in range(NU0, NU)] * next1 + [(2, u) for u in range(NU0)] * next2
    walk2 = []
    for i in range(1, NQ + next1):
        walk2 += [("scores2", i, 0), ("scores2", i, 1), ("pv", i - 1)]
        if i == MAX0 and next1:
            walk2.append(("maxrows", 1, 0))
        if i == LAST_QUAD[0] + 2:
            walk2.append(("outT", 0))
    walk2 += [("pv", NQ - 1)] * (not next1) + [("outT", 1)]
    width = sum(w for _, _, w, _ in QUADS)
    out, units, dealt, walked = [], 0, 0, 0
    all1 = sum(UNITS[u][3] - UNITS[u][2] for _, u in walk1)
    t = dve = act = pool = o_free = 0
    ring = [0] * RING
    read, probs = [900, 1800], {0: 2500}

    while walk2 or units < len(walk1):
        ready = ring[-RING]
        if walk2:
            step = walk2[0]
            if step[0] == "scores2":
                ready = read[step[2]]
            elif step[0] == "pv":
                ready = max(probs[step[1]], o_free if step[1] in FIRST_QUAD else 0)
            elif step[0] == "outT":
                ready = max(o_free, ring[-RING])
            elif units < RING:
                ready = 1e9
        early = walk2 and next2 and dealt * width > all1 * (walked + LEAD)
        if units < len(walk1) and not early and (not walk2 or ring[-RING] <= t or ready > ring[-RING]):
            ahead, u = walk1[units]
            w = UNITS[u][3] - UNITS[u][2]
            t = max(t, ring[-RING]) + w * PE_COL
            dve = max(dve, t + HOP) + w * DVE_COL + DVE_STEP
            ring.append(dve + HOP)
            out.append(("scores1", ahead, u))
            units, dealt = units + 1, dealt + w
            if units == min(NU - NU0 + RING, len(walk1)):
                walk2.insert(0, ("maxrows", 1, 1))
            continue
        walk2.pop(0)
        out.append(step)
        t = max(t, ready)
        if step[0] == "scores2":
            _, _, w, diag = QUADS[step[1] % NQ]
            t += 2 * w * PE_COL
            walked += w / 2
            act = max(act, t + HOP) + 2 * w * ACT_COL + ACT_STEP
            read[step[2]] = probs[step[1]] = act + HOP
            if diag:
                pool = max(pool, act + HOP) + POOL_MASK
                probs[step[1]] = pool + HOP
        elif step[0] == "pv":
            t += 4 * QUADS[step[1]][2] * PE_COL + 60
            if step[1] in LAST_QUAD:
                act = max(act, t + HOP) + CW * ACT_COL + ACT_STEP
                o_free = act + HOP
        elif step[0] == "outT":
            t += CW * PE_COL * 2
            dve = max(dve, t + HOP) + 600
            ring.append(dve + HOP)
        else:
            t += P * PE_COL
            dve = max(dve, t + 500) + 200
            ring.append(dve + HOP)
    return out


LEAD = 100
MAX0 = 3
RING = 3
RING_STEPS = ("scores1", "maxrows", "outT")


def numbered(groups, n):
    out = []
    for steps in groups:
        out.append([])
        for step, *a in steps:
            ringed = step in RING_STEPS
            out[-1].append((step, a, n if ringed else None))
            n += ringed
    return out


def turns(last):
    return numbered([timeline(not last or g + 1 < GROUPS, not last or g + 2 < GROUPS) for g in range(GROUPS)], 0)


def count(turn_list):
    return sum(n is not None for steps in turn_list for _, _, n in steps)


PER_BATCH = count(turns(False))
_START = ([("scores1", 0, u) for u in range(NU0 + RING)] + [("maxrows", 0, 0)]
          + [("scores1", 0, u) for u in range(NU0 + RING, NU)] + [("scores1", 1, u) for u in range(RING)]
          + [("maxrows", 0, 1)] + [("scores1", 1, u) for u in range(RING, NU0)])
EARLY = 3
START = numbered([_START], -len(_START))[0]


def ring_bank(n):
    return (n if n >= 0 else n + PER_BATCH) % RING


def ring_before(n):
    return next(k for k in range(n - 1, n - 2 * RING, -1) if ring_bank(k) == ring_bank(n))


def build(nc, x, wg, wu, wd, wq, wk, wv, wo, memT, norms, gate, out):
    ctx = ExitStack()
    with ctx:
        def sem(name):
            return ctx.enter_context(nc.semaphore(name))

        def sb(name, shape, dt=F32, where=ctx):
            return where.enter_context(nc.sbuf_tensor(name, shape, dt))

        def pair(name, shape, where=ctx):
            return sb(name + "_h", shape, F32R, where), sb(name + "_l", shape, F32R, where)

        def first(n):
            return isinstance(n, int) and n == 0

        def is_last(c):
            return isinstance(c, int) and c == CHUNKS - 1

        q_parts = nc.dram_tensor("q_parts", [3, D, TOK], BF16, kind="Internal").ap()
        k_parts = nc.dram_tensor("k_parts", [3, D, TOK], BF16, kind="Internal").ap()
        v_dram = nc.dram_tensor("v_groups", [B, GROUPS, P, BT, GH * VW], F32, kind="Internal").ap()
        o_dram = nc.dram_tensor("o_groups", [B, GROUPS, P, BT, GH * HD], F32, kind="Internal").ap()

        X = sb("X", [P, TILES, D])
        wgs, wus = pair("wg", [P, DK, F]), pair("wu", [P, DK, F])
        wds = pair("wd", [P, FK, D])
        wos = pair("wo", [P, DK, D])
        ident = sb("ident", [P, P])
        mask = sb("mask", [P, S], BF16)
        mean_w = sb("mean_w", [P, P])
        xT = pair("xT", [P, DK, CW])
        xn = sb("xn", [P, CT, D])
        stats = sb("stats", [P, CT, 6])
        mv = sb("mv", [P, CT, 2])
        veps = sb("veps", [P, CT])
        rstd = sb("rstd", [P, CT])
        neg_half = sb("neg_half", [P, CT])
        gate_sb = sb("gate_sb", [P, 1])
        gate_e = sb("gate_e", [P, 1])
        gate_d = sb("gate_d", [P, 1])
        g_mem = sb("g_mem", [P, 1])
        g_loc = sb("g_loc", [P, 1])

        with ExitStack() as att:
            wqs, wks, wvs = (pair(n, [P, DK, D], att) for n in ("wq", "wk", "wv"))
            mwo = pair("mwo", [P, DK, MEM * D], att)
            nrm = pair("nrm", [P, DK, MEM], att)
            nrm_raw = sb("nrm_raw", [P, DK, MEM], F32, att)
            with ExitStack() as r:
                gT = pair("gT", [P, FK, CW], r)
                silu = sb("silu", [P, 2, CW], F32, r)
                gated = sb("gated", [P, 2, CW], F32, r)
                with ExitStack() as r2:
                    wqkvo_raw = sb("wqkvo_raw", [P, 4, DK, D], F32, r2)
                    memT_raw = sb("memT_raw", [P, MEM, DK, D], F32, r2)
                    wd_raw = sb("wd_raw", [P, FK, D], F32, r2)
                    with ExitStack() as r3:
                        wg_raw, wu_raw = sb("wg_raw", [P, DK, F], F32, r3), sb("wu_raw", [P, DK, F], F32, r3)
                    with ExitStack() as r3:
                        memTs = pair("memTs", [P, MEM, DK, D], r3)
                with ExitStack() as r2:
                    oT = pair("oT", [P, DK, CW], r2)
                    o_in = sb("o_in", [P, CT, GROUPS, GH * HD], F32, r2)
            with ExitStack() as r:
                sig = pair("sig", [P, DK, S], r)
                elu = sb("elu", [P, DK, CW], F32, r)
                rest = sb("rest", [P, 2 * DK, CW], F32, r)
                part = [sb(f"part_{n}", [P, 2 * DK, CW], BF16, r) for n in "hml"]
                va = sb("va", [P, CT, HEADS, VW], F32, r)
                rawT_sb = sb("rawT_sb", [MEM, S], F32, r)
                sums = sb("sums", [MEM, 2], F32, r)
                total = sb("total", [MEM, 1], F32, r)
                sums_d = sb("sums_d", [MEM, MEM], F32, r)
                rawc = sb("rawc", [P, BT, MEM], F32, r)
                rinv = sb("rinv", [P, BT, MEM], F32, r)
                rel = sb("rel", [P, MEM], F32, r)
                rmax = sb("rmax", [P, 1], F32, r)
                rexp = sb("rexp", [P, MEM], F32, r)
                rsum = sb("rsum", [P, 1], F32, r)
                rnorm = sb("rnorm", [P, 1], F32, r)
                wmem = sb("wmem", [P, MEM], F32, r)
                coef = sb("coef", [P, BT, MEM], F32, r)
        with ExitStack() as r:
            Q, K, Vg = ([None] * GROUPS for _ in range(3))

            def slot(g):
                Q[g] = sb(f"Q{g}", [P, 2, GH, CW], BF16, r)
                K[g] = sb(f"K{g}", [P, GH, S], BF16, r)
                Vg[g] = sb(f"Vg{g}", [P, BT, GH * VW], F32, r)

            for g in range(1, GROUPS):
                slot(g)
            PT = sb("PT", [P, 2 * GH, CW], F32, r)
            Osb = sb("Osb", [P, 2, CW], F32, r)
            Lg = sb("Lg", [P, 2, BT, GH * HD], F32, r)
            slot(0)
            rmx = sb("rmx", [P, 2, 3 * MX], F32, r)
            mx_rest = sb("mx_rest", [CT * GH, 2, P], F32, r)
            mx_part = [sb(f"mx_{n}", [CT * GH, 2, P], BF16, r) for n in "hml"]
            rden = sb("rden", [P, 2, CT * GH], F32, r)

        big = [ctx.enter_context(nc.psum_tensor(f"big{i}", [P, 2 * CW], F32)) for i in range(2)]
        bank = [ctx.enter_context(nc.psum_tensor(f"bank{i}", [P, CW], F32)) for i in range(4)]

        def half(i):
            return big[i // 2][:, (i % 2) * CW:(i % 2 + 1) * CW]

        x0_in, x1_in, xr_in = sem("x0_in"), sem("x1_in"), sem("xr_in")
        w_in = {n: sem(f"{n}_in") for n in ("wd", "wqkvo", "memT", "small")}
        up_in = {n: [sem(f"{n}{i}_in") for i in range(UP)] for n in ("wg", "wu")}
        consts, ident_ok = sem("consts"), sem("ident_ok")
        up_hi, up_lo = sem("up_hi"), sem("up_lo")
        wd_hi, wd_lo = sem("wd_hi"), sem("wd_lo")
        st_done, mv_done, ve_done, rs_done = sem("st_done"), sem("mv_done"), sem("ve_done"), sem("rs_done")
        xn_done, xTr_done, xh_done, xl_done = sem("xn_done"), sem("xTr_done"), sem("xh_done"), sem("xl_done")

        class Ffn:
            def __init__(self, tag):
                self.second = tag == "2"
                self.g_ready, self.u_ready = Tally(sem("g_ready" + tag)), Tally(sem("u_ready" + tag))
                self.silu_done = Tally(sem("silu_done" + tag), 2)
                self.mul_done = Tally(sem("mul_done" + tag), 2)
                self.hi_done = Tally(sem("hi_done" + tag))
                self.lo_done = Tally(sem("lo_done" + tag), 2)
                self.d_ready = Tally(sem("d_ready" + tag), 1)
                self.x_done = Tally(sem("x_done" + tag), 2)
                if self.second:
                    self.o_in = Tally(sem("o_in_done"), 0, 16)
                    self.oTr = Tally(sem("oTr"))
                    self.oh, self.ol = Tally(sem("oh")), Tally(sem("ol"))
                    self.stored = sem("out_stored")

            def down_at(self, c):
                if not self.second:
                    return c * CT
                return c * (2 * CT) + (CT if is_last(c) else 2 * CT)

            def proj_at(self, c):
                return 0 if first(c) else c * (2 * CT) - CT

        ffn1, ffn2 = Ffn("1"), Ffn("2")
        sp_hi, sp_lo, mwo_ready = sem("sp_hi"), sem("sp_lo"), Tally(sem("mwo_ready"))
        mwo_hi, mwo_lo = sem("mwo_hi"), Tally(sem("mwo_lo"), 2)
        gate_step = sem("gate_step")
        va_ones = sem("va_ones")
        qk_ready = Tally(sem("qk_ready"))
        ph_done, rest_done = Tally(sem("ph_done")), Tally(sem("rest_done"), 4)
        pm_done, pl_done = Tally(sem("pm_done")), Tally(sem("pl_done"), 4)
        part_out = [Tally(sem(f"part_out{o}"), 1, 48) for o in range(2 * DK)]
        min_done, qe_done = Tally(sem("min_done")), Tally(sem("qe_done"))
        sf_done, sh_done, sl_done = Tally(sem("sf_done"), 2), Tally(sem("sh_done")), Tally(sem("sl_done"), 2)
        v_ready, v_free = Tally(sem("v_ready")), Tally(sem("v_free"))
        va_out = [Tally(sem(f"va_out{t}"), 1, 16) for t in range(CT)]
        raw_ready, raw_step = Tally(sem("raw_ready")), sem("raw_step")
        rawT_done, raw_turned = Tally(sem("rawT_done")), Tally(sem("raw_turned"))
        rel_ready, rexp_done, rmax_done = Tally(sem("rel_ready")), Tally(sem("rexp_done")), Tally(sem("rmax_done"))
        am_ready, am_done = Tally(sem("am_ready")), Tally(sem("am_done"), 2)
        am_step = sem("am_step")
        stack_in = [Tally(sem(f"stack_in{g}"), 0, 16 * 19) for g in range(GROUPS)]
        k_ones = sem("k_ones")
        s_ready, ring_free = Tally(sem("s_ready")), Tally(sem("ring_free"))
        mx_both = Tally(sem("mx_both"))
        st_ready, p_done = Tally(sem("st_ready")), Tally(sem("p_done"), 2)
        masked, pv_done = Tally(sem("masked")), Tally(sem("pv_done"), 2)
        mT_ready = Tally(sem("mT_ready"), 1)
        mh_done = Tally(sem("mh_done"))
        mm_done, ml_done = Tally(sem("mm_done")), Tally(sem("ml_done"))
        mrow_in = [Tally(sem(f"mrow_in{i}"), 1, 16 * 3) for i in range(2)]
        o_out, oT_ready = Tally(sem("o_out"), 1), Tally(sem("oT_ready"), 2)
        rden_done = Tally(sem("rden_done"))
        L_out = [Tally(sem(f"L_out{r}"), 1, 16) for r in range(2)]

        def apart(eng):
            eng.nop(nofuse=True)

        def dve_stats(dve, n, chunk):
            if not first(n):
                dve.wait_ge(mv_done, n * CT)
                dve.wait_ge(ve_done, n)
                apart(dve)
            for t in range(CT):
                dve.bn_stats(stats[:, t, :], X[:, chunk * CT + t, :]).then_inc(st_done, 1)
            for t in range(CT):
                dve.wait_ge(st_done, n * CT + (t + 1))
                apart(dve)
                dve.bn_aggr(mv[:, t, :], stats[:, t, :]).then_inc(mv_done, 1)

        def pool_rstd(pool, n):
            pool.wait_ge(mv_done, n * CT + CT)
            if not first(n):
                pool.wait_ge(rs_done, n)
            apart(pool)
            pool.tensor_scalar(veps[:, :], mv[:, :, 1], LN_EPS, None, ALU.add).then_inc(ve_done, 1)
            pool.wait_ge(ve_done, n + 1)
            if not first(n):
                pool.wait_ge(xn_done, n * CT)
            pool.tensor_tensor(rstd[:, :], veps[:, :], neg_half[:, :], ALU.pow).then_inc(rs_done, 1)

        def dve_norm(dve, n, chunk):
            dve.wait_ge(rs_done, n + 1)
            if not first(n):
                dve.wait_ge(xTr_done, n * DK)
            for t in range(CT):
                dve.tensor_scalar(xn[:, t, :], X[:, chunk * CT + t, :], mv[:, t, 0:1], rstd[:, t:t + 1],
                                  ALU.subtract, ALU.mult).then_inc(xn_done, 1)

        def pe_xT(pe, n):
            pe.wait_ge(xn_done, n * CT + CT)
            if not first(n):
                pe.wait_ge(xl_done, n * DK)
            for k in range(DK):
                for t in range(CT):
                    last = pe.transpose(bank[k][:, t * P:(t + 1) * P], xn[:, t, k * P:(k + 1) * P], ident[:, :])
                last.then_inc(xTr_done, 1)

        def act_xT(act, n):
            for k in range(DK):
                act.wait_ge(xTr_done, n * DK + (k + 1))
                act.activation(xT[0][:, k, :], bank[k][:, :], ACT.Copy).then_inc(xh_done, 1)

        def dve_xT(dve, n):
            for k in range(DK):
                dve.wait_ge(xh_done, n * DK + (k + 1))
                dve.tensor_tensor(xT[1][:, k, :], bank[k][:, :], xT[0][:, k, :].bitcast(F32),
                                  ALU.subtract).then_inc(xl_done, 1)

        def products(pe, dst, w, x_, wi, xi, nk):
            n = 0
            for k in range(nk):
                for a, b in ((0, 0), (0, 1), (1, 0)):
                    last = pe.matmul(dst, wi(w[a], k), xi(x_[b], k), start=n == 0, stop=n == 3 * nk - 1)
                    n += 1
            return last

        def pe_ffn_up(pe, f, c, more, before=None):
            for j in range(FK):
                if before is not None:
                    before(j)
                i = c * FK + j
                for w, dst, ready, free in ((wgs, half(j % 2), f.g_ready, f.silu_done),
                                            (wus, half(2 + j % 2), f.u_ready, f.mul_done)):
                    pe.wait_ge(free.sem, free.after(i - 2))
                    products(pe, dst, w, xT, lambda a, k: a[:, k, j * P:(j + 1) * P],
                             lambda a, k: a[:, k, :], DK).then_inc(ready.sem, 1)
                if f.second and more and j == 3:
                    pe_proj_T(pe, f, c + 1)

        def pe_ffn_down(pe, f, c, t):
            i = f.down_at(c) + t
            dst = bank[2 + t % 2][:, 0:D]
            pe.wait_ge(f.x_done.sem, f.x_done.after(i - 2))
            for j in range(FK):
                if t == 0:
                    pe.wait_ge(f.lo_done.sem, f.lo_done.after(c * FK + j))
                for n, (a, b) in enumerate(((0, 0), (0, 1), (1, 0))):
                    last = pe.matmul(dst, gT[a][:, j, t * P:(t + 1) * P], wds[b][:, j, :],
                                     start=j == 0 and n == 0, stop=j == FK - 1 and n == 2)
            last.then_inc(f.d_ready.sem, 1)

        def pe_proj_T(pe, f, c):
            pe.wait_ge(f.o_in.sem, f.o_in.after(c * GROUPS + (GROUPS - 1)))
            pe.wait_ge(xl_done, (c + 2 * CHUNKS) * DK)
            for k in range(DK):
                for t in range(CT):
                    last = pe.transpose(bank[k][:, t * P:(t + 1) * P],
                                        o_in[:, t, 2 * k:2 * k + 2, :].rearrange("p g e -> p (g e)"), ident[:, :])
                last.then_inc(f.oTr.sem, 1)

        def pe_proj(pe, f, c):
            for t in range(CT):
                dst = bank[2 + t % 2][:, 0:D]
                pe.wait_ge(f.x_done.sem, f.x_done.after(f.proj_at(c) + t - 2))
                pe.wait_ge(f.ol.sem, f.ol.after(c * DK + (DK - 1)))
                products(pe, dst, oT, wos, lambda a, k: a[:, k, t * P:(t + 1) * P],
                         lambda a, k: a[:, k, :], DK).then_inc(f.d_ready.sem, 1)

        def pe_ffn(pe, f, c, n_next, between=None, before=None):
            pe_ffn_up(pe, f, c, n_next is not None, before)
            if before is not None:
                before(FK)
            if between is not None:
                between()
            if f.second and n_next is not None:
                pe_proj(pe, f, c + 1)
            for t in range(CT):
                if n_next is not None and t == (CT - 1 if f.second else 0):
                    pe_xT(pe, n_next)
                pe_ffn_down(pe, f, c, t)

        def act_ffn(act, f, c, n_next, between=None):
            def hi(j):
                i = c * FK + j
                act.wait_ge(f.mul_done.sem, f.mul_done.after(i))
                if j == 0:
                    act.wait_ge(f.d_ready.sem, f.d_ready.after(c * 2 * CT + (CT - 1) if f.second else c * CT - 1))
                act.activation(gT[0][:, j, :], gated[:, j % 2, :], ACT.Copy).then_inc(f.hi_done.sem, 1)

            for j in range(FK):
                i = c * FK + j
                act.wait_ge(f.g_ready.sem, f.g_ready.after(i))
                act.wait_ge(f.mul_done.sem, f.mul_done.after(i - 2))
                act.activation(silu[:, j % 2, :], half(j % 2), ACT.Silu).then_inc(f.silu_done.sem, 1)
                if j:
                    hi(j - 1)
                if f.second and n_next is not None and j == 4:
                    act_proj(act, f, c + 1)
                if between is not None:
                    between(j)
            hi(FK - 1)
            if n_next is not None:
                act_xT(act, n_next)

        def act_proj(act, f, c):
            for k in range(DK):
                act.wait_ge(f.oTr.sem, f.oTr.after(c * DK + k))
                act.activation(oT[0][:, k, :], bank[k][:, :], ACT.Copy).then_inc(f.oh.sem, 1)

        def dve_proj_lo(dve, f, c):
            for k in range(DK):
                dve.wait_ge(f.oh.sem, f.oh.after(c * DK + k))
                dve.tensor_tensor(oT[1][:, k, :], bank[k][:, :], oT[0][:, k, :].bitcast(F32),
                                  ALU.subtract).then_inc(f.ol.sem, 1)

        def dve_residual(dve, f, chunk, i0, scale):
            for t in range(CT):
                dve.wait_ge(f.d_ready.sem, f.d_ready.after(i0 + t))
                dve.scalar_tensor_tensor(X[:, chunk * CT + t, :], bank[2 + t % 2][:, 0:D], scale,
                                         X[:, chunk * CT + t, :], ALU.mult, ALU.add).then_inc(f.x_done.sem, 1)

        def dve_ffn(dve, f, c, n_next, next_chunk, between=None):
            for j in range(FK):
                i = c * FK + j
                dve.wait_ge(f.silu_done.sem, f.silu_done.after(i))
                dve.wait_ge(f.u_ready.sem, f.u_ready.after(i))
                dve.wait_ge(f.lo_done.sem, f.lo_done.after(i - 2))
                dve.tensor_tensor(gated[:, j % 2, :], silu[:, j % 2, :], half(2 + j % 2),
                                  ALU.mult).then_inc(f.mul_done.sem, 1)
                if n_next is not None and not f.second:
                    if j == 2:
                        if f is ffn1:
                            dve.wait_ge(*(x1_in, 16) if first(c) else (xr_in, 16 * (CHUNKS - 2)))
                            if isinstance(c, int) and next_chunk == 0:
                                dve.wait_ge(f.x_done.sem, f.x_done.after(CT - 1))
                        dve_stats(dve, n_next, next_chunk)
                    if j == 5:
                        dve_norm(dve, n_next, next_chunk)
                if n_next is not None and f.second and j == 4:
                    dve_proj_lo(dve, f, c + 1)
                if between is not None:
                    between(j)
            if n_next is not None and f.second:
                dve_residual(dve, f, next_chunk, f.proj_at(c + 1), 1.0)
                dve.wait_ge(f.x_done.sem, f.x_done.after(f.proj_at(c + 1) + (CT - 1)))
                dve_stats(dve, n_next, next_chunk)
                dve_down(dve, f, c, (0, 1))
                dve_norm(dve, n_next, next_chunk)
                dve_down(dve, f, c, (2,))
                dve_xT(dve, n_next)
                dve_down(dve, f, c, (3,))
            elif n_next is not None:
                dve_xT(dve, n_next)
                if between is not None:
                    between(FK)
                dve_down(dve, f, c, range(CT))
            else:
                dve_down(dve, f, c, range(CT))

        def dve_down(dve, f, c, ts):
            for t in ts:
                i = f.down_at(c) + t
                dve.wait_ge(f.d_ready.sem, f.d_ready.after(i))
                dve.scalar_tensor_tensor(X[:, c * CT + t, :], bank[2 + t % 2][:, 0:D], 0.5,
                                         X[:, c * CT + t, :], ALU.mult, ALU.add).then_inc(f.x_done.sem, 1)

        def pool_ffn(pool, f, c, n_next):
            for j in range(FK):
                i = c * FK + j
                pool.wait_ge(f.hi_done.sem, f.hi_done.after(i))
                pool.tensor_tensor(gT[1][:, j, :], gated[:, j % 2, :], gT[0][:, j, :].bitcast(F32),
                                   ALU.subtract).then_inc(f.lo_done.sem, 1)
                if j == 3 and n_next is not None and not f.second:
                    pool_rstd(pool, n_next)
            if n_next is not None and f.second:
                pool_rstd(pool, n_next)

        qk_bank = [half(0), half(1), bank[2][:, :], bank[3][:, :]]

        def v_bank(t):
            return bank[t // 2][:, (t % 2) * D:(t % 2 + 1) * D]

        ring_at = [bank[0], bank[1], bank[3]]

        def ring_done(b, n):
            return ring_free.after(b * PER_BATCH + (n + len(START)))

        block = ctx.enter_context(nc.Block())

        @block.sync
        def _(sp):
            x_v = x.rearrange("(n p) d -> p n d", p=P)
            out_v = out.rearrange("(n p) d -> p n d", p=P)
            sp.dma_start(X[:, 0:CT, :], x_v[:, 0:CT, :]).then_inc(x0_in, 16)
            for i in range(UP):
                cols = slice(i * UW, (i + 1) * UW)
                sp.dma_start(wg_raw[:, :, cols], wg[:, :, cols]).then_inc(up_in["wg"][i], 16)
                sp.dma_start(wu_raw[:, :, cols], wu[:, :, cols]).then_inc(up_in["wu"][i], 16)
            sp.dma_start(X[:, CT:2 * CT, :], x_v[:, CT:2 * CT, :]).then_inc(x1_in, 16)
            sp.dma_start(wd_raw[:, :, :], wd).then_inc(w_in["wd"], 16)
            for c in range(2, CHUNKS):
                sp.dma_start(X[:, c * CT:(c + 1) * CT, :], x_v[:, c * CT:(c + 1) * CT, :]).then_inc(xr_in, 16)
            sp.dma_start(nrm_raw[:, :, :], norms).then_inc(w_in["small"], 16)
            sp.dma_start(gate_sb[:, :], gate.partition_broadcast(P)).then_inc(w_in["small"], 16)
            for i, w in enumerate((wq, wk, wv, wo)):
                sp.dma_start(wqkvo_raw[:, i, :, :], w).then_inc(w_in["wqkvo"], 16)
            sp.dma_start(memT_raw[:, :, :, :], memT).then_inc(w_in["memT"], 16)

            for t in part_out + va_out:
                t.give(sp)

            def project_chunk(b, cc):
                k = b * 2 + cc
                for o in range(2 * DK):
                    dst = q_parts if o < DK else k_parts
                    for s, done in enumerate((ph_done, pm_done, pl_done)):
                        sp.wait_ge(done.sem, done.after(k * 4 + o))
                        sp.dma_start(dst[s, (o % DK) * P:(o % DK + 1) * P, bass.ds(b * S + cc * CW, CW)],
                                     part[s][:, o, :]).then_inc(part_out[o].sem, 16)
                for t in range(CT):
                    sp.wait_ge(v_free.sem, v_free.after(k * CT + t))
                    sp.dma_start(v_dram[b, :, :, cc * CT + t, :].rearrange("g p e -> p g e"),
                                 va[:, t, :, :].rearrange("p (g h) e -> p g (h e)", g=GROUPS)
                                 ).then_inc(va_out[t].sem, 16)

            def load(b, g):
                done = stack_in[g].sem

                def rows_of(parts, s, t0, n):
                    v = parts[s, g * GH * HD:(g + 1) * GH * HD, bass.ds(b * S + t0, n)]
                    return v.rearrange("(h d) t -> d h t", h=GH)

                for i in range(6):
                    rows = slice(i * HD, (i + 1) * HD)
                    for qc in range(2):
                        sp.dma_start(Q[g][rows, qc, :, :], rows_of(q_parts, Q_ROWS[i], qc * CW, CW)).then_inc(done, 16)
                    sp.dma_start(K[g][rows, :, :], rows_of(k_parts, K_ROWS[i], 0, S)).then_inc(done, 16)
                sp.dma_start(Vg[g][:, :, :], v_dram[b, g, :, :, :]).then_inc(done, 16)

            with sp.Fori(0, B - 1) as b:
                for cc in range(2):
                    project_chunk(b, cc)
            for t in part_out + va_out:
                sp.wait_ge(t.sem, t.after(2 * (B - 1) - 1))
            load(0, 0)
            for cc in range(2):
                project_chunk(B - 1, cc)
            for t in part_out + va_out:
                sp.wait_ge(t.sem, t.after(2 * B - 1))

            mrow_in[0].give(sp)
            mrow_in[1].give(sp)
            for t in L_out:
                t.give(sp)

            def max_rows(b, g, i):
                G = b * GROUPS + g
                for s, done in enumerate((mh_done, mm_done, ml_done)):
                    sp.wait_ge(done.sem, done.after(2 * G + i))
                    dst = Q[g][PARTS + s:PARTS + s + 1, i, :, :].rearrange("o h (t q) -> o (h t) q", q=P)
                    sp.dma_start(dst, mx_part[s][:, i, :]).then_inc(mrow_in[i].sem, 16)

            def core_turn(b, last=False):
                plan = turns(last)
                for g in range(GROUPS):
                    G = b * GROUPS + g
                    if not (last and g > 0):
                        if not first(G):
                            sp.wait_ge(pv_done.sem, pv_done.after(G * NQ - 1))
                        load(*after_groups(b, g, 3))
                    if not (last and g == GROUPS - 1):
                        max_rows(*after_groups(b, g, 1), 0)
                        max_rows(*after_groups(b, g, 1), 1)
                    outs = [n for step, a, n in plan[g] if step == "outT"]
                    sp.wait_ge(ring_free.sem, ring_done(b, outs[-1]))
                    sp.dma_start(o_dram[b, g, :, :, :], Lg[:, g % 2, :, :]).then_inc(L_out[g % 2].sem, 16)

            sp.wait_ge(am_done.sem, am_done.after(2 * B * BT - 1))
            load(0, 1)
            load(0, 2)
            max_rows(0, 0, 0)
            max_rows(0, 0, 1)
            with sp.Fori(0, B - 1) as b:
                core_turn(b)
            core_turn(B - 1, True)
            for t in L_out:
                sp.wait_ge(t.sem, t.after(2 * B - 1))

            def load_o(b, cc):
                for g in range(GROUPS):
                    sp.dma_start(o_in[:, :, g, :], o_dram[b, g, :, cc * CT:(cc + 1) * CT, :]).then_inc(ffn2.o_in.sem, 16)

            load_o(0, 0)
            sp.wait_ge(ffn2.oTr.sem, ffn2.oTr.after(DK - 1))
            load_o(0, 1)

            def ffn2_pair(b, last=False):
                for cc in range(2):
                    c = b * 2 + cc
                    if not last:
                        sp.wait_ge(ffn2.oTr.sem, ffn2.oTr.after((c + 1) * DK + (DK - 1)))
                        load_o(b + 1, cc)
                    sp.wait_ge(ffn2.x_done.sem, ffn2.x_done.after(ffn2.down_at(c) + (CT - 1)))
                    sp.dma_start(out_v[:, bass.ds(c * CT, CT), :],
                                 X[:, bass.ds(c * CT, CT), :]).then_inc(ffn2.stored, 16)

            with sp.Fori(0, B - 1) as b:
                ffn2_pair(b)
            ffn2_pair(B - 1, True)
            sp.wait_ge(ffn2.stored, 16 * CHUNKS)

        @block.gpsimd
        def _(pool):
            pool.memset(neg_half[:, :], -0.5).then_inc(consts, 1)
            pool.memset(ident[:, :], 0.0).then_inc(ident_ok, 1)
            pool.memset(mask[:, :], 0.0).then_inc(ident_ok, 1)
            pool.memset(mean_w[:, :], 1.0 / S).then_inc(consts, 1)
            pool.wait_ge(ident_ok, 2)
            pool.affine_select(out=ident[:, :], in_=ident[:, :], compare_op=ALU.not_equal, fill=1.0, base=0,
                               pattern=[[-1, P]], channel_multiplier=1).then_inc(consts, 1)
            tri = mask[:, S - P:S]
            pool.affine_select(out=tri, in_=tri, compare_op=ALU.is_ge, fill=MASKED, base=0,
                               pattern=[[-1, P]], channel_multiplier=1).then_inc(consts, 1)
            pool.wait_ge(consts, 4)
            pool_rstd(pool, 0)
            for t in (ffn1.lo_done, ffn2.lo_done):
                t.give(pool)

            pool_ffn(pool, ffn1, 0, 1)
            with pool.Fori(1, CHUNKS - 1) as c:
                pool_ffn(pool, ffn1, c, c + 1)
            pool_ffn(pool, ffn1, CHUNKS - 1, CHUNKS)

            pool.wait_ge(ffn1.d_ready.sem, ffn1.d_ready.after(CHUNKS * CT - 1))
            pool.wait_ge(mwo_ready.sem, mwo_ready.after(DK * MEM - 1))
            pool.memset(va[:, :, :, HD:VW], 1.0).then_inc(va_ones, 1)
            pl_done.give(pool)
            sl_done.give(pool)

            def project_chunk(b, cc):
                k = b * 2 + cc
                if not first(k):
                    pool_rstd(pool, k + CHUNKS)

                def sig_lo(o):
                    pool.wait_ge(sh_done.sem, sh_done.after(k * DK + o))
                    pool.tensor_tensor(sig[1][:, o, cc * CW:(cc + 1) * CW], elu[:, o, :],
                                       sig[0][:, o, cc * CW:(cc + 1) * CW].bitcast(F32),
                                       ALU.subtract).then_inc(sl_done.sem, 1)

                for o in range(DK):
                    sig_lo(o)
                for o in range(2 * DK):
                    pool.wait_ge(pm_done.sem, pm_done.after(k * 4 + o))
                    pool.wait_ge(part_out[o].sem, part_out[o].after(k - 1))
                    apart(pool)
                    pool.tensor_tensor(part[2][:, o, :], rest[:, o, :], part[1][:, o, :],
                                       ALU.subtract).then_inc(pl_done.sem, 1)

            project_chunk(0, 0)
            project_chunk(0, 1)
            with pool.Fori(0, B - 1) as pb:
                project_chunk(pb + 1, 0)
                project_chunk(pb + 1, 1)

            pool.wait_ge(am_done.sem, am_done.after(2 * B * BT - 1))
            for t in part_out + va_out:
                pool.wait_ge(t.sem, t.after(2 * B - 1))
            for g in range(GROUPS):
                pool.memset(K[g][PARTS:ROWS, :, :], 1.0).then_inc(k_ones, 1)

            def core_maxrows(b, g, i, done):
                m = 2 * (b * GROUPS + g) + i
                pool.wait_ge(ring_free.sem, done)
                pool.wait_ge(mrow_in[i].sem, mrow_in[i].after(b * GROUPS + (g - 1)))
                apart(pool)
                pool.tensor_copy(mx_part[1][:, i, :], mx_rest[:, i, :]).then_inc(mm_done.sem, 1)
                pool.wait_ge(mm_done.sem, mm_done.after(m))
                pool.tensor_tensor(mx_part[2][:, i, :], mx_rest[:, i, :], mx_part[1][:, i, :],
                                   ALU.subtract).then_inc(ml_done.sem, 1)

            def causal(G, i, pair):
                if QUADS[i % NQ][3]:
                    pool.wait_ge(p_done.sem, p_done.after((G * NQ + i) * 2 + pair))
                    h0 = (i % 2) * GH + 2 * pair
                    diag = PT[:, h0:h0 + 2, 0:P]
                    apart(pool)
                    pool.affine_select(out=diag, in_=diag, compare_op=ALU.is_ge, fill=0.0, base=0,
                                       pattern=[[0, 2], [1, P]], channel_multiplier=-1).then_inc(masked.sem, 1)

            def core_turn(b, last=False):
                plan = turns(last)
                for g in range(GROUPS):
                    G = b * GROUPS + g
                    for step, a, n in plan[g]:
                        if step == "scores2":
                            causal(G, *a)
                        elif step == "maxrows":
                            core_maxrows(*after_groups(b, g, a[0]), a[1], ring_done(b, n))

            for step, a, n in START:
                if step == "maxrows":
                    core_maxrows(0, *a, ring_done(0, n))
            causal(0, 0, 0)
            causal(0, 0, 1)
            with pool.Fori(0, B - 1) as b:
                core_turn(b)
            core_turn(B - 1, True)

            pool_rstd(pool, 2 * CHUNKS)
            with pool.Fori(0, CHUNKS - 1) as c:
                pool_ffn(pool, ffn2, c, c + (2 * CHUNKS + 1))
            pool_ffn(pool, ffn2, CHUNKS - 1, None)

        @block.scalar
        def _(act):
            for t in (ffn1.silu_done, ffn2.silu_done):
                t.give(act)
            act.preload_act_table(ACT.Silu)

            def up_part(i):
                cols = slice(i * UW, (i + 1) * UW)
                for n, dst, src in (("wg", wgs, wg_raw), ("wu", wus, wu_raw)):
                    act.wait_ge(up_in[n][i], 16)
                    act.activation(dst[0][:, :, cols], src[:, :, cols], ACT.Copy).then_inc(up_hi, 1)

            def ffn_weights(j):
                if j < UP - 1:
                    up_part(j + 1)
                if j == 4:
                    act.wait_ge(w_in["wd"], 16)
                    for i in range(2):
                        rows = slice(i * FK // 2, (i + 1) * FK // 2)
                        act.activation(wds[0][:, rows, :], wd_raw[:, rows, :], ACT.Copy).then_inc(wd_hi, 1)

            up_part(0)
            act_xT(act, 0)
            act_ffn(act, ffn1, 0, 1, ffn_weights)
            with act.Fori(1, CHUNKS - 1) as c:
                act_ffn(act, ffn1, c, c + 1)

            def attention_weights(j):
                if j == 0:
                    act.wait_ge(w_in["wqkvo"], 64)
                if j < 4:
                    act.activation((wqs, wks, wvs, wos)[j][0][:, :, :], wqkvo_raw[:, j, :, :],
                                   ACT.Copy).then_inc(sp_hi, 1)
                if j == 4:
                    act.wait_ge(w_in["small"], 32)
                    act.activation(nrm[0][:, :, :], nrm_raw[:, :, :], ACT.Copy).then_inc(sp_hi, 1)
                    act.wait_ge(w_in["memT"], 16)
                    act.activation(memTs[0][:, :, :, :], memT_raw[:, :, :, :], ACT.Copy).then_inc(sp_hi, 1)

            act_ffn(act, ffn1, CHUNKS - 1, CHUNKS, attention_weights)
            for i in range(DK * MEM):
                act.wait_ge(mwo_ready.sem, mwo_ready.after(i))
                act.activation(mwo[0][:, i // MEM, (i % MEM) * D:(i % MEM + 1) * D], half(i % 2)[:, 0:D],
                               ACT.Copy).then_inc(mwo_hi, 1)
            act.preload_act_table(ACT.Exp)
            act.activation(gate_e[:, :], gate_sb[:, :], ACT.Exp, scale=-1.0).then_inc(gate_step, 1)

            def project_chunk(b, cc):
                k = b * 2 + cc
                if not first(k):
                    act_xT(act, k + CHUNKS)

                def high(o):
                    act.wait_ge(qk_ready.sem, qk_ready.after(k * 4 + o))
                    act.wait_ge(part_out[o].sem, part_out[o].after(k - 1))
                    act.activation(part[0][:, o, :], qk_bank[o], ACT.Copy).then_inc(ph_done.sem, 1)

                def middle(o):
                    act.wait_ge(rest_done.sem, rest_done.after(k * 4 + o))
                    act.activation(part[1][:, o, :], rest[:, o, :], ACT.Copy).then_inc(pm_done.sem, 1)

                def exp(o):
                    act.wait_ge(min_done.sem, min_done.after(k * DK + o))
                    act.activation(elu[:, o, :], elu[:, o, :], ACT.Exp).then_inc(qe_done.sem, 1)

                def sig_hi(o):
                    act.wait_ge(sf_done.sem, sf_done.after(k * DK + o))
                    act.activation(sig[0][:, o, cc * CW:(cc + 1) * CW], elu[:, o, :], ACT.Copy).then_inc(sh_done.sem, 1)

                high(0)
                exp(0)
                high(1)
                exp(1)
                sig_hi(0)
                middle(0)
                high(2)
                sig_hi(1)
                middle(1)
                high(3)
                middle(2)
                middle(3)
                for t in range(CT):
                    act.wait_ge(v_ready.sem, v_ready.after(k * CT + t // 2 * 2 + 1))
                    act.wait_ge(va_out[t].sem, va_out[t].after(k - 1))
                    if first(k) and t == 0:
                        act.wait_ge(va_ones, 1)
                    act.activation(va[:, t, :, 0:HD], v_bank(t).rearrange("p (h e) -> p h e", h=HEADS),
                                   ACT.Copy).then_inc(v_free.sem, 1)

            def act_project(b):
                for cc in range(2):
                    project_chunk(b, cc)
                for cc in range(2):
                    act.wait_ge(raw_ready.sem, raw_ready.after(b * 2 + cc))
                    act.activation(rawT_sb[:, cc * CW:(cc + 1) * CW], half(2 + cc)[0:MEM, :], ACT.Copy,
                                   accum_out=sums[:, cc:cc + 1]).then_inc(rawT_done.sem, 1)
                act.wait_ge(rmax_done.sem, rmax_done.after(b))
                act.activation(rexp[:, :], rel[:, :], ACT.Exp, bias=rmax[:, 0:1],
                               accum_out=rsum[:, 0:1]).then_inc(rexp_done.sem, 1)

            act_project(0)
            with act.Fori(0, B - 1) as pb:
                act_project(pb + 1)

            p_done.give(act)
            o_out.give(act)

            def core_maxrows(b, g, i, n):
                m = 2 * (b * GROUPS + g) + i
                act.wait_ge(mT_ready.sem, mT_ready.after(m))
                act.wait_ge(mrow_in[i].sem, mrow_in[i].after(b * GROUPS + (g - 1)))
                act.activation(mx_part[0][:, i, :], ring_at[ring_bank(n)][0:MX, 0:P], ACT.Copy, scale=-1.0).then_inc(mh_done.sem, 1)

            def exps(G, i, pair):
                w = QUADS[i % NQ][2]
                if pair == 0:
                    act.wait_ge(pv_done.sem, pv_done.after(G * NQ + i - 2))
                act.wait_ge(st_ready.sem, st_ready.after((G * NQ + i) * 2 + pair))
                st = big[pair][:, :].rearrange("p (h q) -> p h q", h=2)
                h0 = (i % 2) * GH + 2 * pair
                act.activation(PT[:, h0:h0 + 2, 0:w], st[:, :, 0:w], ACT.Exp, scale=SCALE).then_inc(p_done.sem, 1)

            def core_turn(b, last=False):
                plan = turns(last)
                for g in range(GROUPS):
                    G = b * GROUPS + g
                    for step, a, n in plan[g]:
                        if step == "scores2":
                            exps(G, *a)
                        elif step == "maxrows":
                            core_maxrows(*after_groups(b, g, a[0]), a[1], n)
                        elif step == "pv" and a[0] in LAST_QUAD:
                            qc = LAST_QUAD.index(a[0])
                            act.wait_ge(pv_done.sem, pv_done.after(G * NQ + a[0]))
                            act.wait_ge(oT_ready.sem, oT_ready.after(2 * G + qc - 2))
                            act.activation(Osb[:, qc, :], bank[2][:, :], ACT.Copy).then_inc(o_out.sem, 1)

            for step, a, n in START:
                if step == "maxrows":
                    core_maxrows(0, *a, n)
            act.wait_ge(am_done.sem, am_done.after(2 * B * BT - 1))
            exps(0, 0, 0)
            exps(0, 0, 1)
            with act.Fori(0, B - 1) as b:
                core_turn(b)
            core_turn(B - 1, True)

            act.preload_act_table(ACT.Silu)
            act_proj(act, ffn2, 0)
            act_xT(act, 2 * CHUNKS)
            with act.Fori(0, CHUNKS - 1) as c:
                act_ffn(act, ffn2, c, c + (2 * CHUNKS + 1))
            act_ffn(act, ffn2, CHUNKS - 1, None)

        @block.vector
        def _(dve):
            for f in (ffn1, ffn2):
                f.mul_done.give(dve)
                f.x_done.give(dve)
            def up_part(i):
                cols = slice(i * UW, (i + 1) * UW)
                for n, (w, raw) in enumerate(((wgs, wg_raw), (wus, wu_raw))):
                    dve.wait_ge(up_hi, 2 * i + n + 1)
                    dve.tensor_tensor(w[1][:, :, cols], raw[:, :, cols], w[0][:, :, cols].bitcast(F32),
                                      ALU.subtract).then_inc(up_lo, 1)

            def ffn_weights(j):
                if j < UP - 1:
                    up_part(j + 1)
                if j == 6:
                    for i in range(2):
                        rows = slice(i * FK // 2, (i + 1) * FK // 2)
                        dve.wait_ge(wd_hi, i + 1)
                        dve.tensor_tensor(wds[1][:, rows, :], wd_raw[:, rows, :], wds[0][:, rows, :].bitcast(F32),
                                          ALU.subtract).then_inc(wd_lo, 1)

            dve.wait_ge(x0_in, 16)
            dve_stats(dve, 0, 0)
            dve_norm(dve, 0, 0)
            up_part(0)
            dve_xT(dve, 0)
            dve_ffn(dve, ffn1, 0, 1, 1, ffn_weights)
            with dve.Fori(1, CHUNKS - 1) as c:
                dve_ffn(dve, ffn1, c, c + 1, c + 1)

            def attention_weights(j):
                if 1 <= j <= 4:
                    w = (wqs, wks, wvs, wos)[j - 1]
                    dve.wait_ge(sp_hi, j)
                    dve.tensor_tensor(w[1][:, :, :], wqkvo_raw[:, j - 1, :, :], w[0][:, :, :].bitcast(F32),
                                      ALU.subtract).then_inc(sp_lo, 1)
                if j == 6:
                    dve.wait_ge(sp_hi, 6)
                    dve.tensor_tensor(nrm[1][:, :, :], nrm_raw[:, :, :], nrm[0][:, :, :].bitcast(F32),
                                      ALU.subtract).then_inc(sp_lo, 1)
                    dve.tensor_tensor(memTs[1][:, :, :, :], memT_raw[:, :, :, :], memTs[0][:, :, :, :].bitcast(F32),
                                      ALU.subtract).then_inc(sp_lo, 1)
                if j == FK:
                    for i in range(DK * MEM):
                        dve.wait_ge(mwo_hi, i + 1)
                        at = (slice(None), i // MEM, slice((i % MEM) * D, (i % MEM + 1) * D))
                        dve.tensor_tensor(mwo[1][at], half(i % 2)[:, 0:D], mwo[0][at].bitcast(F32),
                                          ALU.subtract).then_inc(mwo_lo.sem, 1)

            mwo_lo.give(dve)
            dve_ffn(dve, ffn1, CHUNKS - 1, CHUNKS, 0, attention_weights)

            dve.wait_ge(gate_step, 1)
            dve.tensor_scalar(gate_d[:, :], gate_e[:, :], 1.0, None, ALU.add).then_inc(gate_step, 1)
            dve.wait_ge(gate_step, 2)
            dve.reciprocal(g_mem[:, :], gate_d[:, :]).then_inc(gate_step, 1)
            dve.wait_ge(gate_step, 3)
            dve.tensor_scalar(g_loc[:, :], g_mem[:, :], -1.0, 1.0, ALU.mult, ALU.add).then_inc(gate_step, 1)
            dve.wait_ge(gate_step, 4)
            for t in (rest_done, sf_done, am_done):
                t.give(dve)

            def project_chunk(b, cc):
                k = b * 2 + cc

                def low(o):
                    dve.wait_ge(ph_done.sem, ph_done.after(k * 4 + o))
                    dve.wait_ge(pl_done.sem, pl_done.after(k * 4 + (o - 4)))
                    dve.tensor_tensor(rest[:, o, :], qk_bank[o], part[0][:, o, :],
                                      ALU.subtract).then_inc(rest_done.sem, 1)

                def q_min(o):
                    dve.wait_ge(ph_done.sem, ph_done.after(k * 4 + o))
                    dve.wait_ge(sl_done.sem, sl_done.after(k * DK + (o - DK)))
                    apart(dve)
                    dve.tensor_scalar(elu[:, o, :], qk_bank[o], 0.0, None, ALU.min).then_inc(min_done.sem, 1)

                def q_elu(o):
                    dve.wait_ge(qe_done.sem, qe_done.after(k * DK + o))
                    dve.scalar_tensor_tensor(elu[:, o, :], qk_bank[o], 0.0, elu[:, o, :], ALU.max,
                                             ALU.add).then_inc(sf_done.sem, 1)

                q_min(0)
                low(0)
                q_min(1)
                q_elu(0)
                low(1)
                q_elu(1)
                low(2)
                low(3)

            def memory_weights(b):
                dve.wait_ge(rawT_done.sem, rawT_done.after(b * 2 + 1))
                dve.tensor_tensor(total[:, :], sums[:, 0:1], sums[:, 1:2], ALU.add).then_inc(raw_step, 1)
                dve.wait_ge(raw_step, b * RAW + 1)
                apart(dve)
                dve.tensor_scalar(sums_d[:, :], ident[0:MEM, 0:MEM], total[:, 0:1], None,
                                  ALU.mult).then_inc(raw_step, 1)
                dve.wait_ge(raw_turned.sem, raw_turned.after(b))
                dve.tensor_scalar(rawc[:, :, :], half(2)[:, 0:BT * MEM].rearrange("p (t m) -> p t m", m=MEM),
                                  MEM_EPS, None, ALU.max).then_inc(raw_step, 1)
                dve.wait_ge(raw_step, b * RAW + 3)
                dve.reciprocal(rinv[:, :, :], rawc[:, :, :]).then_inc(raw_step, 1)
                dve.wait_ge(rel_ready.sem, rel_ready.after(b))
                dve.tensor_copy(rel[:, :], half(3)[:, 0:MEM]).then_inc(raw_step, 1)
                dve.wait_ge(raw_step, b * RAW + 5)
                dve.tensor_reduce(rmax[:, :], rel[:, :], AX.X, ALU.max, negate=True).then_inc(rmax_done.sem, 1)
                dve.wait_ge(rexp_done.sem, rexp_done.after(b))
                dve.reciprocal(rnorm[:, :], rsum[:, :]).then_inc(raw_step, 1)
                dve.wait_ge(raw_step, b * RAW + 6)
                dve.tensor_scalar(wmem[:, :], rexp[:, :], rnorm[:, 0:1], g_mem[:, 0:1], ALU.mult,
                                  ALU.mult).then_inc(raw_step, 1)
                dve.wait_ge(raw_step, b * RAW + 7)
                dve.tensor_tensor(coef[:, :, :], rinv[:, :, :], wmem[:, :].unsqueeze(1).broadcast_to([P, BT, MEM]),
                                  ALU.mult).then_inc(raw_step, 1)
                dve.wait_ge(raw_step, b * RAW + 8)

            def memory_add(b, t):
                for m in range(MEM):
                    if m % 2 == 0:
                        dve.wait_ge(am_ready.sem, am_ready.after((b * BT + t) * 2 + m // 2))
                    tile = X[:, b * BT + t, :]
                    last = dve.scalar_tensor_tensor(tile, half(2 + m // 2)[:, m % 2 * D:(m % 2 + 1) * D],
                                                    coef[:, t, m:m + 1], tile, ALU.mult, ALU.add)
                    if m % 2:
                        last.then_inc(am_done.sem, 1)
                        if m < MEM - 1:
                            dve.wait_ge(am_done.sem, am_done.after((b * BT + t) * 2))
                    else:
                        last.then_inc(am_step, 1)
                        dve.wait_ge(am_step, (b * BT + t) * 2 + (m // 2 + 1))

            project_chunk(0, 0)
            dve_stats(dve, CHUNKS + 1, 1)
            dve_norm(dve, CHUNKS + 1, 1)
            dve_xT(dve, CHUNKS + 1)
            project_chunk(0, 1)
            memory_weights(0)
            with dve.Fori(0, B - 1) as pb:
                for cc in range(2):
                    k = pb * 2 + (2 + cc)
                    dve_stats(dve, k + CHUNKS, k)
                    memory_add(pb, cc * CT)
                    dve_norm(dve, k + CHUNKS, k)
                    memory_add(pb, cc * CT + 1)
                    memory_add(pb, cc * CT + 2)
                    dve_xT(dve, k + CHUNKS)
                    memory_add(pb, cc * CT + 3)
                    project_chunk(pb + 1, cc)
                memory_weights(pb + 1)


            def row_max(b, g, u, n, done):
                G = b * GROUPS + g
                qt, h, k0, k1 = UNITS[u]
                s = ring_at[ring_bank(n)][:, 0:k1 - k0]
                col = (qt // CT + k0 // CW) * MX + h * CT + qt % CT
                dve.wait_ge(s_ready.sem, s_ready.after(G * NU + u))
                if u == 0 and not first(G) and not first(G - 1):
                    dve.wait_ge(mT_ready.sem, mT_ready.after(2 * G - 3))
                apart(dve)
                dve.tensor_tensor_reduce(out=s, in0=s, in1=mask[:, S - qt * P - P + k0:S - qt * P - P + k1], scale=1.0,
                                         scalar=-3.0e38, op0=ALU.add, op1=ALU.max,
                                         accum_out=rmx[:, g % 2, col:col + 1]).then_inc(ring_free.sem, 1)
                if u == NU - 1:
                    dve.wait_ge(ring_free.sem, done)
                    h1 = rmx[:, g % 2, MX:2 * MX]
                    dve.tensor_tensor(h1, h1, rmx[:, g % 2, 2 * MX:3 * MX], ALU.max).then_inc(mx_both.sem, 1)

            def core_maxrows(b, g, i, n):
                m = 2 * (b * GROUPS + g) + i
                dve.wait_ge(mh_done.sem, mh_done.after(m))
                dve.wait_ge(mrow_in[i].sem, mrow_in[i].after(b * GROUPS + (g - 1)))
                dve.scalar_tensor_tensor(mx_rest[:, i, :], ring_at[ring_bank(n)][0:MX, 0:P], -1.0, mx_part[0][:, i, :],
                                         ALU.mult, ALU.subtract).then_inc(ring_free.sem, 1)

            def heads_out(b, g, qc, n):
                G = b * GROUPS + g
                i = 2 * G + qc
                o = ring_at[ring_bank(n)][:, :].rearrange("p (x e) -> p x e", e=VW)
                dve.wait_ge(oT_ready.sem, oT_ready.after(i))
                dve.reciprocal(rden[:, qc, :], o[:, :, HD]).then_inc(rden_done.sem, 1)
                dve.wait_ge(rden_done.sem, rden_done.after(i))
                if qc == 0:
                    dve.wait_ge(L_out[g % 2].sem, L_out[g % 2].after(b * 2 + (g // 2 - 1)))
                dve.scalar_tensor_tensor(
                    Lg[:, g % 2, qc * CT:(qc + 1) * CT, :].rearrange("p t (h e) -> p (t h) e", e=HD),
                    o[:, :, 0:HD], g_loc[:, 0:1], rden[:, qc, :].unsqueeze(2).broadcast_to([P, CT * GH, HD]),
                    ALU.mult, ALU.mult).then_inc(ring_free.sem, 1)

            def core_turn(b, last=False):
                plan = turns(last)
                for g in range(GROUPS):
                    for step, a, n in plan[g]:
                        if step == "scores1":
                            row_max(*after_groups(b, g, a[0]), a[1], n, ring_done(b, n))
                        elif step == "maxrows":
                            core_maxrows(*after_groups(b, g, a[0]), a[1], n)
                        elif step == "outT":
                            heads_out(b, g, a[0], n)

            def start(steps):
                for step, a, n in steps:
                    if step == "scores1":
                        row_max(0, *a, n, ring_done(0, n))
                    else:
                        core_maxrows(0, *a, n)

            for t in range(BT):
                memory_add(B - 1, t)
                start(START[t * EARLY:(t + 1) * EARLY])
            start(START[BT * EARLY:])
            with dve.Fori(0, B - 1) as b:
                core_turn(b)
            core_turn(B - 1, True)

            dve_proj_lo(dve, ffn2, 0)
            dve_residual(dve, ffn2, 0, 0, 1.0)
            dve.wait_ge(ffn2.x_done.sem, ffn2.x_done.after(CT - 1))
            dve_stats(dve, 2 * CHUNKS, 0)
            dve_norm(dve, 2 * CHUNKS, 0)
            dve_xT(dve, 2 * CHUNKS)
            with dve.Fori(0, CHUNKS - 1) as c:
                dve_ffn(dve, ffn2, c, c + (2 * CHUNKS + 1), c + 1)
            dve_ffn(dve, ffn2, CHUNKS - 1, None, None)

        @block.tensor
        def _(pe):
            pe.wait_ge(consts, 4)
            for f in (ffn1, ffn2):
                f.d_ready.give(pe)
            pe_xT(pe, 0)
            pe.wait_ge(xl_done, DK)

            def ffn_weights(j):
                if j == FK:
                    pe.wait_ge(wd_lo, 2)
                elif j % (FK // UP) == 0:
                    pe.wait_ge(up_lo, 2 * (j // (FK // UP)) + 2)

            pe_ffn(pe, ffn1, 0, 1, before=ffn_weights)
            with pe.Fori(1, CHUNKS - 1) as c:
                pe.wait_ge(xl_done, c * DK + DK)
                pe_ffn(pe, ffn1, c, c + 1)
            pe.wait_ge(xl_done, CHUNKS * DK)

            def memories_wo():
                pe.wait_ge(ffn1.silu_done.sem, ffn1.silu_done.after(CHUNKS * FK - 1))
                pe.wait_ge(sp_lo, 6)
                pe_xT(pe, CHUNKS)
                for i in range(DK * MEM):
                    dk, m = i // MEM, i % MEM
                    pe.wait_ge(mwo_lo.sem, mwo_lo.after(i - 2))
                    products(pe, half(i % 2)[:, 0:D], memTs, wos, lambda a, k: a[:, m, k, dk * P:(dk + 1) * P],
                             lambda a, k: a[:, k, :], DK).then_inc(mwo_ready.sem, 1)

            pe_ffn(pe, ffn1, CHUNKS - 1, None, memories_wo)

            pe.wait_ge(ffn1.x_done.sem, ffn1.x_done.after(CHUNKS * CT - 1))
            pe.wait_ge(ffn1.mul_done.sem, ffn1.mul_done.after(CHUNKS * FK - 1))
            pe.wait_ge(mwo_lo.sem, mwo_lo.after(DK * MEM - 1))

            def project_chunk(b, cc):
                k = b * 2 + cc
                pe.wait_ge(xl_done, (k + CHUNKS) * DK + DK)
                for o in range(2 * DK):
                    w = wqs if o < DK else wks
                    if o < DK:
                        pe.wait_ge(sf_done.sem, sf_done.after(k * DK + (o - DK)))
                    pe.wait_ge(rest_done.sem, rest_done.after(k * 4 + (o - 4)))
                    products(pe, qk_bank[o], w, xT, lambda a, kk: a[:, kk, (o % DK) * P:(o % DK + 1) * P],
                             lambda a, kk: a[:, kk, :], DK).then_inc(qk_ready.sem, 1)
                for t in range(CT):
                    products(pe, v_bank(t), xT, wvs, lambda a, kk: a[:, kk, t * P:(t + 1) * P],
                             lambda a, kk: a[:, kk, :], DK).then_inc(v_ready.sem, 1)

            def norms_of(b):
                pe.wait_ge(am_done.sem, am_done.after(b * 2 * BT - 1))
                for cc in range(2):
                    pe.wait_ge(sl_done.sem, sl_done.after(b * 4 + (2 * cc + 1)))
                    products(pe, half(2 + cc)[0:MEM, :], nrm, sig, lambda a, k: a[:, k, :],
                             lambda a, k: a[:, k, cc * CW:(cc + 1) * CW], DK).then_inc(raw_ready.sem, 1)
                pe.wait_ge(rawT_done.sem, rawT_done.after(b * 2 + 1))
                apart(pe)
                for t in range(BT):
                    m = pe.transpose(half(2)[:, t * MEM:(t + 1) * MEM], rawT_sb[:, t * P:(t + 1) * P],
                                     ident[0:MEM, 0:MEM])
                m.then_inc(raw_turned.sem, 1)
                pe.wait_ge(raw_step, b * RAW + 2)
                pe.matmul(half(3)[:, 0:MEM], mean_w[0:MEM, :], sums_d[:, :], start=True,
                          stop=True).then_inc(rel_ready.sem, 1)

            def memory_tile(b, t):
                for hf in range(2):
                    if t == 0:
                        pe.wait_ge(raw_step, b * RAW + (3, 5)[hf])
                    pe.wait_ge(am_done.sem, am_done.after((b * BT + t) * 2 + (hf - 2)))
                    products(pe, half(2 + hf), sig, mwo, lambda a, k: a[:, k, t * P:(t + 1) * P],
                             lambda a, k: a[:, k, hf * CW:(hf + 1) * CW], DK).then_inc(am_ready.sem, 1)

            def project_xT(k):
                pe.wait_ge(v_free.sem, v_free.after(k * CT - 1))
                pe_xT(pe, k + CHUNKS)

            project_chunk(0, 0)
            project_xT(1)
            project_chunk(0, 1)
            norms_of(0)
            with pe.Fori(0, B - 1) as pb:
                for cc in range(2):
                    for t in range(CT - 1):
                        memory_tile(pb, cc * CT + t)
                    project_xT(pb * 2 + (2 + cc))
                    memory_tile(pb, cc * CT + CT - 1)
                    project_chunk(pb + 1, cc)
                norms_of(pb + 1)

            pv_done.give(pe)
            mT_ready.give(pe)
            oT_ready.give(pe)

            def next_bank(b, n):
                if ring_before(n) >= -len(START):
                    pe.wait_ge(ring_free.sem, ring_done(b, ring_before(n)))
                return ring_at[ring_bank(n)]

            def scores1(b, g, u, s):
                qt, h, k0, k1 = UNITS[u]
                if u == 0:
                    pe.wait_ge(stack_in[g].sem, stack_in[g].after(b))
                pe.matmul(s[:, 0:k1 - k0], Q[g][0:PARTS, qt // CT, h, qt % CT * P:(qt % CT + 1) * P],
                          K[g][0:PARTS, h, k0:k1], start=True, stop=True).then_inc(s_ready.sem, 1)

            def scores2(b, g, i, pair):
                n = ((b * GROUPS + g) * NQ + i) * 2 + pair
                b, g = after_groups(b, g, i // NQ)
                qc, kb, w, _ = QUADS[i % NQ]
                G = b * GROUPS + g
                if i % NQ in FIRST_QUAD and pair == 0:
                    pe.wait_ge(mrow_in[qc].sem, mrow_in[qc].after(G))
                pe.wait_ge(p_done.sem, p_done.after(n - 2))
                for j in range(2):
                    h = 2 * pair + j
                    last = pe.matmul(big[pair][:, j * CW:j * CW + w], K[g][0:ROWS, h, kb * P:(kb + 1) * P],
                                     Q[g][0:ROWS, qc, h, CW - w:CW], start=True, stop=True)
                last.then_inc(st_ready.sem, 1)

            def pv(b, g, i):
                qc, kb, w, diag = QUADS[i]
                G = b * GROUPS + g
                if i in FIRST_QUAD:
                    pe.wait_ge(o_out.sem, o_out.after(2 * G + qc - 1))
                if diag:
                    pe.wait_ge(masked.sem, masked.after((G * NDIAG + DIAG[i]) * 2 + 1))
                else:
                    pe.wait_ge(p_done.sem, p_done.after((G * NQ + i) * 2 + 1))
                for h in range(GH):
                    last = pe.matmul(bank[2][h * VW:(h + 1) * VW, CW - w:CW], Vg[g][:, kb, h * VW:(h + 1) * VW],
                                     PT[:, (i % 2) * GH + h, 0:w], start=i in FIRST_QUAD, stop=i in LAST_QUAD)
                last.then_inc(pv_done.sem, 1)

            def core_maxrows(b, g, i, s):
                if i:
                    pe.wait_ge(mx_both.sem, mx_both.after(b * GROUPS + g))
                pe.transpose(s[0:MX, 0:P], rmx[:, g % 2, i * MX:(i + 1) * MX], ident[:, :]).then_inc(mT_ready.sem, 1)

            def core_outT(b, g, qc, s):
                pe.wait_ge(o_out.sem, o_out.after(2 * (b * GROUPS + g) + qc))
                for t in range(CT):
                    last = pe.transpose(s[:, t * P:(t + 1) * P], Osb[:, qc, t * P:(t + 1) * P], ident[:, :])
                last.then_inc(oT_ready.sem, 1)

            def core_turn(b, last=False):
                plan = turns(last)
                for g in range(GROUPS):
                    for step, a, n in plan[g]:
                        if step == "scores1":
                            s = next_bank(b, n)
                            scores1(*after_groups(b, g, a[0]), a[1], s)
                        elif step == "scores2":
                            scores2(b, g, *a)
                        elif step == "pv":
                            pv(b, g, a[0])
                        elif step == "maxrows":
                            s = next_bank(b, n)
                            core_maxrows(*after_groups(b, g, a[0]), a[1], s)
                        elif step == "outT":
                            s = next_bank(b, n)
                            core_outT(b, g, a[0], s)

            def start(steps):
                for step, a, n in steps:
                    s = next_bank(0, n)
                    if step == "scores1":
                        scores1(0, *a, s)
                    else:
                        core_maxrows(0, *a, s)

            pe.wait_ge(v_free.sem, v_free.after(2 * B * CT - 1))
            pe.wait_ge(rest_done.sem, rest_done.after(8 * B - 1))
            for t in range(BT):
                memory_tile(B - 1, t)
                start(START[t * EARLY:(t + 1) * EARLY])
            pe.wait_ge(am_done.sem, am_done.after(2 * B * BT - 1))
            start(START[BT * EARLY:])
            pe.wait_ge(k_ones, GROUPS)
            scores2(0, 0, 0, 0)
            scores2(0, 0, 0, 1)
            with pe.Fori(0, B - 1) as b:
                core_turn(b)
            core_turn(B - 1, True)

            pe.wait_ge(ring_free.sem, ring_done(B - 1, count(turns(True)) - 1))
            pe_proj_T(pe, ffn2, 0)
            pe_proj(pe, ffn2, 0)
            pe_xT(pe, 2 * CHUNKS)
            with pe.Fori(0, CHUNKS - 1) as c:
                pe.wait_ge(xl_done, c * DK + (2 * CHUNKS + 1) * DK)
                pe_ffn(pe, ffn2, c, c + (2 * CHUNKS + 1))
            pe.wait_ge(xl_done, 3 * CHUNKS * DK)
            pe_ffn(pe, ffn2, CHUNKS - 1, None)


_INS = ("x", "wg", "wu", "wd", "wq", "wk", "wv", "wo", "memT", "norms", "gate")


def kernel(L0_attn_x, L0_attn_w_q, L0_attn_w_k, L0_attn_w_v, L0_attn_w_o, L0_attn_gate, L0_attn_memories,
           L0_attn_memory_norms, L0_ffn_w_gate, L0_ffn_w_up, L0_ffn_w_down):
    import numpy as np
    import concourse.bacc as bacc
    from concourse.bass_utils import run_bass_kernel_spmd

    def by_partition(w):
        k, n = w.shape
        return w.reshape(k // P, P, n).transpose(1, 0, 2)

    mem = np.asarray(L0_attn_memories).transpose(2, 0, 1)
    data = dict(
        x=np.asarray(L0_attn_x).reshape(TOK, D),
        wg=by_partition(np.asarray(L0_ffn_w_gate).T), wu=by_partition(np.asarray(L0_ffn_w_up).T),
        wd=by_partition(np.asarray(L0_ffn_w_down).T),
        wq=by_partition(np.asarray(L0_attn_w_q).T), wk=by_partition(np.asarray(L0_attn_w_k).T),
        wv=by_partition(np.asarray(L0_attn_w_v).T), wo=by_partition(np.asarray(L0_attn_w_o).T),
        memT=mem.reshape(DK, P, MEM, D).transpose(1, 2, 0, 3),
        norms=by_partition(np.asarray(L0_attn_memory_norms).T),
        gate=np.asarray(L0_attn_gate),
    )
    nc = bacc.Bacc("TRN2", target_bir_lowering=False, num_devices=1)
    arrays, args = {}, []
    for name in _INS:
        a = np.ascontiguousarray(data[name])
        arrays["in_" + name] = a
        args.append(nc.dram_tensor("in_" + name, a.shape, mybir.dt.from_np(a.dtype), kind="ExternalInput").ap())
    args.append(nc.dram_tensor("out_0", (TOK, D), F32, kind="ExternalOutput").ap())
    build(nc, *args)
    r = run_bass_kernel_spmd(nc, [arrays], core_ids=[0])
    return r.results[0]["out_0"].reshape(B, S, D)
```
